# Optimizing a Trainium2 kernel written in Bass

```python
import numpy as np
import jax
import jax.numpy as jnp

def _softmax(x, axis=-1):
    return jax.nn.softmax(x, axis=axis)

def _gelu(x):
    return jax.nn.gelu(x, approximate=True)

def _silu(x):
    return jax.nn.silu(x)

def _sigmoid(x):
    return jax.nn.sigmoid(x)

def _layernorm(x, axis=-1, eps=1e-05):
    m = jnp.mean(x, axis=axis, keepdims=True)
    v = jnp.var(x, axis=axis, keepdims=True)
    return (x - m) / jnp.sqrt(v + eps)

def _scatter_add(tgt, idx, src, axis=0):
    return tgt.at[idx].add(src)

def _segment_sum(src, seg, n):
    return jax.ops.segment_sum(src, seg, n)
kernel_name = 'mk_flamingo_gated_d2_seqx_r8_328ec3'

def setup_inputs(seed: int=0):
    np.random.seed(seed)
    _w = jnp.asarray

    def _rec_inputs():
        import jax
        import jax.numpy as jnp
        _rk = jax.random.key(seed)
        x = 7.22e-05 + 1 * jax.random.normal(jax.random.fold_in(_rk, 1), (8, 256, 256), jnp.float32)
        _lenS = 256 - jax.random.randint(jax.random.fold_in(_rk, 7), (8,), 0, max(1, 256 // 4) + 1, jnp.int32)
        _lenS2 = 64 - jax.random.randint(jax.random.fold_in(_rk, 8), (8,), 0, max(1, 64 // 4) + 1, jnp.int32)
        _ctx_2048P = jax.random.normal(jax.random.fold_in(_rk, 11), (8, 16, 256), jnp.float32)
        _ctx_2048c = jax.random.dirichlet(jax.random.fold_in(_rk, 511), 0.3 * jnp.ones((16,), jnp.float32), (8, 64))
        _ctx_2048t = jnp.einsum('bsk,bkd->bsd', _ctx_2048c, _ctx_2048P)
        _ctx_2048t = _ctx_2048t * jax.lax.rsqrt(jnp.mean(jnp.square(_ctx_2048t)) + 1e-12) * 0.953939
        ctx_2048 = 4.13588e-05 + 0.999923 * (_ctx_2048t + 0.3 * jax.random.normal(jax.random.fold_in(_rk, 611), (8, 64, 256), jnp.float32))
        _g = jax.random.normal(jax.random.fold_in(_rk, 9001), (2, 2), jnp.float32)
        _g = jnp.sign(_g) * jnp.maximum(jnp.abs(_g), 1.0) + (_g == 0) * 1.0
        g_xattn = _g[0]
        g_ffn = _g[1]
        return (x, ctx_2048, _lenS2, g_xattn, g_ffn)
    x, ctx_2048, _lenS2, g_xattn, g_ffn = _rec_inputs()

    def _L0_xattn_setup():
        import math
        import jax, jax.numpy as jnp
        import numpy as np
        HEADS = 16
        MASKED_BIAS = -10000.0

        def _mha(q, k, v):
            B, Sq, D = q.shape
            Sk = k.shape[-2]
            hd = D // HEADS
            qh = q.reshape(B, Sq, HEADS, hd).transpose(0, 2, 1, 3)
            kh = k.reshape(B, Sk, HEADS, hd).transpose(0, 2, 1, 3)
            vh = v.reshape(B, Sk, HEADS, hd).transpose(0, 2, 1, 3)
            scores = jnp.einsum('bhqd,bhkd->bhqk', qh, kh) / math.sqrt(hd)
            qi = jnp.arange(Sq)[:, None] + (Sk - Sq)
            ki = jnp.arange(Sk)[None, :]
            causal = ki <= qi
            scores = jnp.where(causal[None, None], scores, jnp.asarray(MASKED_BIAS, scores.dtype))
            attn = jax.nn.softmax(scores, axis=-1)
            out = jnp.einsum('bhqk,bhkd->bhqd', attn, vh)
            return out.transpose(0, 2, 1, 3).reshape(B, Sq, D)
        key = jax.random.key(seed)
        kq, kk, kv = jax.random.split(key, 3)
        B, S, D = (4, 128, 256)
        q = jax.random.normal(kq, (B, S, D), dtype=jnp.float32)
        k = jax.random.normal(kk, (B, S, D), dtype=jnp.float32)
        v = jax.random.normal(kv, (B, S, D), dtype=jnp.float32)
        return {'q': q, 'k': k, 'v': v}
    _L0_xattn_all = _L0_xattn_setup()
    _L0_xattn_in = {k: v for k, v in _L0_xattn_all.items() if k in ()}
    del _L0_xattn_all

    def _L0_ffn_setup():
        import jax, jax.numpy as jnp
        import numpy as np
        B, S, H = (2, 128, 256)
        E, K = (8, 2)
        F = 176
        FS = 704
        NORM_TOPK = False

        def _swiglu(x, wg, wu, wd):
            return jax.nn.silu(x @ wg) * (x @ wu) @ wd
        key = jax.random.key(seed)
        ks = jax.random.split(key, 9)
        s = 0.02
        return {'hidden_states': jax.random.normal(ks[0], (B, S, H), dtype=jnp.float32), 'Wr': jax.random.normal(ks[1], (H, E), dtype=jnp.float32) * s, 'Wg': jax.random.normal(ks[2], (E, H, F), dtype=jnp.float32) * s, 'Wu': jax.random.normal(ks[3], (E, H, F), dtype=jnp.float32) * s, 'Wd': jax.random.normal(ks[4], (E, F, H), dtype=jnp.float32) * s, 'Sg': jax.random.normal(ks[5], (H, FS), dtype=jnp.float32) * s, 'Su': jax.random.normal(ks[6], (H, FS), dtype=jnp.float32) * s, 'Sd': jax.random.normal(ks[7], (FS, H), dtype=jnp.float32) * s, 'Wsg': jax.random.normal(ks[8], (H, 1), dtype=jnp.float32) * s}
    _L0_ffn_all = _L0_ffn_setup()
    _L0_ffn_in = {k: v for k, v in _L0_ffn_all.items() if k in ('Wr', 'Wg', 'Wu', 'Wd', 'Sg', 'Su', 'Sd', 'Wsg')}
    del _L0_ffn_all

    def _L1_xattn_setup():
        import jax, jax.numpy as jnp
        import numpy as np
        DIM = 256
        HEADS = 16
        HEAD_DIM = DIM // HEADS
        EPS = 1e-06
        IMG_TOKENS = 257
        B, L1, L2 = (2, 512, 769)
        SCALE = 1.0 / np.sqrt(HEAD_DIM).astype(np.float32)

        def rms_norm(x, g):
            return x * jax.lax.rsqrt(jnp.mean(x * x, axis=-1, keepdims=True) + EPS) * g

        def attention(q, k, v, kv_mask=None):
            s = jnp.einsum('bqhd,bkhd->bhqk', q, k) * SCALE
            if kv_mask is not None:
                s = jnp.where(kv_mask[:, None, None, :], s, jnp.float32(-1000000000.0))
            p = jax.nn.softmax(s, axis=-1)
            return jnp.einsum('bhqk,bkhd->bqhd', p, v)
        key = jax.random.key(seed)
        ks = jax.random.split(key, 20)
        std = 0.02

        def lin(i):
            return (jax.random.normal(ks[i], (DIM, DIM), jnp.float32) * std, jnp.zeros((DIM,), jnp.float32))
        w_q, b_q = lin(0)
        w_k, b_k = lin(1)
        w_v, b_v = lin(2)
        w_k_img, b_k_img = lin(3)
        w_v_img, b_v_img = lin(4)
        w_o, b_o = lin(5)
        return {'x': jax.random.normal(ks[6], (B, L1, DIM), jnp.float32), 'context': jax.random.normal(ks[7], (B, L2, DIM), jnp.float32), 'context_lens': jax.random.randint(ks[8], (B,), 32, 513, jnp.int64 if jax.config.jax_enable_x64 else jnp.int32), 'w_q': w_q, 'b_q': b_q, 'w_k': w_k, 'b_k': b_k, 'w_v': w_v, 'b_v': b_v, 'w_k_img': w_k_img, 'b_k_img': b_k_img, 'w_v_img': w_v_img, 'b_v_img': b_v_img, 'w_o': w_o, 'b_o': b_o, 'g_q': jnp.ones((DIM,), jnp.float32), 'g_k': jnp.ones((DIM,), jnp.float32), 'g_k_img': jnp.ones((DIM,), jnp.float32)}
    _L1_xattn_all = _L1_xattn_setup()
    _L1_xattn_in = {k: v for k, v in _L1_xattn_all.items() if k in ('w_q', 'b_q', 'w_k', 'b_k', 'w_v', 'b_v', 'w_k_img', 'b_k_img', 'w_v_img', 'b_v_img', 'w_o', 'b_o', 'g_q', 'g_k', 'g_k_img')}
    del _L1_xattn_all

    def _L1_ffn_setup():
        import jax, jax.numpy as jnp
        import numpy as np
        DIM_IN = 256
        DIM_HIDDEN = 1024
        key = jax.random.key(seed)
        k_x, k_g, k_u, k_d = jax.random.split(key, 4)
        s_in = 1.0 / np.sqrt(DIM_IN)
        s_hid = 1.0 / np.sqrt(DIM_HIDDEN)
        x = jax.random.normal(k_x, (4, 256, DIM_IN), dtype=jnp.float32)
        w_gate = jax.random.uniform(k_g, (DIM_HIDDEN, DIM_IN), jnp.float32, -s_in, s_in)
        w_up = jax.random.uniform(k_u, (DIM_HIDDEN, DIM_IN), jnp.float32, -s_in, s_in)
        w_down = jax.random.uniform(k_d, (DIM_IN, DIM_HIDDEN), jnp.float32, -s_hid, s_hid)
        return {'x': x, 'w_gate': w_gate, 'w_up': w_up, 'w_down': w_down}
    _L1_ffn_all = _L1_ffn_setup()
    _L1_ffn_in = {k: v for k, v in _L1_ffn_all.items() if k in ('w_gate', 'w_up', 'w_down')}
    del _L1_ffn_all
    return {'x': x, 'ctx_2048': ctx_2048, '_lenS2': _lenS2, 'g_xattn': g_xattn, 'g_ffn': g_ffn, 'L0_ffn_Wr': _L0_ffn_in['Wr'], 'L0_ffn_Wg': _L0_ffn_in['Wg'], 'L0_ffn_Wu': _L0_ffn_in['Wu'], 'L0_ffn_Wd': _L0_ffn_in['Wd'], 'L0_ffn_Sg': _L0_ffn_in['Sg'], 'L0_ffn_Su': _L0_ffn_in['Su'], 'L0_ffn_Sd': _L0_ffn_in['Sd'], 'L0_ffn_Wsg': _L0_ffn_in['Wsg'], 'L1_xattn_w_q': _L1_xattn_in['w_q'], 'L1_xattn_b_q': _L1_xattn_in['b_q'], 'L1_xattn_w_k': _L1_xattn_in['w_k'], 'L1_xattn_b_k': _L1_xattn_in['b_k'], 'L1_xattn_w_v': _L1_xattn_in['w_v'], 'L1_xattn_b_v': _L1_xattn_in['b_v'], 'L1_xattn_w_k_img': _L1_xattn_in['w_k_img'], 'L1_xattn_b_k_img': _L1_xattn_in['b_k_img'], 'L1_xattn_w_v_img': _L1_xattn_in['w_v_img'], 'L1_xattn_b_v_img': _L1_xattn_in['b_v_img'], 'L1_xattn_w_o': _L1_xattn_in['w_o'], 'L1_xattn_b_o': _L1_xattn_in['b_o'], 'L1_xattn_g_q': _L1_xattn_in['g_q'], 'L1_xattn_g_k': _L1_xattn_in['g_k'], 'L1_xattn_g_k_img': _L1_xattn_in['g_k_img'], 'L1_ffn_w_gate': _L1_ffn_in['w_gate'], 'L1_ffn_w_up': _L1_ffn_in['w_up'], 'L1_ffn_w_down': _L1_ffn_in['w_down']}

def reference(x, ctx_2048, _lenS2, g_xattn, g_ffn, L0_ffn_Wr, L0_ffn_Wg, L0_ffn_Wu, L0_ffn_Wd, L0_ffn_Sg, L0_ffn_Su, L0_ffn_Sd, L0_ffn_Wsg, L1_xattn_w_q, L1_xattn_b_q, L1_xattn_w_k, L1_xattn_b_k, L1_xattn_w_v, L1_xattn_b_v, L1_xattn_w_k_img, L1_xattn_b_k_img, L1_xattn_w_v_img, L1_xattn_b_v_img, L1_xattn_w_o, L1_xattn_b_o, L1_xattn_g_q, L1_xattn_g_k, L1_xattn_g_k_img, L1_ffn_w_gate, L1_ffn_w_up, L1_ffn_w_down):
    import jax
    import jax.numpy as jnp

    def _L0_xattn_ref(q, k, v):
        import math
        import jax, jax.numpy as jnp
        import numpy as np
        HEADS = 16
        MASKED_BIAS = -10000.0

        def _mha(q, k, v):
            B, Sq, D = q.shape
            Sk = k.shape[-2]
            hd = D // HEADS
            qh = q.reshape(B, Sq, HEADS, hd).transpose(0, 2, 1, 3)
            kh = k.reshape(B, Sk, HEADS, hd).transpose(0, 2, 1, 3)
            vh = v.reshape(B, Sk, HEADS, hd).transpose(0, 2, 1, 3)
            scores = jnp.einsum('bhqd,bhkd->bhqk', qh, kh) / math.sqrt(hd)
            qi = jnp.arange(Sq)[:, None] + (Sk - Sq)
            ki = jnp.arange(Sk)[None, :]
            causal = ki <= qi
            scores = jnp.where(causal[None, None], scores, jnp.asarray(MASKED_BIAS, scores.dtype))
            attn = jax.nn.softmax(scores, axis=-1)
            out = jnp.einsum('bhqk,bhkd->bhqd', attn, vh)
            return out.transpose(0, 2, 1, 3).reshape(B, Sq, D)
        return _mha(q, k, v)

    def _L0_ffn_ref(hidden_states, Wr, Wg, Wu, Wd, Sg, Su, Sd, Wsg):
        import jax, jax.numpy as jnp
        import numpy as np
        B, S, H = (2, 128, 256)
        E, K = (8, 2)
        F = 176
        FS = 704
        NORM_TOPK = False

        def _swiglu(x, wg, wu, wd):
            return jax.nn.silu(x @ wg) * (x @ wu) @ wd
        b, s, h = hidden_states.shape
        x = hidden_states.reshape(-1, h)
        router_logits = x @ Wr
        probs = jax.nn.softmax(router_logits.astype(jnp.float32), axis=-1)
        routing_weights, selected = jax.lax.top_k(probs, K)
        if NORM_TOPK:
            routing_weights = routing_weights / routing_weights.sum(-1, keepdims=True)
        routing_weights = routing_weights.astype(x.dtype)
        C = jnp.einsum('tk,tke->te', routing_weights, jax.nn.one_hot(selected, E, dtype=x.dtype))
        expert_out = jax.vmap(lambda wg, wu, wd: _swiglu(x, wg, wu, wd))(Wg, Wu, Wd)
        moe_out = jnp.einsum('te,eth->th', C, expert_out)
        shared = _swiglu(x, Sg, Su, Sd)
        shared = jax.nn.sigmoid(x @ Wsg) * shared
        out = (moe_out + shared).reshape(b, s, h)
        return out

    def _L1_xattn_ref(x, context, context_lens, w_q, b_q, w_k, b_k, w_v, b_v, w_k_img, b_k_img, w_v_img, b_v_img, w_o, b_o, g_q, g_k, g_k_img):
        import jax, jax.numpy as jnp
        import numpy as np
        DIM = 256
        HEADS = 16
        HEAD_DIM = DIM // HEADS
        EPS = 1e-06
        IMG_TOKENS = 257
        B, L1, L2 = (2, 512, 769)
        SCALE = 1.0 / np.sqrt(HEAD_DIM).astype(np.float32)

        def rms_norm(x, g):
            return x * jax.lax.rsqrt(jnp.mean(x * x, axis=-1, keepdims=True) + EPS) * g

        def attention(q, k, v, kv_mask=None):
            s = jnp.einsum('bqhd,bkhd->bhqk', q, k) * SCALE
            if kv_mask is not None:
                s = jnp.where(kv_mask[:, None, None, :], s, jnp.float32(-1000000000.0))
            p = jax.nn.softmax(s, axis=-1)
            return jnp.einsum('bhqk,bkhd->bqhd', p, v)
        b = x.shape[0]
        ctx_img = context[:, :IMG_TOKENS]
        ctx_txt = context[:, IMG_TOKENS:]
        q = rms_norm(x @ w_q.T + b_q, g_q).reshape(b, -1, HEADS, HEAD_DIM)
        k = rms_norm(ctx_txt @ w_k.T + b_k, g_k).reshape(b, -1, HEADS, HEAD_DIM)
        v = (ctx_txt @ w_v.T + b_v).reshape(b, -1, HEADS, HEAD_DIM)
        k_img = rms_norm(ctx_img @ w_k_img.T + b_k_img, g_k_img).reshape(b, -1, HEADS, HEAD_DIM)
        v_img = (ctx_img @ w_v_img.T + b_v_img).reshape(b, -1, HEADS, HEAD_DIM)
        txt_len = ctx_txt.shape[1]
        kv_mask = jnp.arange(txt_len)[None, :] < context_lens[:, None]
        img_x = attention(q, k_img, v_img)
        txt_x = attention(q, k, v, kv_mask)
        out = (txt_x + img_x).reshape(b, -1, DIM)
        return out @ w_o.T + b_o

    def _L1_ffn_ref(x, w_gate, w_up, w_down):
        import jax, jax.numpy as jnp
        import numpy as np
        DIM_IN = 256
        DIM_HIDDEN = 1024
        gate = jnp.einsum('bsd,hd->bsh', x, w_gate)
        up = jnp.einsum('bsd,hd->bsh', x, w_up)
        gated = jax.nn.silu(gate) * up
        return jnp.einsum('bsh,dh->bsd', gated, w_down)
    x = x + jnp.tanh(g_xattn[0]) * _L0_xattn_ref(_layernorm(x, axis=-1), ctx_2048, ctx_2048)
    x = x + jnp.tanh(g_ffn[0]) * _L0_ffn_ref(_layernorm(x, axis=-1), L0_ffn_Wr, L0_ffn_Wg, L0_ffn_Wu, L0_ffn_Wd, L0_ffn_Sg, L0_ffn_Su, L0_ffn_Sd, L0_ffn_Wsg)
    x = x + jnp.tanh(g_xattn[1]) * _L1_xattn_ref(_layernorm(x, axis=-1), ctx_2048, _lenS2, L1_xattn_w_q, L1_xattn_b_q, L1_xattn_w_k, L1_xattn_b_k, L1_xattn_w_v, L1_xattn_b_v, L1_xattn_w_k_img, L1_xattn_b_k_img, L1_xattn_w_v_img, L1_xattn_b_v_img, L1_xattn_w_o, L1_xattn_b_o, L1_xattn_g_q, L1_xattn_g_k, L1_xattn_g_k_img)
    x = x + jnp.tanh(g_ffn[1]) * _L1_ffn_ref(_layernorm(x, axis=-1), L1_ffn_w_gate, L1_ffn_w_up, L1_ffn_w_down)
    return x

_drawn_inputs = setup_inputs


def setup_inputs(seed=0):
    import zlib

    import numpy as np

    out = dict(_drawn_inputs(seed))
    spreads = {'g_ffn': (-1.0, 0.6),
     'L1_xattn_b_q': (0.0, 2.0),
     'L1_xattn_b_k': (0.0, 0.1),
     'L1_xattn_b_v': (0.0, 0.1),
     'L1_xattn_b_k_img': (0.0, 2.0),
     'L1_xattn_b_v_img': (0.0, 1.624),
     'L1_xattn_b_o': (0.0, 0.506),
     'L1_xattn_g_q': (1.0, 0.6),
     'L1_xattn_g_k': (1.0, 0.2),
     'L1_xattn_g_k_img': (1.0, 0.6)}
    factors = {'L0_ffn_Wr': 8.0,
     'L0_ffn_Wg': 8.0,
     'L0_ffn_Wu': 8.0,
     'L0_ffn_Wd': 8.0,
     'L0_ffn_Sg': 5.847,
     'L0_ffn_Su': 5.788,
     'L0_ffn_Sd': 5.786,
     'L0_ffn_Wsg': 8.0,
     'L1_xattn_w_q': 27.368,
     'L1_xattn_w_k_img': 26.064,
     'L1_xattn_w_v_img': 5.974,
     'L1_xattn_w_o': 3.135,
     'L1_ffn_w_gate': 3.64,
     'L1_ffn_w_up': 3.523,
     'L1_ffn_w_down': 3.527}
    for name, (base, spread) in spreads.items():
        noise = np.random.default_rng([zlib.crc32(name.encode()), seed]).standard_normal(out[name].shape)
        drawn = base * np.exp(spread * noise) if base else spread * noise
        out[name] = jnp.asarray(drawn.astype(out[name].dtype))
    for name, factor in factors.items():
        out[name] = (out[name] * factor).astype(out[name].dtype)
    return out
```

```python
from contextlib import ExitStack

import concourse.bass as bass
from concourse import mybir

F32 = mybir.dt.float32
F32R = mybir.dt.float32r
ALU = mybir.AluOpType
ACT = mybir.ActivationFunctionType
AX = mybir.AxisListType

P = 128
NB, SQ, D = 8, 256, 256
SK = 64
NH, HD = 16, 16
NT = NB * SQ // P
NE, FE, FS = 8, 176, 704
GT = 4
GN = GT * P
NG = NT // GT
NC0 = -(-(NE * FE + FS) // P)
HID0 = NC0 * P
HID1 = 1024
NC1 = HID1 // P
SCALE = 0.25
MASKED = -10000.0 / SCALE
LN_EPS, RMS_EPS = 1e-5, 1e-6
RMS_SCALE = 1 / 16
MOE_COLS = 6 * HID0
FFN_COLS = 6 * HID1
PIECE0 = MOE_COLS // (2 * NB)
PIECE1 = FFN_COLS // NB
C_ID, C_HM, C_VM, C_ONE, C_NH, C_W8, C_LE, C_RE = 0, 128, 136, 392, 424, 428, 436, 440
CST = 444


def wait(eng, sem, n):
    if isinstance(n, int) and n <= 0:
        return
    eng.wait_ge(sem, n)


def build(nc, x, ctx, ctx_t, xw, rw, moe_w, ffn_w, bias, gx, gf, consts, sel, out):
    nsb = [-(-nc.sbuf_base // 32) * 32]

    def sb(name, shape, dt=F32, at=None):
        cur = nsb if at is None else at
        size = 4
        for s in shape[1:]:
            size *= s
        h = nc.alloc_sbuf_tensor_at(name, list(shape), dt, offset=cur[0])
        cur[0] += -(-size // 32) * 32
        assert cur[0] <= nc.sbuf_top, (name, cur)
        return h

    es = ExitStack()
    with es:
        def sem(name):
            return es.enter_context(nc.semaphore(name))

        x_sb = sb("x_sb", [P, NT, D])
        cst = sb("cst", [P, CST])
        avg = sb("avg", [P, P])
        gates = sb("gates", [P, 4])
        bias_sb = sb("bias_sb", [P, 6, D])
        xw_hi = sb("xw_hi", [P, 4, 2, D], F32R)
        xw_lo = sb("xw_lo", [P, 4, 2, D], F32R)
        w_hi = sb("w_hi", [P, MOE_COLS], F32R)
        w_lo = sb("w_lo", [P, MOE_COLS], F32R)
        stage = sb("stage", [P, 2, PIECE0])
        stat = sb("stat", [P, 4, 6])
        mv = sb("mv", [P, 4, 2])
        ve = sb("ve", [P, 4])
        rstd = sb("rstd", [P, 4])
        rw_raw = sb("rw_raw", [P, 2, P])
        rw_hi = sb("rw_hi", [P, 2, P], F32R)
        rw_lo = sb("rw_lo", [P, 2, P], F32R)
        sel_sb = sb("sel_sb", [P, HID0], F32R)
        ident = cst[:, C_ID:C_ID + P]
        headmask = cst[:, C_HM:C_HM + 8]
        vmask = cst[:, C_VM:C_VM + D]
        oneblk = cst[:, C_ONE:C_ONE + 32]
        neghalf = cst[:, C_NH:C_NH + 4]
        w8 = cst[:, C_W8:C_W8 + 8]
        ln_eps = cst[:, C_LE:C_LE + 4]
        rms_eps = cst[:, C_RE:C_RE + 4]

        ra = [nsb[0]]
        ctxt = sb("ctxt", [P, 2, NB * SK], F32, ra)
        ctxd = sb("ctxd", [P, NB, D], F32, ra)
        a_kb = sb("a_kb", [P, 2, 2, 512], F32, ra)
        a_v = sb("a_v", [P, 2, D], F32, ra)
        a_xnb = sb("a_xnb", [P, D], F32, ra)
        a_qt = sb("a_qt", [P, 2, P], F32, ra)
        a_s = sb("a_s", [P, 2, NH * SK], F32, ra)
        a_mx = sb("a_mx", [P, NH], F32, ra)
        a_sm = sb("a_sm", [P, NH], F32, ra)
        a_ri = sb("a_ri", [P, NH], F32, ra)
        a_ptb = sb("a_ptb", [P, 8, P], F32, ra)
        a_at = sb("a_at", [P, 2, P], F32, ra)
        a_tmpb = sb("a_tmpb", [P, D], F32, ra)
        xw_raw = sb("xw_raw", [P, 4, 2, D], F32, ra)
        sel_raw = sb("sel_raw", [P, HID0], F32, ra)
        rf = [nsb[0]]
        f_xnb = sb("f_xnb", [P, GT, D], F32, rf)
        xt_hi = sb("xt_hi", [P, 2, 2, GN], F32R, rf)
        xt_lo = sb("xt_lo", [P, 2, 2, GN], F32R, rf)
        s_sb = sb("s_sb", [P, 2, GN], F32, rf)
        t_sb = sb("t_sb", [P, 2, GN], F32, rf)
        h_sb = sb("h_sb", [P, 2, GN], F32, rf)
        h_hi = sb("h_hi", [P, 3, GN], F32R, rf)
        h_lo = sb("h_lo", [P, 3, GN], F32R, rf)
        y_t = sb("y_t", [P, 2, GN], F32, rf)
        lgt = sb("lgt", [P, GN], F32, rf)
        c_t = sb("c_t", [P, 2, GN], F32R, rf)
        lg = sb("lg", [P, GT, 9], F32, rf)
        r_z = sb("r_z", [P, GT, 8], F32, rf)
        r_p = sb("r_p", [P, GT, 8], F32, rf)
        r_den = sb("r_den", [P, GT, 2], F32, rf)
        r_inv = sb("r_inv", [P, GT, 2], F32, rf)
        r_es = sb("r_es", [P, GT, 1], F32, rf)
        r_m = sb("r_m", [P, GT], F32, rf)
        r_k = sb("r_k", [P, GT, 8], F32, rf)
        r_o1 = sb("r_o1", [P, GT, 8], F32, rf)
        r_o2 = sb("r_o2", [P, GT, 8], F32, rf)
        r_c = sb("r_c", [P, GT, 9], F32, rf)
        r_cd = sb("r_cd", [P, GT, P], F32R, rf)
        rc = [nsb[0]]
        kt_hi = sb("kt_hi", [P, 2, NB * SK], F32R, rc)
        kt_lo = sb("kt_lo", [P, 2, NB * SK], F32R, rc)
        v1 = sb("v1", [P, NB, D], F32, rc)
        rc0 = [rc[0]]
        ctxt2 = sb("ctxt2", [P, 2, NB * SK], F32, rc0)
        ct_hi = sb("ct_hi", [P, 2, NB, SK], F32R, rc0)
        ct_lo = sb("ct_lo", [P, 2, NB, SK], F32R, rc0)
        cd_hi = sb("cd_hi", [P, 2, NB, 2, SK], F32R, rc0)
        cd_lo = sb("cd_lo", [P, 2, NB, 2, SK], F32R, rc0)
        k_sb = sb("k_sb", [P, 4, D], F32, rc0)
        kn_sb = sb("kn_sb", [P, 4, D], F32, rc0)
        k_ss = sb("k_ss", [P, 4], F32, rc0)
        k_sq = sb("k_sq", [P, D], F32, rc0)
        v_t = sb("v_t", [P, 2, D], F32, rc0)
        c_kbh = sb("c_kbh", [P, 2, 512], F32R, rc)
        c_kbl = sb("c_kbl", [P, 2, 512], F32R, rc)
        c_v = sb("c_v", [P, D], F32, rc)
        c_xnb = sb("c_xnb", [P, 2, D], F32, rc)
        c_xth = sb("c_xth", [P, 2, SQ], F32R, rc)
        c_xtl = sb("c_xtl", [P, 2, SQ], F32R, rc)
        c_qb = sb("c_qb", [P, 2, D], F32, rc)
        c_qnb = sb("c_qnb", [P, 2, D], F32, rc)
        c_ss = sb("c_ss", [P, 2], F32, rc)
        c_ve = sb("c_ve", [P, 2], F32, rc)
        c_rq = sb("c_rq", [P, 2], F32, rc)
        c_qth = sb("c_qth", [P, 2, SQ], F32R, rc)
        c_qtl = sb("c_qtl", [P, 2, SQ], F32R, rc)
        c_e = sb("c_e", [P, 2, NH * SK], F32, rc)
        c_mx = sb("c_mx", [P, 2, NH], F32, rc)
        c_ptb = sb("c_ptb", [P, 8, SQ], F32, rc)
        c_atb = sb("c_atb", [P, 2, SQ], F32, rc)
        c_athb = sb("c_athb", [P, 2, SQ], F32R, rc)
        c_atlb = sb("c_atlb", [P, 2, SQ], F32R, rc)


        bank = [es.enter_context(nc.psum_tensor(f"bank{i}", [P, 512], F32)) for i in range(8)]

        S = {}

        def done(name):
            if name not in S:
                S[name] = es.enter_context(nc.semaphore(name))
            return S[name]

        block = es.enter_context(nc.Block())
        x_v = x.rearrange("b (j p) d -> p (b j) d", p=P)
        out_v = out.rearrange("b (j p) d -> p (b j) d", p=P)
        out_flat = out.rearrange("b s d -> (b s) d")

        @block.sync
        def _(sp):
            sp.dma_start(x_sb[:, 0:2, :], x_v[:, 0:2, :]).then_inc(done("x0_in"), 16)
            sp.dma_start(cst[:], consts).then_inc(done("setup_in"), 16)
            sp.dma_start(ctxt[:], ctx_t).then_inc(done("setup_in"), 16)
            sp.dma_start(gates[:, 0:2], gx.rearrange("(a n) -> a n", a=1).broadcast_to([P, 2])).then_inc(done("gates_in"), 16)
            sp.dma_start(gates[:, 2:4], gf.rearrange("(a n) -> a n", a=1).broadcast_to([P, 2])).then_inc(done("gates_in"), 16)
            for half in range(2):
                sp.dma_start(ctxd[half * SK:(half + 1) * SK], ctx.rearrange("b k d -> k b d")).then_inc(done("setup_in"), 16)
            sp.dma_start(x_sb[:, 2:4, :], x_v[:, 2:4, :]).then_inc(done("x1_in"), 16)
            for u in range(2):
                sp.dma_start(stage[:, u], moe_w[:, u * PIECE0:(u + 1) * PIECE0]).then_inc(done(f"w0_in{u}"), 16)
            for q in range(2):
                a, b = 4 + 6 * q, 10 + 6 * q
                sp.dma_start(x_sb[:, a:b, :], x_v[:, a:b, :]).then_inc(done("x_in"), 16)
            sp.dma_start(rw_raw[:], rw).then_inc(done("late_in"), 16)
            sp.dma_start(sel_raw[:], sel).then_inc(done("late_in"), 16)
            sp.dma_start(xw_raw[:], xw).then_inc(done("late_in"), 16)
            sp.dma_start(bias_sb[:], bias.rearrange("(a n) d -> a n d", a=1).broadcast_to([P, 6, D])).then_inc(done("late_in"), 16)
            with sp.Fori(1, NB) as b:
                for u in range(2):
                    sp.wait_ge(done(f"w0_lo{u}"), b)
                    sp.dma_start(stage[:, u], moe_w[:, bass.ds((2 * b + u) * PIECE0, PIECE0)]).then_inc(done(f"w0_in{u}"), 16)
            sp.wait_ge(done("w0_lo0"), NB)
            sp.wait_ge(done("b_x"), 2 * NG)
            sp.dma_start(ctxt2[:], ctx_t).then_inc(done("ctxt2_in"), 16)
            with sp.Fori(0, NB) as b:
                sp.wait_ge(done("w1_lo"), b)
                sp.dma_start(stage[:, 0, 0:PIECE1], ffn_w[:, bass.ds(b * PIECE1, PIECE1)]).then_inc(done("w1_in"), 16)
            with sp.Fori(0, 2 * NG) as q:
                sp.wait_ge(done("d_x"), q + 1)
                sp.dma_start(out_v[:, bass.ds(2 * q, 2), :], x_sb[:, bass.ds(2 * q, 2), :]).then_inc(done("out_done"), 16)
            sp.wait_ge(done("out_done"), 16 * 2 * NG)

        def split_matmul(pe, dst, w_h, w_l, m_h, m_l, first, last):
            pe.matmul(dst, w_h, m_h, start=first, stop=False)
            pe.matmul(dst, w_h, m_l, start=False, stop=False)
            return pe.matmul(dst, w_l, m_h, start=False, stop=last)

        def back(c, ring, chunks):
            if c >= ring:
                return ring
            return c + chunks - max(k for k in range(chunks) if k % ring == c % ring)

        def ffn_weights(ph, kind, kk, c):
            hid = ph["chunks"] * P
            if kind == "down":
                return slice(4 * hid + c * D + kk * P, 4 * hid + c * D + kk * P + P)
            at = (2 * hid if kind == "up" else 0) + kk * hid + c * P
            return slice(at, at + P)

        def pe_front(pe, ph, g):
            p, bk = ph["name"], bank[7]
            for f in range(2):
                wait(pe, done(p + "xn"), GT * (g + 1))
                if f == 0:
                    wait(pe, done(p + "x"), 2 * (g - 1))
                    if ph["moe"]:
                        wait(pe, done(p + "ct"), g)
                wait(pe, done(p + "xtl"), 2 * g + f)
                for t in range(GT):
                    mm = pe.transpose(bk[:, t * P:(t + 1) * P], f_xnb[:, t, f * P:(f + 1) * P], ident)
                mm.then_inc(done(p + "xt_ps"), 1)
                yield
            if ph["moe"]:
                wait(pe, done(p + "xtl"), 2 * g + 2)
                for kk in range(2):
                    mm = split_matmul(pe, bk[:, :], rw_hi[:, kk, :], rw_lo[:, kk, :],
                                      xt_hi[:, g % 2, kk, :], xt_lo[:, g % 2, kk, :], kk == 0, kk == 1)
                mm.then_inc(done(p + "lg_ps"), 1)
                yield
                wait(pe, done(p + "lgt"), g + 1)
                for t in range(GT):
                    mm = pe.transpose(bk[:, t * P:(t + 1) * P], lgt[:, t * P:(t + 1) * P], ident)
                mm.then_inc(done(p + "lt_ps"), 1)
                yield
                wait(pe, done(p + "c"), g + 1)
                for t in range(GT):
                    mm = pe.transpose(bk[:, t * P:(t + 1) * P], r_cd[:, t, :].bitcast(F32), ident)
                mm.then_inc(done(p + "ct_ps"), 1)
                yield

        def pe_down(pe, ph, g, c, n):
            p = ph["name"]
            wait(pe, done(p + "hlo"), n + 1)
            for f in range(2):
                if c == 0:
                    wait(pe, done(p + "y"), 2 * g)
                w = ffn_weights(ph, "down", f, c)
                mm = split_matmul(pe, bank[5 + f][:, :], w_hi[:, w], w_lo[:, w], h_hi[:, c % 3, :], h_lo[:, c % 3, :],
                                  c == 0, c == ph["chunks"] - 1)
            mm.then_inc(done(p + "dn"), 1)

        def pe_tail(pe, ph, g, q):
            p = ph["name"]
            wait(pe, done(p + "y"), 2 * (g + 1))
            wait(pe, done(p + "x"), 2 * g + q)
            for t in range(2):
                for f in range(2):
                    mm = pe.transpose(bank[7][:, t * D + f * P:t * D + (f + 1) * P],
                                      y_t[:, f, (2 * q + t) * P:(2 * q + t + 1) * P], ident)
            mm.then_inc(done(p + "yt_ps"), 1)

        def pe_ffn(pe, ph):
            p, nch = ph["name"], ph["chunks"]

            def group(g, prev, nxt):
                front = pe_front(pe, ph, g + 1) if nxt else None
                for c in range(nch):
                    n = g * nch + c
                    if c == 0:
                        wait(pe, done(p + "xtl"), 2 * (g + 1))
                    for kind, bk, freed in (("gate", bank[c % 2], "silu"), ("up", bank[2 + c % 2], "t")):
                        wait(pe, done(p + freed), n - back(c, 2, nch) + 1)
                        for kk in range(2):
                            w = ffn_weights(ph, kind, kk, c)
                            mm = split_matmul(pe, bk[:, :], w_hi[:, w], w_lo[:, w],
                                              xt_hi[:, g % 2, kk, :], xt_lo[:, g % 2, kk, :], kk == 0, kk == 1)
                        mm.then_inc(done(p + kind + "_ps"), 1)
                    if ph["moe"]:
                        wait(pe, done(p + "h"), n)
                        wait(pe, done(p + "ct"), g + 1)
                        pe.matmul(bank[4][:, :], sel_sb[:, c * P:(c + 1) * P], c_t[:, g % 2, :],
                                  start=True, stop=True).then_inc(done(p + "cb_ps"), 1)
                    if c >= 2:
                        pe_down(pe, ph, g, c - 2, n - 2)
                    elif prev:
                        pe_down(pe, ph, g - 1, nch - 2 + c, n - 2)
                    if prev and c in ph["tail_at"]:
                        if c == ph["tail_at"][0]:
                            wait(pe, done(p + ("ct" if ph["moe"] else "xtl")), (1 if ph["moe"] else 2) * (g + 1))
                        pe_tail(pe, ph, g - 1, ph["tail_at"].index(c))
                    if nxt and c in ph["front_at"]:
                        next(front)

            for _ in pe_front(pe, ph, 0):
                pass
            group(0, False, True)
            with pe.Fori(1, NG - 1) as g:
                group(g, True, True)
            group(NG - 1, True, False)
            for c in (nch - 2, nch - 1):
                pe_down(pe, ph, NG - 1, c, (NG - 1) * nch + c)
            wait(pe, done(p + ("ct" if ph["moe"] else "xtl")), (1 if ph["moe"] else 2) * NG)
            for q in range(2):
                pe_tail(pe, ph, NG - 1, q)

        MOE = dict(name="b_", moe=True, chunks=NC0, gate=2, tail_at=(3, 4), front_at=(6, 7, 9, 10, 14))
        FFN = dict(name="d_", moe=False, chunks=NC1, gate=3, tail_at=(3, 4), front_at=(5, 6))

        @block.tensor
        def _(pe):
            def turn_a(b):
                wait(pe, done("a_xn"), b + 1)
                wait(pe, done("a_qt"), b)
                for f in range(2):
                    mm = pe.transpose(bank[4][:, f * P:(f + 1) * P], a_xnb[:, f * P:(f + 1) * P], ident)
                mm.then_inc(done("a_xt_ps"), 1)

            def step_a(i, u, score, turn, rest):
                if score:
                    wait(pe, done("a_qt"), i + 1)
                    wait(pe, done("a_kb"), 2 * (i + 1))
                    wait(pe, done("a_s"), 2 * i)
                    for f in range(2):
                        mm = pe.matmul(bank[f][:, :], a_qt[:, f, :], a_kb[:, u, f, :], start=True, stop=True)
                    mm.then_inc(done("a_s_ps"), 1)
                if rest:
                    j, w = i - 1, 1 - u
                    wait(pe, done("a_exp"), j + 1)
                    for h in range(2):
                        for c in range(4):
                            cc = 4 * h + c
                            mm = pe.transpose(bank[2 + h][:, c * P:(c + 1) * P], a_s[:, w, cc * P:(cc + 1) * P], ident)
                        mm.then_inc(done("a_pt_ps"), 1)
                if turn:
                    turn_a(i + 1)
                if rest:
                    wait(pe, done("a_v"), j + 1)
                    wait(pe, done("a_xm"), j)
                    pe.matmul(bank[7][:, 0:D], avg[:], a_v[:, w, :], start=True, stop=True).then_inc(done("a_m_ps"), 1)
                    wait(pe, done("a_pt"), 2 * j + 2)
                    wait(pe, done("a_at"), j)
                    for c in range(8):
                        r = 32 * (c % 4)
                        mm = pe.matmul(bank[5][r:r + 32, (c // 4) * P:(c // 4 + 1) * P], a_v[:, w, c * 32:(c + 1) * 32],
                                       a_ptb[:, c, :], start=True, stop=True)
                    mm.then_inc(done("a_pv_ps"), 1)
                    wait(pe, done("a_at"), j + 1)
                    wait(pe, done("a_tmp"), j)
                    for f in range(2):
                        mm = pe.transpose(bank[6][:, f * P:(f + 1) * P], a_at[:, f, :], ident)
                    mm.then_inc(done("a_o_ps"), 1)

            pe.wait_ge(done("setup_in"), 64)
            pe.wait_ge(done("avg_set"), 1)
            turn_a(0)
            step_a(0, 0, True, True, False)
            with pe.Fori(0, (NB - 2) // 2) as k:
                for u in (1, 0):
                    step_a(2 * k + 2 - u, u, True, True, True)
            step_a(NB - 1, 1, True, False, True)
            step_a(NB, 0, False, False, True)

            pe.wait_ge(done("a_x"), NB)
            pe.wait_ge(done("w0_lo0"), NB)
            pe.wait_ge(done("w0_lo1"), NB)
            pe.wait_ge(done("late_lo"), 1)
            pe.wait_ge(done("late_hi"), 2)
            pe_ffn(pe, MOE)

            pe.wait_ge(done("b_x"), 2 * NG)
            pe.wait_ge(done("late_lo"), 2)
            pe.wait_ge(done("ct_lo"), 1)
            for q in range(4):
                for kk in range(2):
                    mm = split_matmul(pe, bank[q][:, 0:D], ct_hi[:, kk, 2 * q:2 * q + 2, :], ct_lo[:, kk, 2 * q:2 * q + 2, :],
                                      xw_hi[:, 1, kk, :], xw_lo[:, 1, kk, :], kk == 0, kk == 1)
                mm.then_inc(done("k_ps"), 1)
            pe.wait_ge(done("ct_lo"), 3)
            for b in range(NB):
                wait(pe, done("v_m"), b - 3)
                for kk in range(2):
                    mm = split_matmul(pe, bank[4 + b % 4][:, 0:D], cd_hi[:, kk, b, :, :], cd_lo[:, kk, b, :, :],
                                      xw_hi[:, 2, kk, :], xw_lo[:, 2, kk, :], kk == 0, kk == 1)
                mm.then_inc(done("v_ps"), 1)
            for q in range(4):
                wait(pe, done("kn"), q + 1)
                for f in range(2):
                    mm = pe.transpose(bank[q][:, f * P:(f + 1) * P], kn_sb[:, q, f * P:(f + 1) * P], ident)
                mm.then_inc(done("kt_ps"), 1)

            def turn_tokens(src, bk):
                for f in range(2):
                    for t in range(2):
                        mm = pe.transpose(bk[:, f * SQ + t * P:f * SQ + (t + 1) * P], src[:, t, f * P:(f + 1) * P], ident)
                return mm

            def x_turn(b):
                wait(pe, done("c_xn"), 2 * (b + 1))
                wait(pe, done("c_qtl"), b)
                turn_tokens(c_xnb, bank[6]).then_inc(done("c_xt_ps"), 1)

            def q_proj(b):
                wait(pe, done("c_xtl"), b + 1)
                for t in range(2):
                    for kk in range(2):
                        tok = slice(t * P, (t + 1) * P)
                        mm = split_matmul(pe, bank[6][:, t * D:(t + 1) * D], c_xth[:, kk, tok], c_xtl[:, kk, tok],
                                          xw_hi[:, 0, kk, :], xw_lo[:, 0, kk, :], kk == 0, kk == 1)
                mm.then_inc(done("c_q_ps"), 1)

            def p_turn(b, t):
                wait(pe, done("c_exp"), 2 * b + t + 1)
                for h in range(2):
                    if t == 1:
                        pe.wait_ge(done("c_pt"), 4 * b + h + 1)
                    if t == 0 and h == 0:
                        wait(pe, done("c_rd"), b)
                    for c in range(4):
                        cc = 4 * h + c
                        mm = pe.transpose(bank[4 + h][:, c * P:(c + 1) * P], c_e[:, t, cc * P:(cc + 1) * P], ident)
                    mm.then_inc(done("c_pt_ps"), 1)

            def scores(b, t):
                wait(pe, done("c_qtl"), b + 1)
                wait(pe, done("c_kb"), 4 * (b + 1))
                wait(pe, done("c_sub"), 4 * b + 2 * t - 2)
                tok = slice(t * P, (t + 1) * P)
                for f in range(2):
                    mm = split_matmul(pe, bank[2 * t + f][:, :], c_qth[:, f, tok], c_qtl[:, f, tok],
                                      c_kbh[:, f, :], c_kbl[:, f, :], True, True)
                mm.then_inc(done("c_s_ps"), 1)

            def step_c(i, mid, front, rest):
                j = i - 1
                if mid:
                    wait(pe, done("c_qn"), 2 * (i + 1))
                    turn_tokens(c_qnb, bank[6]).then_inc(done("c_qt_ps"), 1)
                if rest:
                    p_turn(j, 0)
                if mid:
                    scores(i, 0)
                if front:
                    x_turn(i + 1)
                if rest:
                    p_turn(j, 1)
                if mid:
                    scores(i, 1)
                if rest:
                    wait(pe, done("c_pt"), 4 * j + 4)
                    wait(pe, done("c_v"), j + 1)
                    wait(pe, done("c_x"), j)
                    for dst, w, what in ((bank[4], None, "c_d_ps"), (bank[7], c_v, "c_pv_ps")):
                        for c in range(8):
                            r = 32 * (c % 4)
                            lhs = oneblk if w is None else w[:, c * 32:(c + 1) * 32]
                            mm = pe.matmul(dst[r:r + 32, (c // 4) * SQ:(c // 4 + 1) * SQ], lhs, c_ptb[:, c, :],
                                           start=True, stop=True)
                        mm.then_inc(done(what), 1)
                if front:
                    q_proj(i + 1)
                if rest:
                    wait(pe, done("c_atl"), j + 1)
                    for t in range(2):
                        tok = slice(t * P, (t + 1) * P)
                        for kk in range(2):
                            mm = split_matmul(pe, bank[7][:, t * D:(t + 1) * D], c_athb[:, kk, tok], c_atlb[:, kk, tok],
                                              xw_hi[:, 3, kk, :], xw_lo[:, 3, kk, :], kk == 0, kk == 1)
                    mm.then_inc(done("c_o_ps"), 1)

            pe.wait_ge(done("kt_lo"), 4)
            pe.wait_ge(done("v1_set"), NB)
            x_turn(0)
            q_proj(0)
            step_c(0, True, True, False)
            with pe.Fori(1, NB - 1) as i:
                step_c(i, True, True, True)
            step_c(NB - 1, True, False, True)
            step_c(NB, False, False, True)

            pe.wait_ge(done("c_x"), NB)
            pe.wait_ge(done("w1_lo"), NB)
            pe_ffn(pe, FFN)

        def act_front(act, ph, g):
            p = ph["name"]
            for f in range(2):
                wait(act, done(p + "xt_ps"), 2 * g + f + 1)
                act.activation(xt_hi[:, g % 2, f, :], bank[7][:, :], ACT.Copy).then_inc(done(p + "xth"), 1)
                yield
            if ph["moe"]:
                wait(act, done(p + "lg_ps"), g + 1)
                act.activation(lgt[:], bank[7][:, :], ACT.Copy).then_inc(done(p + "lgt"), 1)
                yield
                wait(act, done(p + "z"), g + 1)
                act.activation(r_p[:], r_z[:], ACT.Exp).then_inc(done(p + "e"), 1)
                act.activation(r_es[:], lg[:, :, 8:9], ACT.Exp, scale=-1.0).then_inc(done(p + "es"), 1)
                yield
                wait(act, done(p + "ct_ps"), g + 1)
                act.activation(c_t[:, g % 2, :], bank[7][:, :], ACT.Copy).then_inc(done(p + "ct"), 1)
                yield

        def act_ffn(act, ph):
            p, nch = ph["name"], ph["chunks"]

            def hi(c, n):
                wait(act, done(p + ("h" if ph["moe"] else "t")), n + 1)
                wait(act, done(p + "dn"), n - back(c, 3, nch) + 1)
                act.activation(h_hi[:, c % 3, :], h_sb[:, c % 2, :], ACT.Copy).then_inc(done(p + "hhi"), 1)

            def y_out(g):
                wait(act, done(p + "dn"), (g + 1) * nch)
                wait(act, done(p + "yt_ps"), 2 * g)
                for f in range(2):
                    act.activation(y_t[:, f, :], bank[5 + f][:, :], ACT.Copy).then_inc(done(p + "y"), 1)

            def group(g, prev, nxt):
                front = act_front(act, ph, g + 1) if nxt else None
                for c in range(nch):
                    n = g * nch + c
                    wait(act, done(p + "gate_ps"), n + 1)
                    wait(act, done(p + "t"), n - back(c, 2, nch) + 1)
                    act.activation(s_sb[:, c % 2, :], bank[c % 2][:, :], ACT.Silu).then_inc(done(p + "silu"), 1)
                    if c >= 1:
                        hi(c - 1, n - 1)
                    elif prev:
                        hi(nch - 1, n - 1)
                    if prev and c == 2:
                        y_out(g - 1)
                    if nxt and c in ph["front_at"]:
                        next(front)

            for _ in act_front(act, ph, 0):
                pass
            group(0, False, True)
            with act.Fori(1, NG - 1) as g:
                group(g, True, True)
            group(NG - 1, True, False)
            hi(nch - 1, NG * nch - 1)
            y_out(NG - 1)

        @block.scalar
        def _(act):
            act.wait_ge(done("gates_in"), 32)
            act.activation(gates[:], gates[:], ACT.Tanh).then_inc(done("gates"), 1)

            def q_out(b):
                wait(act, done("a_xt_ps"), b + 1)
                wait(act, done("a_s_ps"), b)
                act.activation(a_qt[:], bank[4][:, 0:D].rearrange("p (f t) -> p f t", f=2), ACT.Copy).then_inc(done("a_qt"), 1)

            def step_a(i, u, score, turn, rest):
                j = i - 1
                if score:
                    wait(act, done("a_s_ps"), i + 1)
                    wait(act, done("a_pt_ps"), 2 * (i - 1))
                    wait(act, done("a_sm"), i - 1)
                    act.activation(a_s[:, u, 0:512], bank[0][:, :], ACT.Copy).then_inc(done("a_s"), 1)
                    act.activation(a_s[:, u, 512:1024], bank[1][:, :], ACT.Copy).then_inc(done("a_s"), 1)
                if rest:
                    for h in range(2):
                        wait(act, done("a_pt_ps"), 2 * j + h + 1)
                        wait(act, done("a_pv_ps"), j)
                        act.activation(a_ptb[:, 4 * h:4 * h + 4, :], bank[2 + h][:, :].rearrange("p (c t) -> p c t", c=4),
                                       ACT.Copy).then_inc(done("a_pt"), 1)
                if turn:
                    q_out(i + 1)
                if score:
                    for w in range(2):
                        wait(act, done(f"w0_in{w}"), 16 * (i + 1))
                        act.activation(w_hi[:, bass.ds((2 * i + w) * PIECE0, PIECE0)], stage[:, w], ACT.Copy)\
                           .then_inc(done(f"w0_hi{w}"), 1)
                if rest:
                    wait(act, done("a_pv_ps"), j + 1)
                    wait(act, done("a_o_ps"), j)
                    act.activation(a_at[:], bank[5][:, 0:D].rearrange("p (f t) -> p f t", f=2), ACT.Copy).then_inc(done("a_at"), 1)
                if score:
                    wait(act, done("a_sub"), i + 1)
                    act.activation(a_s[:, u, :], a_s[:, u, :], ACT.Exp, scale=SCALE).then_inc(done("a_exp"), 1)

            q_out(0)
            step_a(0, 0, True, True, False)
            with act.Fori(0, (NB - 2) // 2) as k:
                for u in (1, 0):
                    step_a(2 * k + 2 - u, u, True, True, True)
            step_a(NB - 1, 1, True, False, True)
            act.wait_ge(done("late_in"), 64)
            act.activation(rw_hi[:], rw_raw[:], ACT.Copy).then_inc(done("late_hi"), 1)
            act.activation(sel_sb[:], sel_raw[:], ACT.Copy).then_inc(done("late_hi"), 1)
            act.activation(xw_hi[:], xw_raw[:], ACT.Copy).then_inc(done("late_hi"), 1)
            step_a(NB, 0, False, False, True)

            act.wait_ge(done("a_x"), NB)
            act.wait_ge(done("late_lo"), 2)
            act_ffn(act, MOE)

            act.wait_ge(done("b_x"), 2 * NG)
            act.wait_ge(done("ctxt2_in"), 16)
            act.activation(ct_hi[:], ctxt2[:].rearrange("p f (b k) -> p f b k", b=NB), ACT.Copy).then_inc(done("ct_hi"), 1)
            for half in range(2):
                act.activation(cd_hi[:, :, :, half, :], ctxt2[:].rearrange("p f (b k) -> p f b k", b=NB), ACT.Copy)\
                   .then_inc(done("ct_hi"), 1)
            for q in range(4):
                wait(act, done("k_b"), q + 1)
                wait(act, done("k_sq"), q)
                act.activation(k_sq[:], k_sb[:, q, :], ACT.Square, scale=RMS_SCALE, accum_out=k_ss[:, q:q + 1]).then_inc(done("k_sq"), 1)
            for q in range(4):
                wait(act, done("kt_ps"), q + 1)
                act.activation(kt_hi[:, :, q * P:(q + 1) * P], bank[q][:, 0:D].rearrange("p (f t) -> p f t", f=2),
                               ACT.Copy).then_inc(done("kt_hi"), 1)

            def halves(bk):
                return bk[:, :].rearrange("p (f t) -> p f t", f=2)

            def xt_out(b):
                wait(act, done("c_xt_ps"), b + 1)
                wait(act, done("c_q_ps"), b)
                act.activation(c_xth[:], halves(bank[6]), ACT.Copy).then_inc(done("c_xth"), 1)

            def squares(b):
                wait(act, done("c_q"), b + 1)
                wait(act, done("c_rq_ve"), b)
                wait(act, done("c_qt_ps"), b)
                for t in range(2):
                    act.activation(c_qnb[:, t, :], c_qb[:, t, :], ACT.Square, scale=RMS_SCALE, accum_out=c_ss[:, t:t + 1]).then_inc(done("c_sq"), 1)

            def p_out(b, t):
                for h in range(2):
                    n = 4 * b + 2 * t + h
                    wait(act, done("c_pt_ps"), n + 1)
                    wait(act, done("c_pv_ps"), b)
                    act.activation(c_ptb[:, 4 * h:4 * h + 4, t * P:(t + 1) * P],
                                   bank[4 + h][:, :].rearrange("p (c t) -> p c t", c=4), ACT.Copy).then_inc(done("c_pt"), 1)

            def exps(b, t):
                wait(act, done("c_sub"), 4 * b + 2 * t + 2)
                act.activation(c_e[:, t, :], c_e[:, t, :], ACT.Exp, scale=SCALE).then_inc(done("c_exp"), 1)

            def step_c(i, mid, front, rest):
                j = i - 1
                if mid:
                    wait(act, done("c_qt_ps"), i + 1)
                    wait(act, done("c_s_ps"), 2 * i)
                    act.activation(c_qth[:], halves(bank[6]), ACT.Copy).then_inc(done("c_qth"), 1)
                if rest:
                    p_out(j, 0)
                if front:
                    xt_out(i + 1)
                if mid:
                    exps(i, 0)
                if rest:
                    p_out(j, 1)
                if mid:
                    exps(i, 1)
                if front:
                    squares(i + 1)
                if mid:
                    wait(act, done("w1_in"), 16 * (i + 1))
                    act.activation(w_hi[:, bass.ds(i * PIECE1, PIECE1)], stage[:, 0, 0:PIECE1], ACT.Copy).then_inc(done("w1_hi"), 1)
                if rest:
                    wait(act, done("c_at"), j + 1)
                    wait(act, done("c_o_ps"), j)
                    act.activation(c_athb[:], c_atb[:], ACT.Copy).then_inc(done("c_ath"), 1)

            xt_out(0)
            squares(0)
            step_c(0, True, True, False)
            with act.Fori(1, NB - 1) as i:
                step_c(i, True, True, True)
            step_c(NB - 1, True, False, True)
            step_c(NB, False, False, True)

            act.wait_ge(done("c_x"), NB)
            act_ffn(act, FFN)

        def dve_stats(dve, ph, g):
            p = ph["name"]
            wait(dve, done(p + "xn"), GT * g)
            for t in range(GT):
                dve.bn_stats(stat[:, t, :], x_sb[:, GT * g + t, :]).then_inc(done(p + "bn"), 1)

        def dve_aggr(dve, ph):
            for t in range(GT):
                dve.bn_aggr(mv[:, t, :], stat[:, t, :]).then_inc(done(ph["name"] + "mv"), 1)

        def dve_norm(dve, ph, g):
            p = ph["name"]
            dve.wait_ge(done(p + "rstd"), g + 1)
            wait(dve, done(p + "xt_ps"), 2 * g)
            for t in range(GT):
                dve.tensor_scalar(f_xnb[:, t, :], x_sb[:, GT * g + t, :], mv[:, t, 0:1], rstd[:, t:t + 1],
                                  ALU.subtract, ALU.mult).then_inc(done(p + "xn"), 1)

        def dve_front(dve, ph, g):
            p = ph["name"]
            for f in range(2):
                dve.wait_ge(done(p + "xth"), 2 * g + f + 1)
                dve.tensor_tensor(xt_lo[:, g % 2, f, :], bank[7][:, :], xt_hi[:, g % 2, f, :].bitcast(F32),
                                  ALU.subtract).then_inc(done(p + "xtl"), 1)
                yield
            if ph["moe"]:
                dve.wait_ge(done(p + "lt_ps"), g + 1)
                wait(dve, done(p + "c"), g)
                dve.tensor_copy(lg[:], bank[7][:, :].rearrange("p (t e) -> p t e", t=GT)[:, :, 0:9]).then_inc(done(p + "lg"), 1)
                dve.wait_ge(done(p + "lg"), g + 1)
                dve.tensor_reduce(r_m[:], lg[:, :, 0:8], AX.X, ALU.max).then_inc(done(p + "m"), 1)
                dve.wait_ge(done(p + "m"), g + 1)
                dve.tensor_tensor(r_z[:], lg[:, :, 0:8], over(r_m), ALU.subtract).then_inc(done(p + "z"), 1)
                yield
                dve.wait_ge(done(p + "es"), g + 1)
                n = [0]

                def link(ins):
                    n[0] += 1
                    ins.then_inc(done(p + "r"), 1)
                    dve.wait_ge(done(p + "r"), ROUTER_STEPS * g + n[0])

                link(dve.tensor_reduce(r_den[:, :, 0:1], r_p[:], AX.X, ALU.add))
                link(dve.tensor_scalar(r_den[:, :, 1:2], r_es[:], 1.0, None, ALU.add))
                link(dve.reciprocal(r_inv[:], r_den[:]))
                link(dve.tensor_tensor(r_p[:], r_p[:], r_inv[:, :, 0:1].broadcast_to([P, GT, 8]), ALU.mult))
                link(dve.tensor_reduce(r_m[:], r_p[:], AX.X, ALU.max))
                link(dve.tensor_tensor(r_k[:], r_p[:], over(r_m), ALU.is_equal))
                link(dve.tensor_tensor(r_k[:], r_k[:], w8.unsqueeze(1).broadcast_to([P, GT, 8]), ALU.mult))
                link(dve.tensor_reduce(r_m[:], r_k[:], AX.X, ALU.max))
                link(dve.tensor_tensor(r_o1[:], r_k[:], over(r_m), ALU.is_equal))
                link(dve.scalar_tensor_tensor(out=r_z[:], in0=r_o1[:], scalar=-2.0, in1=r_p[:], op0=ALU.mult, op1=ALU.add))
                link(dve.tensor_reduce(r_m[:], r_z[:], AX.X, ALU.max))
                link(dve.tensor_tensor(r_k[:], r_z[:], over(r_m), ALU.is_equal))
                link(dve.tensor_tensor(r_k[:], r_k[:], w8.unsqueeze(1).broadcast_to([P, GT, 8]), ALU.mult))
                link(dve.tensor_reduce(r_m[:], r_k[:], AX.X, ALU.max))
                link(dve.tensor_tensor(r_o2[:], r_k[:], over(r_m), ALU.is_equal))
                link(dve.tensor_tensor(r_o1[:], r_o1[:], r_o2[:], ALU.add))
                link(dve.tensor_tensor(r_c[:, :, 0:8], r_o1[:], r_p[:], ALU.mult))
                link(dve.tensor_copy(r_c[:, :, 8:9], r_inv[:, :, 1:2]))
                wait(dve, done(p + "ct_ps"), g)
                link(dve.tensor_copy(r_cd[:, :, 0:9], r_c[:]))
                assert n[0] == ROUTER_STEPS
                dve.tensor_tensor(r_cd[:, :, 32:41], r_c[:], r_cd[:, :, 0:9].bitcast(F32), ALU.subtract)\
                   .then_inc(done(p + "c"), 1)
                yield
                yield

        ROUTER_STEPS = 19

        def over(m):
            return m[:].unsqueeze(2).broadcast_to([P, GT, 8])

        def dve_ffn(dve, ph):
            p, nch = ph["name"], ph["chunks"]

            def tail(g, q):
                dve.wait_ge(done(p + "yt_ps"), 2 * g + q + 1)
                xs = x_sb[:, bass.ds(GT * g + 2 * q, 2), :]
                dve.scalar_tensor_tensor(out=xs, in0=bank[7][:, :].rearrange("p (t d) -> p t d", t=2),
                                         scalar=gates[:, ph["gate"]:ph["gate"] + 1], in1=xs,
                                         op0=ALU.mult, op1=ALU.add).then_inc(done(p + "x"), 1)

            def group(g, prev, nxt):
                front = dve_front(dve, ph, g + 1) if nxt else None
                for c in range(nch):
                    n = g * nch + c
                    if nxt and c == 1:
                        dve.wait_ge(done(p + "bn"), GT * (g + 2))
                    dve.wait_ge(done(p + "silu"), n + 1)
                    dve.wait_ge(done(p + "up_ps"), n + 1)
                    wait(dve, done(p + "h" if ph["moe"] else p + "hlo"), n - back(c, 2, nch) + 1)
                    if ph["moe"]:
                        dve.tensor_tensor(t_sb[:, c % 2, :], s_sb[:, c % 2, :], bank[2 + c % 2][:, :], ALU.mult)\
                           .then_inc(done(p + "t"), 1)
                        dve.wait_ge(done(p + "t"), n + 1)
                        dve.wait_ge(done(p + "cb_ps"), n + 1)
                        wait(dve, done(p + "hlo"), n - back(c, 2, nch) + 1)
                        dve.tensor_tensor(h_sb[:, c % 2, :], t_sb[:, c % 2, :], bank[4][:, :], ALU.mult)\
                           .then_inc(done(p + "h"), 1)
                    else:
                        dve.tensor_tensor(h_sb[:, c % 2, :], s_sb[:, c % 2, :], bank[2 + c % 2][:, :], ALU.mult)\
                           .then_inc(done(p + "t"), 1)
                    if nxt and c == 0:
                        dve_stats(dve, ph, g + 1)
                    if nxt and c == 1:
                        dve_aggr(dve, ph)
                    if nxt and c == 2:
                        dve_norm(dve, ph, g + 1)
                    if prev and c in ph["tail_at"]:
                        tail(g - 1, ph["tail_at"].index(c))
                    if nxt and c in ph["front_at"]:
                        next(front)

            dve_stats(dve, ph, 0)
            dve.wait_ge(done(p + "bn"), GT)
            dve_aggr(dve, ph)
            dve_norm(dve, ph, 0)
            for _ in dve_front(dve, ph, 0):
                pass
            group(0, False, True)
            with dve.Fori(1, NG - 1) as g:
                group(g, True, True)
            group(NG - 1, True, False)
            for q in range(2):
                tail(NG - 1, q)

        @block.vector
        def _(dve):
            dve.memset(avg[:], 1.0 / SK).then_inc(done("avg_set"), 1)

            def stats_a(b):
                wait(dve, done("a_xn"), b)
                dve.bn_stats(stat[:, 0, :], x_sb[:, 2 * b + 1, :]).then_inc(done("a_bn"), 1)
                dve.wait_ge(done("a_bn"), b + 1)

            def aggr_a():
                dve.bn_aggr(mv[:, 0, :], stat[:, 0, :]).then_inc(done("a_mv"), 1)

            def norm_a(b):
                dve.wait_ge(done("a_rstd"), b + 1)
                wait(dve, done("a_xt_ps"), b)
                dve.tensor_scalar(a_xnb[:], x_sb[:, 2 * b + 1, :], mv[:, 0, 0:1], rstd[:, 0:1],
                                  ALU.subtract, ALU.mult).then_inc(done("a_xn"), 1)

            def by_key(t):
                return t.rearrange("p (h k) -> p h k", h=NH)

            def per_head(t):
                return t.unsqueeze(2).broadcast_to([P, NH, SK])

            def step_a(i, u, score, turn, rest):
                j = i - 1
                if turn:
                    stats_a(i + 1)
                if score:
                    dve.wait_ge(done("a_msk"), i + 1)
                    dve.tensor_reduce(a_mx[:], by_key(a_s[:, u, :]), AX.X, ALU.max).then_inc(done("a_mx"), 1)
                    if turn:
                        aggr_a()
                    dve.wait_ge(done("a_mx"), i + 1)
                    dve.tensor_tensor(by_key(a_s[:, u, :]), by_key(a_s[:, u, :]), per_head(a_mx[:]), ALU.subtract)\
                       .then_inc(done("a_sub"), 1)
                if turn:
                    norm_a(i + 1)
                if score:
                    dve.wait_ge(done("w0_hi1"), i + 1)
                    dve.tensor_tensor(w_lo[:, bass.ds((2 * i + 1) * PIECE0, PIECE0)], stage[:, 1],
                                      w_hi[:, bass.ds((2 * i + 1) * PIECE0, PIECE0)].bitcast(F32), ALU.subtract)\
                       .then_inc(done("w0_lo1"), 1)
                if rest:
                    dve.wait_ge(done("a_exp"), j + 1)
                    dve.tensor_reduce(a_sm[:], by_key(a_s[:, 1 - u, :]), AX.X, ALU.add).then_inc(done("a_sm"), 1)
                    dve.wait_ge(done("a_sm"), j + 1)
                    dve.reciprocal(a_ri[:], a_sm[:]).then_inc(done("a_ri"), 1)
                    dve.wait_ge(done("a_ri"), j + 1)
                    dve.wait_ge(done("a_o_ps"), j + 1)
                    dve.tensor_tensor(a_tmpb[:].rearrange("p (h e) -> p h e", h=NH),
                                      bank[6][:, 0:D].rearrange("p (h e) -> p h e", h=NH),
                                      a_ri[:].unsqueeze(2).broadcast_to([P, NH, HD]), ALU.mult).then_inc(done("a_tmp"), 1)
                    dve.wait_ge(done("a_tmp"), j + 1)
                    xs = x_sb[:, 2 * j + 1, :]
                    dve.scalar_tensor_tensor(out=xs, in0=a_tmpb[:], scalar=gates[:, 0:1], in1=xs,
                                             op0=ALU.mult, op1=ALU.add).then_inc(done("a_x"), 1)
                    dve.wait_ge(done("a_m_ps"), j + 1)
                    xs = x_sb[:, 2 * j, :]
                    dve.scalar_tensor_tensor(out=xs, in0=bank[7][:, 0:D], scalar=gates[:, 0:1], in1=xs,
                                             op0=ALU.mult, op1=ALU.add).then_inc(done("a_xm"), 1)
                    dve.wait_ge(done("a_x"), j + 1)

            dve.wait_ge(done("x0_in"), 16)
            stats_a(0)
            aggr_a()
            norm_a(0)
            dve.wait_ge(done("x1_in"), 16)
            dve.wait_ge(done("gates"), 1)
            step_a(0, 0, True, True, False)
            dve.wait_ge(done("x_in"), 32)
            with dve.Fori(0, (NB - 2) // 2) as k:
                for u in (1, 0):
                    step_a(2 * k + 2 - u, u, True, True, True)
            step_a(NB - 1, 1, True, False, True)
            dve.wait_ge(done("late_hi"), 1)
            dve.tensor_tensor(rw_lo[:], rw_raw[:], rw_hi[:].bitcast(F32), ALU.subtract).then_inc(done("late_lo"), 1)
            dve.wait_ge(done("late_hi"), 3)
            dve.tensor_tensor(xw_lo[:], xw_raw[:], xw_hi[:].bitcast(F32), ALU.subtract).then_inc(done("late_lo"), 1)
            step_a(NB, 0, False, False, True)

            dve.wait_ge(done("a_xm"), NB)
            dve.wait_ge(done("late_lo"), 2)
            dve.wait_ge(done("late_hi"), 2)
            dve.memset(r_cd[:].bitcast(F32), 0.0).then_inc(done("cd_zero"), 1)
            dve.wait_ge(done("cd_zero"), 1)
            dve_ffn(dve, MOE)

            dve.wait_ge(done("b_x"), 2 * NG)
            dve.wait_ge(done("late_in"), 64)
            dve.tensor_tensor(bias_sb[:, 2, :], bias_sb[:, 2, :], vmask, ALU.mult).then_inc(done("bvm"), 1)
            dve.tensor_scalar(bias_sb[:, 3, :], bias_sb[:, 3, :], gates[:, 1:2], None, ALU.mult).then_inc(done("tgbo"), 1)
            dve.wait_ge(done("ct_hi"), 1)
            dve.tensor_tensor(ct_lo[:], ctxt2[:].rearrange("p f (b k) -> p f b k", b=NB), ct_hi[:].bitcast(F32), ALU.subtract)\
               .then_inc(done("ct_lo"), 1)
            for half in range(2):
                dve.wait_ge(done("ct_hi"), half + 2)
                dve.tensor_tensor(cd_lo[:, :, :, half, :], ctxt2[:].rearrange("p f (b k) -> p f b k", b=NB),
                                  cd_hi[:, :, :, half, :].bitcast(F32), ALU.subtract).then_inc(done("ct_lo"), 1)
            for q in range(4):
                dve.wait_ge(done("k_ps"), q + 1)
                dve.tensor_tensor(k_sb[:, q, :], bank[q][:, 0:D], bias_sb[:, 1, :], ALU.add).then_inc(done("k_b"), 1)
            for b in range(NB):
                dve.wait_ge(done("v_ps"), b + 1)
                wait(dve, done("v1_set"), b - 1)
                dve.tensor_tensor(v_t[:, b % 2, :], bank[4 + b % 4][:, 0:D], vmask, ALU.mult).then_inc(done("v_m"), 1)
                dve.wait_ge(done("v_m"), b + 1)
                dve.wait_ge(done("bvm"), 1)
                dve.tensor_tensor(v1[:, b, :], v_t[:, b % 2, :], bias_sb[:, 2, :], ALU.add).then_inc(done("v1_set"), 1)
            dve.wait_ge(done("k_r"), 1)
            for q in range(4):
                dve.scalar_tensor_tensor(out=kn_sb[:, q, :], in0=k_sb[:, q, :], scalar=rstd[:, q:q + 1], in1=bias_sb[:, 5, :],
                                         op0=ALU.mult, op1=ALU.mult).then_inc(done("kn"), 1)
            for q in range(4):
                dve.wait_ge(done("kt_hi"), q + 1)
                dve.tensor_tensor(kt_lo[:, :, q * P:(q + 1) * P], bank[q][:, 0:D].rearrange("p (f t) -> p f t", f=2),
                                  kt_hi[:, :, q * P:(q + 1) * P].bitcast(F32), ALU.subtract).then_inc(done("kt_lo"), 1)

            def halves(bk):
                return bk[:, :].rearrange("p (f t) -> p f t", f=2)

            def stats_c(b):
                wait(dve, done("c_xn"), 2 * b)
                for t in range(2):
                    dve.bn_stats(stat[:, t, :], x_sb[:, 2 * b + t, :]).then_inc(done("c_bn"), 1)
                dve.wait_ge(done("c_bn"), 2 * (b + 1))

            def norm_c(b):
                for t in range(2):
                    dve.bn_aggr(mv[:, t, :], stat[:, t, :]).then_inc(done("c_mv"), 1)
                dve.wait_ge(done("c_rstd"), b + 1)
                wait(dve, done("c_xt_ps"), b)
                for t in range(2):
                    dve.tensor_scalar(c_xnb[:, t, :], x_sb[:, 2 * b + t, :], mv[:, t, 0:1], rstd[:, t:t + 1],
                                      ALU.subtract, ALU.mult).then_inc(done("c_xn"), 1)

            def xt_low(b):
                dve.wait_ge(done("c_xth"), b + 1)
                dve.tensor_tensor(c_xtl[:], halves(bank[6]), c_xth[:].bitcast(F32), ALU.subtract).then_inc(done("c_xtl"), 1)

            def q_bias(b):
                dve.wait_ge(done("c_q_ps"), b + 1)
                wait(dve, done("c_qn"), 2 * b)
                dve.tensor_tensor(c_qb[:], halves(bank[6]), bias_sb[:, 0, :].unsqueeze(1).broadcast_to([P, 2, D]), ALU.add)\
                   .then_inc(done("c_q"), 1)

            def q_norm(b):
                dve.wait_ge(done("c_rq"), b + 1)
                wait(dve, done("c_qt_ps"), b)
                for t in range(2):
                    dve.scalar_tensor_tensor(out=c_qnb[:, t, :], in0=c_qb[:, t, :], scalar=c_rq[:, t:t + 1], in1=bias_sb[:, 4, :],
                                             op0=ALU.mult, op1=ALU.mult).then_inc(done("c_qn"), 1)

            def shift(b, t):
                dve.wait_ge(done("c_s_ps"), 2 * b + t + 1)
                for f in range(2):
                    n = 4 * b + 2 * t + f
                    dve.tensor_reduce(c_mx[:, t, 8 * f:8 * f + 8], bank[2 * t + f][:, :].rearrange("p (h k) -> p h k", h=8),
                                      AX.X, ALU.max).then_inc(done("c_mx"), 1)
                wait(dve, done("c_pt_ps"), 4 * b + 2 * t - 2)
                for f in range(2):
                    dve.wait_ge(done("c_mx"), 4 * b + 2 * t + f + 1)
                    sub = dve.tensor_tensor(c_e[:, t, 512 * f:512 * f + 512].rearrange("p (h k) -> p h k", h=8),
                                            bank[2 * t + f][:, :].rearrange("p (h k) -> p h k", h=8),
                                            c_mx[:, t, 8 * f:8 * f + 8].unsqueeze(2).broadcast_to([P, 8, SK]), ALU.subtract)
                    sub.then_inc(done("c_sub"), 1)

            def step_c(i, mid, front, rest):
                j = i - 1
                if front:
                    stats_c(i + 1)
                if mid:
                    dve.wait_ge(done("c_qth"), i + 1)
                    dve.tensor_tensor(c_qtl[:], halves(bank[6]), c_qth[:].bitcast(F32), ALU.subtract).then_inc(done("c_qtl"), 1)
                if front:
                    norm_c(i + 1)
                if mid:
                    shift(i, 0)
                if front:
                    xt_low(i + 1)
                if mid:
                    shift(i, 1)
                if rest:
                    dve.wait_ge(done("c_d_ps"), j + 1)
                    wait(dve, done("c_atl"), j)
                    dve.reciprocal(c_atb[:], halves(bank[4])).then_inc(done("c_rd"), 1)
                    dve.wait_ge(done("c_rd"), j + 1)
                    dve.wait_ge(done("c_pv_ps"), j + 1)
                    dve.tensor_tensor(c_atb[:], halves(bank[7]), c_atb[:], ALU.mult).then_inc(done("c_at"), 1)
                if front:
                    q_bias(i + 1)
                    q_norm(i + 1)
                if rest:
                    dve.wait_ge(done("c_o_ps"), j + 1)
                    dve.wait_ge(done("c_xb"), j + 1)
                    xs = x_sb[:, bass.ds(2 * j, 2), :]
                    dve.scalar_tensor_tensor(out=xs, in0=halves(bank[7]), scalar=gates[:, 1:2], in1=xs,
                                             op0=ALU.mult, op1=ALU.add).then_inc(done("c_x"), 1)

            stats_c(0)
            norm_c(0)
            xt_low(0)
            q_bias(0)
            q_norm(0)
            step_c(0, True, True, False)
            with dve.Fori(1, NB - 1) as i:
                step_c(i, True, True, True)
            step_c(NB - 1, True, False, True)
            step_c(NB, False, False, True)

            dve.wait_ge(done("c_x"), NB)
            dve_ffn(dve, FFN)

        def power(pool, var, scratch, dst, eps, after, name):
            n = var.shape[1]
            pool.tensor_tensor(scratch, var, eps[:, 0:n], ALU.add).then_inc(done(name + "_ve"), 1)
            pool.wait_ge(done(name + "_ve"), after)
            pool.tensor_tensor(dst, scratch, neghalf[:, 0:n], ALU.pow).then_inc(done(name), 1)

        def pool_ffn(pool, ph):
            p, nch = ph["name"], ph["chunks"]

            def rsqrt(g):
                pool.wait_ge(done(p + "mv"), GT * (g + 1))
                wait(pool, done(p + "xn"), GT * g)
                power(pool, mv[:, :, 1], ve[:], rstd[:], ln_eps, g + 1, p + "rstd")

            def group(g, nxt):
                for c in range(nch):
                    n = g * nch + c
                    if nxt and c == 1:
                        rsqrt(g + 1)
                    pool.wait_ge(done(p + "hhi"), n + 1)
                    wait(pool, done(p + "dn"), n - back(c, 3, nch) + 1)
                    pool.tensor_tensor(h_lo[:, c % 3, :], h_sb[:, c % 2, :], h_hi[:, c % 3, :].bitcast(F32), ALU.subtract)\
                        .then_inc(done(p + "hlo"), 1)

            rsqrt(0)
            group(0, True)
            with pool.Fori(1, NG - 1) as g:
                group(g, True)
            group(NG - 1, False)

        def spread(pool, dst, keys):
            return pool.tensor_tensor(dst.rearrange("p (h k) -> p h k", h=8), keys.unsqueeze(1).broadcast_to([P, 8, SK]),
                                      headmask.unsqueeze(2).broadcast_to([P, 8, SK]), ALU.mult)

        @block.gpsimd
        def _(pool):
            def rsqrt_a(b):
                pool.wait_ge(done("a_mv"), b + 1)
                power(pool, mv[:, 0, 1:2], ve[:, 0:1], rstd[:, 0:1], ln_eps, b + 1, "a_rstd")

            def keys_a(b, u):
                wait(pool, done("a_s_ps"), b - 1)
                spread(pool, a_kb[:, u, 0, :], ctxt[:, 0, bass.ds(b * SK, SK)]).then_inc(done("a_kb"), 1)
                spread(pool, a_kb[:, u, 1, :], ctxt[:, 1, bass.ds(b * SK, SK)]).then_inc(done("a_kb"), 1)

            def values_a(b, u):
                wait(pool, done("a_m_ps"), b - 1)
                wait(pool, done("a_pv_ps"), b - 1)
                pool.tensor_tensor(a_v[:, u, :], ctxd[:, b, :], vmask, ALU.mult).then_inc(done("a_v"), 1)

            def step_a(i, u, turn):
                fill = pool.to_reg(MASKED)
                n = 2 * (i + 1)
                if not isinstance(n, int):
                    n = pool.to_reg(n)
                pool.wait_ge(done("setup_in"), 64)
                pool.wait_ge(done("a_s"), n)
                v = a_s[:, u, :].rearrange("p (h k) -> p h k", h=NH)
                pool.affine_select(out=v, in_=v, compare_op=ALU.is_ge, fill=fill, base=-SK,
                                   pattern=[[0, NH], [-1, SK]], channel_multiplier=1).then_inc(done("a_msk"), 1)
                if turn:
                    rsqrt_a(i + 1)
                    keys_a(i + 1, 1 - u)
                    values_a(i + 1, 1 - u)
                pool.wait_ge(done("w0_hi0"), i + 1)
                at = bass.ds(2 * i * PIECE0, PIECE0)
                pool.tensor_tensor(w_lo[:, at], stage[:, 0], w_hi[:, at].bitcast(F32), ALU.subtract).then_inc(done("w0_lo0"), 1)

            pool.wait_ge(done("setup_in"), 64)
            rsqrt_a(0)
            keys_a(0, 0)
            values_a(0, 0)
            step_a(0, 0, True)
            with pool.Fori(0, (NB - 2) // 2) as k:
                for u in (1, 0):
                    step_a(2 * k + 2 - u, u, True)
            step_a(NB - 1, 1, False)

            pool.wait_ge(done("a_x"), NB)
            pool_ffn(pool, MOE)

            pool.wait_ge(done("b_x"), 2 * NG)
            pool.wait_ge(done("k_sq"), 4)
            power(pool, k_ss[:], ve[:], rstd[:], rms_eps, 1, "k_r")

            def front_c(b):
                pool.wait_ge(done("c_mv"), 2 * (b + 1))
                power(pool, mv[:, 0:2, 1], ve[:, 0:2], rstd[:, 0:2], ln_eps, b + 1, "c_rstd")
                wait(pool, done("c_s_ps"), 2 * b)
                for f in range(2):
                    for dst, src in ((c_kbh, kt_hi), (c_kbl, kt_lo)):
                        spread(pool, dst[:, f, :], src[:, f, bass.ds(b * SK, SK)].bitcast(F32)).then_inc(done("c_kb"), 1)
                pool.wait_ge(done("c_xn"), 2 * (b + 1))
                xs = x_sb[:, bass.ds(2 * b, 2), :]
                pool.tensor_tensor(xs, xs, bias_sb[:, 3, :].unsqueeze(1).broadcast_to([P, 2, D]), ALU.add).then_inc(done("c_xb"), 1)

            def rsqrt_q(b):
                pool.wait_ge(done("c_sq"), 2 * (b + 1))
                wait(pool, done("c_qn"), 2 * b)
                power(pool, c_ss[:], c_ve[:], c_rq[:], rms_eps, b + 1, "c_rq")

            def step_c(i, mid, front, rest):
                j = i - 1
                if front:
                    front_c(i + 1)
                if mid:
                    wait(pool, done("c_pv_ps"), i)
                    pool.tensor_copy(c_v[:], v1[:, i, :]).then_inc(done("c_v"), 1)
                if front:
                    rsqrt_q(i + 1)
                if rest:
                    pool.wait_ge(done("c_ath"), j + 1)
                    pool.tensor_tensor(c_atlb[:], c_atb[:], c_athb[:].bitcast(F32), ALU.subtract).then_inc(done("c_atl"), 1)
                if mid:
                    pool.wait_ge(done("w1_hi"), i + 1)
                    at = bass.ds(i * PIECE1, PIECE1)
                    pool.tensor_tensor(w_lo[:, at], stage[:, 0, 0:PIECE1], w_hi[:, at].bitcast(F32), ALU.subtract)\
                        .then_inc(done("w1_lo"), 1)

            pool.wait_ge(done("kt_lo"), 4)
            pool.wait_ge(done("v1_set"), NB)
            pool.wait_ge(done("tgbo"), 1)
            front_c(0)
            rsqrt_q(0)
            step_c(0, True, True, False)
            with pool.Fori(1, NB - 1) as i:
                step_c(i, True, True, True)
            step_c(NB - 1, True, False, True)
            step_c(NB, False, False, True)

            pool.wait_ge(done("c_x"), NB)
            pool_ffn(pool, FFN)


def kernel(**inputs):
    import numpy as np
    import concourse.bacc as bacc
    from concourse.bass_utils import run_bass_kernel_spmd

    a = {k: np.asarray(v) for k, v in inputs.items()}

    def halves(w):
        return w.reshape(2, P, -1).transpose(1, 0, 2)

    def packed(gate, up, down):
        parts = [halves(gate), halves(up), down.reshape(-1, P, D).transpose(1, 0, 2)]
        return np.ascontiguousarray(np.concatenate([q.reshape(P, -1) for q in parts], axis=1))

    def experts(w, shared):
        w = np.concatenate([w.transpose(1, 0, 2).reshape(D, NE * FE), shared], axis=1)
        return np.concatenate([w, np.zeros((D, HID0 - w.shape[1]), w.dtype)], axis=1)

    down0 = np.concatenate([a["L0_ffn_Wd"].reshape(NE * FE, D), a["L0_ffn_Sd"],
                            np.zeros((HID0 - NE * FE - FS, D), np.float32)], axis=0)
    xw = np.stack([halves(a[f"L1_xattn_w_{n}"].T) for n in ("q", "k_img", "v_img", "o")], axis=1)
    rw = np.concatenate([a["L0_ffn_Wr"], a["L0_ffn_Wsg"], np.zeros((D, P - NE - 1), np.float32)], axis=1)
    p = np.arange(P)[:, None]
    col = np.arange(D)[None, :]
    consts = np.concatenate([
        p == np.arange(P)[None, :],
        p // HD == np.arange(8)[None, :],
        col // HD % 2 == p // SK,
        np.arange(32)[None, :] // HD == p // SK,
        np.full((P, 4), -0.5),
        np.broadcast_to(np.arange(8, 0, -1), (P, 8)),
        np.full((P, 4), LN_EPS), np.full((P, 4), RMS_EPS),
    ], axis=1).astype(np.float32)
    unit = np.arange(HID0)
    owner = np.where(unit < NE * FE, unit // FE, np.where(unit < NE * FE + FS, NE, -1))
    row = np.arange(P)[:, None]
    sel = ((row < 64) & (row % 32 == owner[None, :])).astype(np.float32)

    arrays = {
        "x": a["x"], "ctx": a["ctx_2048"],
        "ctx_t": np.ascontiguousarray(halves(a["ctx_2048"].reshape(NB * SK, D).T)),
        "xw": np.ascontiguousarray(xw), "rw": np.ascontiguousarray(halves(rw)),
        "moe_w": packed(experts(a["L0_ffn_Wg"], a["L0_ffn_Sg"]), experts(a["L0_ffn_Wu"], a["L0_ffn_Su"]), down0),
        "ffn_w": packed(a["L1_ffn_w_gate"].T, a["L1_ffn_w_up"].T, a["L1_ffn_w_down"].T),
        "bias": np.stack([a["L1_xattn_" + n] for n in ("b_q", "b_k_img", "b_v_img", "b_o", "g_q", "g_k_img")]),
        "gx": a["g_xattn"], "gf": a["g_ffn"], "consts": consts, "sel": sel,
    }
    nc = bacc.Bacc("TRN2", target_bir_lowering=False, num_devices=1, dynamic_dma_scratch_size=1024)
    args = {k: nc.dram_tensor("in_" + k, v.shape, mybir.dt.from_np(v.dtype), kind="ExternalInput").ap()
            for k, v in arrays.items()}
    args["out"] = nc.dram_tensor("result", (NB, SQ, D), F32, kind="ExternalOutput").ap()
    build(nc, **args)
    r = run_bass_kernel_spmd(nc, [{"in_" + k: v for k, v in arrays.items()}], core_ids=[0])
    return r.results[0]["result"]
```

```python
from contextlib import ExitStack

import concourse.bass as bass
from concourse import mybir

F32 = mybir.dt.float32
F32R = mybir.dt.float32r
ALU = mybir.AluOpType
ACT = mybir.ActivationFunctionType
AX = mybir.AxisListType

P = 128
NB, SQ, D = 8, 256, 256
SK = 64
NH, HD = 16, 16
NT = NB * SQ // P
NE, FE, FS = 8, 176, 704
GT = 4
GN = GT * P
NG = NT // GT
NC0 = -(-(NE * FE + FS) // P)
HID0 = NC0 * P
HID1 = 1024
NC1 = HID1 // P
SCALE = 0.25
MASKED = -10000.0 / SCALE
LN_EPS, RMS_EPS = 1e-5, 1e-6
RMS_SCALE = 1 / 16
CHUNK = 6 * P
EARLY1 = 3
EARLY = 8
C_ID, C_HM, C_VM, C_ONE, C_NH, C_W8, C_LE, C_RE, C_RQ, C_R0 = 0, 128, 136, 392, 424, 428, 436, 440, 444, 448
CST = 576


def wait(eng, sem, n):
    if isinstance(n, int) and n <= 0:
        return
    eng.wait_ge(sem, n)


def build(nc, x, ctx_v, ctx_t, xw_kv, xw_qo, rw, moe_w, ffn_w, bias_kv, bias_qo, gx, gf, consts, sel, out):
    first = [-(-nc.sbuf_base // 32) * 32]

    def sb(name, shape, dt=F32, at=None):
        cur = first if at is None else at
        size = 4
        for s in shape[1:]:
            size *= s
        h = nc.alloc_sbuf_tensor_at(name, list(shape), dt, offset=cur[0])
        cur[0] += -(-size // 32) * 32
        assert cur[0] <= nc.sbuf_top, (name, cur)
        return h

    with ExitStack() as es:
        x_sb = sb("x_sb", [P, NT, D])
        cst = sb("cst", [P, CST])
        avg = sb("avg", [P, P])
        gates = sb("gates", [P, 4])
        bias_sb = sb("bias_sb", [P, 2, D])
        xw = sb("xw", [P, 2, 2, D])
        w_hi = sb("w_hi", [P, NC0 * CHUNK], F32R)
        w_lo = sb("w_lo", [P, NC0 * CHUNK], F32R)
        stage = sb("stage", [P, 2, CHUNK])
        stat = sb("stat", [P, 4, 6])
        mv = sb("mv", [P, 4, 2])
        ve = sb("ve", [P, 4])
        rstd = sb("rstd", [P, 4])
        rw_hi = sb("rw_hi", [P, 2, P], F32R)
        rw_lo = sb("rw_lo", [P, 2, P], F32R)
        sel_sb = sb("sel_sb", [P, HID0], F32R)
        kt_hi = sb("kt_hi", [P, 2, NB * SK], F32R)
        kt_lo = sb("kt_lo", [P, 2, NB * SK], F32R)
        v1 = sb("v1", [P, NB, D])
        c_mx = sb("c_mx", [P, 2, NH])
        c_ss = sb("c_ss", [P, 2])
        c_ve = sb("c_ve", [P, 2])
        c_rq = sb("c_rq", [P, 2])
        ident = cst[:, C_ID:C_ID + P]
        headmask = cst[:, C_HM:C_HM + 8]
        vmask = cst[:, C_VM:C_VM + D]
        oneblk = cst[:, C_ONE:C_ONE + 32]
        neghalf = cst[:, C_NH:C_NH + 4]
        w8 = cst[:, C_W8:C_W8 + 8]
        ln_eps = cst[:, C_LE:C_LE + 4]
        rms_eps = cst[:, C_RE:C_RE + 4]
        rmsq_eps = cst[:, C_RQ:C_RQ + 4]
        row0 = cst[:, C_R0:C_R0 + P]

        ra = [first[0]]
        ctxt = sb("ctxt", [P, 2, NB * SK], F32, ra)
        a_kb = sb("a_kb", [P, 2, 2, 512], F32, ra)
        a_s = sb("a_s", [P, 2, NH * SK], F32, ra)
        ctxv = sb("ctxv", [P, NB, D], F32, ra)
        a_xnb = sb("a_xnb", [P, D], F32, ra)
        a_qt = sb("a_qt", [P, 2, P], F32, ra)
        a_mx = sb("a_mx", [P, NH], F32, ra)
        a_sm = sb("a_sm", [P, NH], F32, ra)
        a_ri = sb("a_ri", [P, NH], F32, ra)
        a_ptb = sb("a_ptb", [P, 8, P], F32, ra)
        a_at = sb("a_at", [P, 2, P], F32, ra)
        a_tmpb = sb("a_tmpb", [P, D], F32, ra)
        kv_raw = sb("kv_raw", [P, 2, 2, D], F32, ra)
        rw_raw = sb("rw_raw", [P, 2, P], F32, ra)
        sel_raw = sb("sel_raw", [P, HID0], F32, ra)
        bkv = sb("bkv", [P, 4, D], F32, ra)
        k_ss = sb("k_ss", [P, NG], F32, ra)
        k_ve = sb("k_ve", [P, NG], F32, ra)
        k_r = sb("k_r", [P, NG], F32, ra)
        kn_sb = sb("kn_sb", [P, D], F32, ra)
        rf = [first[0]]
        f_xnb = sb("f_xnb", [P, GT, D], F32, rf)
        xt = sb("xt", [P, 2, 2, 2, GN], F32R, rf)
        s_sb = sb("s_sb", [P, 2, GN], F32, rf)
        t_sb = sb("t_sb", [P, 2, GN], F32, rf)
        h_sb = sb("h_sb", [P, 2, GN], F32, rf)
        h_hi = sb("h_hi", [P, 3, GN], F32R, rf)
        h_lo = sb("h_lo", [P, 3, GN], F32R, rf)
        y_t = sb("y_t", [P, 2, GN], F32, rf)
        lgt = sb("lgt", [P, GN], F32, rf)
        c_t = sb("c_t", [P, 2, GN], F32R, rf)
        lg = sb("lg", [P, GT, 9], F32, rf)
        r_z = sb("r_z", [P, GT, 8], F32, rf)
        r_p = sb("r_p", [P, GT, 8], F32, rf)
        r_den = sb("r_den", [P, GT, 2], F32, rf)
        r_inv = sb("r_inv", [P, GT, 2], F32, rf)
        r_es = sb("r_es", [P, GT, 1], F32, rf)
        r_m = sb("r_m", [P, GT], F32, rf)
        r_k = sb("r_k", [P, GT, 8], F32, rf)
        r_o1 = sb("r_o1", [P, GT, 8], F32, rf)
        r_o2 = sb("r_o2", [P, GT, 8], F32, rf)
        r_c = sb("r_c", [P, GT, 9], F32, rf)
        r_cd = sb("r_cd", [P, GT, P], F32R, rf)
        rc = [first[0]]
        c_xnb = sb("c_xnb", [P, 2, D], F32, rc)
        c_qb = sb("c_qb", [P, 2, D], F32, rc)
        c_xt = sb("c_xt", [P, 2, SQ], F32, rc)
        c_qth = sb("c_qth", [P, 2, SQ], F32R, rc)
        c_qtl = sb("c_qtl", [P, 2, SQ], F32R, rc)
        rc[0] += 2048 + 8192
        c_kbh = sb("c_kbh", [P, 2, 512], F32R, rc)
        c_kbl = sb("c_kbl", [P, 2, 512], F32R, rc)
        c_e = sb("c_e", [P, 2, NH * SK], F32, rc)
        c_ptb = sb("c_ptb", [P, 8, SQ], F32, rc)
        c_v = sb("c_v", [P, D], F32, rc)
        c_atb = sb("c_atb", [P, 2, SQ], F32, rc)

        bank = [es.enter_context(nc.psum_tensor(f"bank{i}", [P, 512], F32)) for i in range(8)]

        S = {}

        def done(name):
            if name not in S:
                S[name] = es.enter_context(nc.semaphore(name))
            return S[name]

        block = es.enter_context(nc.Block())
        x_v = x.rearrange("b (j p) d -> p (b j) d", p=P)
        out_v = out.rearrange("b (j p) d -> p (b j) d", p=P)
        lower, upper = slice(0, 64), slice(64, P)
        own = (lower, upper)

        def halves(bk):
            return bk[:, :].rearrange("p (f t) -> p f t", f=2)

        def left(bk):
            return bk[:, 0:D].rearrange("p (f t) -> p f t", f=2)

        def by_head(t, n):
            return t.rearrange("p (h k) -> p h k", h=n)

        MOE = dict(name="b_", moe=True, chunks=NC0, gate=2, tail_at=(3, 4), front_at=(6, 7, 9, 10, 14), front0=bank[4])
        FFN = dict(name="d_", moe=False, chunks=NC1, gate=3, tail_at=(3, 4), front_at=(5, 6), front0=bank[6])

        @block.sync
        def _(sp):
            sp.dma_start(x_sb[lower, 1, :], x_v[upper, 1, :]).then_inc(done("x0_in"), 16)
            sp.dma_start(x_sb[:, 2:4, :], x_v[:, 2:4, :]).then_inc(done("x0_in"), 16)
            sp.dma_start(x_sb[upper, 1, :], x_v[lower, 1, :]).then_inc(done("x0_in"), 16)
            sp.dma_start(gates[:, 0:2], gx.rearrange("(a n) -> a n", a=1).broadcast_to([P, 2])).then_inc(done("gates_in"), 16)
            sp.dma_start(gates[:, 2:4], gf.rearrange("(a n) -> a n", a=1).broadcast_to([P, 2])).then_inc(done("gates_in"), 16)
            sp.dma_start(kv_raw[:], xw_kv).then_inc(done("kv_in"), 16)
            sp.dma_start(bkv[:], bias_kv.rearrange("(a n) d -> a n d", a=1).broadcast_to([P, 4, D])).then_inc(done("kv_in"), 16)
            sp.dma_start(x_sb[lower, GT + 1::GT, :], x_v[upper, GT + 1::GT, :]).then_inc(done("x_in"), 16)
            sp.dma_start(x_sb[upper, GT + 1::GT, :], x_v[lower, GT + 1::GT, :]).then_inc(done("x_in"), 16)
            sp.dma_start(x_sb[:, GT + 3::GT, :], x_v[:, GT + 3::GT, :]).then_inc(done("x_in"), 16)
            for u in range(2):
                sp.dma_start(stage[:, u], moe_w[:, u * CHUNK:(u + 1) * CHUNK]).then_inc(done(f"w0_in{u}"), 16)
            sp.dma_start(x_sb[:, GT + 2::GT, :], x_v[:, GT + 2::GT, :]).then_inc(done("x_rest_in"), 16)
            sp.dma_start(x_sb[:, 0::GT, :], x_v[:, 0::GT, :]).then_inc(done("x_rest_in"), 16)
            sp.dma_start(rw_raw[:], rw).then_inc(done("late_in"), 16)
            sp.dma_start(sel_raw[:], sel).then_inc(done("late_in"), 16)
            sp.dma_start(xw[:], xw_qo).then_inc(done("late_in"), 16)
            sp.dma_start(bias_sb[:], bias_qo.rearrange("(a n) d -> a n d", a=1).broadcast_to([P, 2, D])).then_inc(done("late_in"), 16)
            with sp.Fori(1, NC0 // 2) as b:
                for u in range(2):
                    sp.wait_ge(done(f"w0_lo{u}"), b)
                    sp.dma_start(stage[:, u], moe_w[:, bass.ds((2 * b + u) * CHUNK, CHUNK)]).then_inc(done(f"w0_in{u}"), 16)
            sp.wait_ge(done("w0_lo0"), NC0 // 2)
            sp.dma_start(stage[:, 0], moe_w[:, (NC0 - 1) * CHUNK:]).then_inc(done("w0_in0"), 16)
            sp.wait_ge(done("w0_lo0"), NC0 // 2 + 1)
            sp.dma_start(stage[:, 0], ffn_w[:, 0:CHUNK]).then_inc(done("w1_in"), 16)
            with sp.Fori(1, NC1) as c:
                sp.wait_ge(done("w1_lo"), c)
                sp.dma_start(stage[:, 0], ffn_w[:, bass.ds(c * CHUNK, CHUNK)]).then_inc(done("w1_in"), 16)
            with sp.Fori(0, NG) as g:
                sp.wait_ge(done("d_x"), 2 * g + 1)
                sp.dma_start(out_v[:, bass.ds(GT * g, 1), :], x_sb[:, bass.ds(GT * g, 1), :]).then_inc(done("out_done"), 16)
                sp.dma_start(out_v[upper, bass.ds(GT * g + 1, 1), :], x_sb[lower, bass.ds(GT * g + 1, 1), :]).then_inc(done("out_done"), 16)
                sp.dma_start(out_v[lower, bass.ds(GT * g + 1, 1), :], x_sb[upper, bass.ds(GT * g + 1, 1), :]).then_inc(done("out_done"), 16)
                sp.wait_ge(done("d_x"), 2 * g + 2)
                sp.dma_start(out_v[:, bass.ds(GT * g + 2, 2), :], x_sb[:, bass.ds(GT * g + 2, 2), :]).then_inc(done("out_done"), 16)
            sp.wait_ge(done("out_done"), 16 * 4 * NG)

        def split_matmul(pe, dst, w_h, w_l, m_h, m_l, first, last):
            pe.matmul(dst, w_h, m_h, start=first, stop=False)
            pe.matmul(dst, w_h, m_l, start=False, stop=False)
            return pe.matmul(dst, w_l, m_h, start=False, stop=last)

        def back(c, ring, chunks):
            if c >= ring:
                return ring
            return c + chunks - max(k for k in range(chunks) if k % ring == c % ring)

        def weights(kind, kk, c):
            at = c * CHUNK + {"gate": 0, "up": 2 * P, "down": 4 * P}[kind] + kk * P
            return slice(at, at + P)

        def pe_front(pe, ph, g, bk):
            p = ph["name"]
            for f in range(2):
                wait(pe, done(p + "xn"), GT * (g + 1))
                if f == 0:
                    wait(pe, done(p + "x"), 2 * (g - 1))
                    if ph["moe"]:
                        wait(pe, done(p + "ct"), g)
                wait(pe, done(p + "xtl"), 2 * g + f)
                for t in range(GT):
                    mm = pe.transpose(bk[:, t * P:(t + 1) * P], f_xnb[:, t, f * P:(f + 1) * P], ident)
                mm.then_inc(done(p + "xt_ps"), 1)
                yield
            if ph["moe"]:
                wait(pe, done(p + "xtl"), 2 * g + 2)
                for kk in range(2):
                    mm = split_matmul(pe, bk[:, :], rw_hi[:, kk, :], rw_lo[:, kk, :],
                                      xt[:, g % 2, 0, kk, :], xt[:, g % 2, 1, kk, :], kk == 0, kk == 1)
                mm.then_inc(done(p + "lg_ps"), 1)
                yield
                wait(pe, done(p + "lgt"), g + 1)
                for t in range(GT):
                    mm = pe.transpose(bk[:, t * P:(t + 1) * P], lgt[:, t * P:(t + 1) * P], ident)
                mm.then_inc(done(p + "lt_ps"), 1)
                yield
                wait(pe, done(p + "c"), g + 1)
                for t in range(GT):
                    mm = pe.transpose(bk[:, t * P:(t + 1) * P], r_cd[:, t, :].bitcast(F32), ident)
                mm.then_inc(done(p + "ct_ps"), 1)
                yield

        def pe_down(pe, ph, g, c, n):
            p = ph["name"]
            wait(pe, done(p + "hlo"), n + 1)
            for f in range(2):
                if c == 0:
                    wait(pe, done(p + "y"), 2 * g)
                w = weights("down", f, c)
                mm = split_matmul(pe, bank[5 + f][:, :], w_hi[:, w], w_lo[:, w], h_hi[:, c % 3, :], h_lo[:, c % 3, :],
                                  c == 0, c == ph["chunks"] - 1)
            mm.then_inc(done(p + "dn"), 1)

        def pe_tail(pe, ph, g, q):
            p = ph["name"]
            wait(pe, done(p + "y"), 2 * (g + 1))
            if q == 1:
                wait(pe, done(p + "x"), 2 * g + 1)
            for t in range(2):
                for f in range(2):
                    mm = pe.transpose(bank[7][:, t * D + f * P:t * D + (f + 1) * P],
                                      y_t[:, f, (2 * q + t) * P:(2 * q + t + 1) * P], ident)
            mm.then_inc(done(p + "yt_ps"), 1)

        def pe_ffn(pe, ph, own, after):
            p, nch, moe = ph["name"], ph["chunks"], ph["moe"]

            def spread_weights(g, c, n):
                wait(pe, done(p + "h"), n)
                if c == 0:
                    wait(pe, done(p + "ct"), g + 1)
                pe.matmul(bank[4][:, :], sel_sb[:, c * P:(c + 1) * P], c_t[:, g % 2, :],
                          start=True, stop=True).then_inc(done(p + "cb_ps"), 1)

            def group(g, prev, nxt, split, after):
                front = pe_front(pe, ph, g + 1, bank[7]) if nxt else None
                for c in range(nch):
                    n = g * nch + c
                    if c == 0:
                        wait(pe, done(p + "xtl"), 2 * (g + 1))
                    if split and moe:
                        wait(pe, done(f"w0_lo{c % 2}"), c // 2 + 1)
                    elif split:
                        wait(pe, done("w1_lo"), c + 1)
                    for kind, bk, freed in (("gate", bank[c % 2], "silu"), ("up", bank[2 + c % 2], "t")):
                        wait(pe, done(p + freed), n - back(c, 2, nch) + 1)
                        for kk in range(2):
                            w = weights(kind, kk, c)
                            mm = split_matmul(pe, bk[:, :], w_hi[:, w], w_lo[:, w],
                                              xt[:, g % 2, 0, kk, :], xt[:, g % 2, 1, kk, :], kk == 0, kk == 1)
                        mm.then_inc(done(p + kind + "_ps"), 1)
                    if moe and split and c < 2:
                        next(own)
                        if c == 1:
                            spread_weights(g, 0, n - 1)
                            spread_weights(g, 1, n)
                    elif moe:
                        spread_weights(g, c, n)
                    if c >= 2:
                        pe_down(pe, ph, g, c - 2, n - 2)
                    elif prev:
                        pe_down(pe, ph, g - 1, nch - 2 + c, n - 2)
                    if prev and c in ph["tail_at"]:
                        if c == ph["tail_at"][0]:
                            wait(pe, done(p + ("ct" if moe else "xtl")), (1 if moe else 2) * (g + 1))
                        pe_tail(pe, ph, g - 1, ph["tail_at"].index(c))
                    if nxt and c in ph["front_at"]:
                        next(front)
                    if c in after:
                        after[c]()

            group(0, False, True, True, after.get("first", {}))
            with pe.Fori(1, NG - 1) as g:
                group(g, True, True, False, {})
            group(NG - 1, True, False, False, after)
            for c in (nch - 2, nch - 1):
                pe_down(pe, ph, NG - 1, c, (NG - 1) * nch + c)

        @block.tensor
        def _(pe):
            def turn_a(k):
                wait(pe, done("a_xn"), 2 * (k + 1))
                wait(pe, done("kt_lo"), k - 1)
                for f in range(2):
                    mm = pe.transpose(bank[4][:, f * P:(f + 1) * P], a_xnb[:, f * P:(f + 1) * P], ident)
                mm.then_inc(done("a_xt_ps"), 1)

            def keys_values(k):
                if k == 0:
                    pe.wait_ge(done("kv_in"), 32)
                wait(pe, done("a_tmp"), k - 1)
                pair = slice(2 * k * SK, 2 * (k + 1) * SK)
                for kk in range(2):
                    pe.matmul(bank[6][:, 0:D], ctxt[:, kk, pair], kv_raw[:, 0, kk, :], start=kk == 0, stop=False)
                pe.matmul(bank[6][:, 0:D], row0, bkv[:, 0, :], start=False, stop=True).then_inc(done("k_ps"), 1)
                yield
                wait(pe, done("v1_set"), k)
                wait(pe, done("a_xm"), 3 * (k - 1))
                for e in range(2):
                    one = slice((2 * k + e) * SK, (2 * k + e + 1) * SK)
                    for kk in range(3):
                        for half in own:
                            lhs, rhs = (row0[:, 0:SK], bkv[:, 1, :]) if kk == 2 else (ctxt[:, kk, one], kv_raw[:, 1, kk, :])
                            mm = pe.matmul(bank[7][half, e * D:(e + 1) * D], lhs, rhs, start=kk == 0, stop=kk == 2)
                mm.then_inc(done("v_ps"), 1)
                yield

            def keys_turn(k):
                wait(pe, done("kn"), k + 1)
                wait(pe, done("a_qt"), min(k + 2, NG))
                for f in range(2):
                    mm = pe.transpose(bank[4][:, f * P:(f + 1) * P], kn_sb[:, f * P:(f + 1) * P], ident)
                mm.then_inc(done("kt_ps"), 1)

            pe.wait_ge(done("setup_in"), 32)
            turn_a(0)
            for i in range(NG + 1):
                j, w = i - 1, (i - 1) % 2
                kv = keys_values(i) if i < NG else None
                if i == NG:
                    own_b = pe_front(pe, MOE, 0, MOE["front0"])
                    wait(pe, done("kt_lo"), NG)
                if i < NG:
                    wait(pe, done("a_qt"), i + 1)
                    wait(pe, done("a_s"), 2 * i)
                    for f in range(2):
                        for e in range(2):
                            if f == 0:
                                wait(pe, done("a_kb"), 4 * i + 2 * (e + 1))
                            mm = pe.matmul(bank[f][own[e], :], a_qt[:, f, e * SK:(e + 1) * SK], a_kb[:, e, f, :],
                                           start=True, stop=True)
                        mm.then_inc(done("a_s_ps"), 1)
                if i < NG:
                    next(kv)
                if i == 0:
                    next(kv)
                if j >= 0:
                    wait(pe, done("a_exp"), j + 1)
                    for h in range(2):
                        wait(pe, done("a_pt"), 2 * (j - 1) + h + 1)
                        for c in range(4):
                            cc = 4 * h + c
                            mm = pe.transpose(bank[2 + h][:, c * P:(c + 1) * P], a_s[:, w, cc * P:(cc + 1) * P], ident)
                        mm.then_inc(done("a_pt_ps"), 1)
                if i == NG:
                    next(own_b)
                elif i > 0:
                    next(kv)
                if i + 1 < NG:
                    turn_a(i + 1)
                if j >= 0:
                    wait(pe, done("v_in"), 16)
                    wait(pe, done("a_pt"), 2 * j + 2)
                    wait(pe, done("a_at"), j)
                    for c in range(8):
                        r = 32 * (c % 4)
                        for e in range(2):
                            at = (c // 4) * P + e * SK
                            mm = pe.matmul(bank[5][r:r + 32, at:at + SK], ctxv[:, 2 * j + e, c * 32:(c + 1) * 32],
                                           a_ptb[:, c, e * SK:(e + 1) * SK], start=True, stop=True)
                    mm.then_inc(done("a_pv_ps"), 1)
                if i < NG:
                    keys_turn(i)
                else:
                    next(own_b)
                if j >= 0:
                    wait(pe, done("avg_set"), 1)
                    wait(pe, done("v1_set"), min(i + 1, NG))
                    wait(pe, done("a_xm"), 3 * j)
                    pe.matmul(bank[7][:, :], avg[:], ctxv[:, 2 * j:2 * j + 2, :], start=True, stop=True).then_inc(done("a_m_ps"), 1)
                    wait(pe, done("a_at"), j + 1)
                    wait(pe, done("a_tmp"), j)
                    wait(pe, done("kn"), min(i + 1, NG))
                    for f in range(2):
                        mm = pe.transpose(bank[6][:, f * P:(f + 1) * P], a_at[:, f, :], ident)
                    mm.then_inc(done("a_o_ps"), 1)

            def turn_tokens(src, bk):
                for f in range(2):
                    for t in range(2):
                        mm = pe.transpose(bk[:, f * SQ + t * P:f * SQ + (t + 1) * P], src[:, t, f * P:(f + 1) * P], ident)
                return mm

            def x_turn(b, bk):
                wait(pe, done("c_xn"), b + 1)
                wait(pe, done("c_qtl"), b)
                turn_tokens(c_xnb, bk).then_inc(done("c_xt_ps"), 1)

            def projection(bk, src, which):
                for t in range(2):
                    for kk in range(2):
                        mm = pe.matmul(bk[:, t * D:(t + 1) * D], src[:, kk, t * P:(t + 1) * P], xw[:, which, kk, :],
                                       start=kk == 0, stop=kk == 1)
                return mm

            def q_proj(b, bk):
                wait(pe, done("c_xt"), b + 1)
                projection(bk, c_xt, 0).then_inc(done("c_q_ps"), 1)

            def q_turn(b, bk):
                wait(pe, done("c_q"), b + 1)
                turn_tokens(c_qb, bk).then_inc(done("c_qt_ps"), 1)

            def p_turn(b, t):
                wait(pe, done("c_exp"), 2 * b + t + 1)
                for h in range(2):
                    if t == 1:
                        pe.wait_ge(done("c_pt"), 4 * b + h + 1)
                    for c in range(4):
                        cc = 4 * h + c
                        mm = pe.transpose(bank[4 + h][:, c * P:(c + 1) * P], c_e[:, t, cc * P:(cc + 1) * P], ident)
                    mm.then_inc(done("c_pt_ps"), 1)

            def scores(b, t, divided=False):
                wait(pe, done("c_qtl"), b + 1)
                if not (isinstance(b, int) and b == 0):
                    wait(pe, done("c_sub"), 4 * b + 2 * t - 2)
                tok = slice(t * P, (t + 1) * P)
                if divided:
                    wait(pe, done("c_rd"), b - 1)
                for f in range(2):
                    if t == 0:
                        wait(pe, done("c_kb"), 4 * b + 2 * (f + 1))
                    mm = split_matmul(pe, bank[2 * t + f][:, :], c_qth[:, f, tok], c_qtl[:, f, tok],
                                      c_kbh[:, f, :], c_kbl[:, f, :], True, True)
                mm.then_inc(done("c_s_ps"), 1)

            def o_proj(m):
                wait(pe, done("c_at"), m + 1)
                projection(bank[7], c_atb, 1).then_inc(done("c_o_ps"), 1)

            def step_c(i, mid=True, front=True, rest=True, out=True, tails=(), fronts=()):
                j, m = i - 1, i - 2
                if rest:
                    p_turn(j, 0)
                if front and not tails:
                    x_turn(i + 1, bank[6])
                for t in fronts[:1]:
                    next(t)
                if rest:
                    p_turn(j, 1)
                if front and not tails:
                    q_proj(i + 1, bank[6])
                if mid:
                    scores(i, 0, out)
                for q in tails:
                    pe_tail(pe, MOE, NG - 1, q)
                if front and tails:
                    x_turn(i + 1, bank[6])
                    q_proj(i + 1, bank[6])
                if out:
                    o_proj(m)
                for t in fronts[1:]:
                    next(t)
                if mid:
                    scores(i, 1)
                if rest:
                    wait(pe, done("c_pt"), 4 * j + 4)
                    wait(pe, done("c_v"), j + 1)
                    if mid:
                        wait(pe, done("c_sub"), 4 * i + 2)
                    for dst, w, what in ((bank[0 if mid else 4], None, "c_d_ps"), (bank[7], c_v, "c_pv_ps")):
                        if w is not None and out:
                            wait(pe, done("c_x"), j)
                        elif w is not None:
                            wait(pe, done("b_x"), 2 * NG)
                        for c in range(8):
                            r = 32 * (c % 4)
                            lhs = oneblk if w is None else w[:, c * 32:(c + 1) * 32]
                            mm = pe.matmul(dst[r:r + 32, (c // 4) * SQ:(c // 4 + 1) * SQ], lhs, c_ptb[:, c, :],
                                           start=True, stop=True)
                        mm.then_inc(done(what), 1)
                if front:
                    q_turn(i + 1, bank[6])

            pe.wait_ge(done("late_lo"), 1)
            pe.wait_ge(done("late_hi"), 2)

            def x_turn0():
                pe.wait_ge(done("b_x"), 2 * (NG - 1))
                x_turn(0, bank[7])

            next(own_b)
            pe_ffn(pe, MOE, own_b, {5: x_turn0, 7: lambda: q_proj(0, bank[7]), 9: lambda: q_turn(0, bank[7])})

            step_c(0, rest=False, out=False, tails=(0, 1))
            step_c(1, out=False)
            with pe.Fori(2, NB - 2) as i:
                step_c(i)
            step_c(NB - 2)
            step_c(NB - 1, front=False)
            own_d = pe_front(pe, FFN, 0, FFN["front0"])
            step_c(NB, mid=False, front=False, fronts=(own_d, own_d))

            def last_bank():
                wait(pe, done("c_x"), NB)
            pe_ffn(pe, FFN, None, {"first": {1: lambda: o_proj(NB - 1), FFN["front_at"][0] - 1: last_bank}})
            for q in range(2):
                pe_tail(pe, FFN, NG - 1, q)

        def act_front(act, ph, g, bk):
            p = ph["name"]
            for f in range(2):
                wait(act, done(p + "xt_ps"), 2 * g + f + 1)
                act.activation(xt[:, g % 2, 0, f, :], bk[:, :], ACT.Copy).then_inc(done(p + "xth"), 1)
                yield
            if ph["moe"]:
                wait(act, done(p + "lg_ps"), g + 1)
                act.activation(lgt[:], bk[:, :], ACT.Copy).then_inc(done(p + "lgt"), 1)
                yield
                wait(act, done(p + "z"), g + 1)
                act.activation(r_p[:], r_z[:], ACT.Exp).then_inc(done(p + "e"), 1)
                act.activation(r_es[:], lg[:, :, 8:9], ACT.Exp, scale=-1.0).then_inc(done(p + "es"), 1)
                yield
                wait(act, done(p + "ct_ps"), g + 1)
                act.activation(c_t[:, g % 2, :], bk[:, :], ACT.Copy).then_inc(done(p + "ct"), 1)
                yield

        def act_split0(act, n):
            wait(act, done(f"w0_in{n % 2}"), 16 * (n // 2 + 1))
            act.activation(w_hi[:, n * CHUNK:(n + 1) * CHUNK], stage[:, n % 2], ACT.Copy).then_inc(done("w0_hi"), 1)

        def act_ffn(act, ph, own, after):
            p, nch, moe = ph["name"], ph["chunks"], ph["moe"]

            def hi(c, n):
                wait(act, done(p + ("h" if moe else "t")), n + 1)
                wait(act, done(p + "dn"), n - back(c, 3, nch) + 1)
                act.activation(h_hi[:, c % 3, :], h_sb[:, c % 2, :], ACT.Copy).then_inc(done(p + "hhi"), 1)

            def y_out(g):
                wait(act, done(p + "dn"), (g + 1) * nch)
                for f in range(2):
                    act.activation(y_t[:, f, :], bank[5 + f][:, :], ACT.Copy).then_inc(done(p + "y"), 1)

            def group(g, prev, nxt, split, after):
                front = act_front(act, ph, g + 1, bank[7]) if nxt else None
                for c in range(nch):
                    n = g * nch + c
                    wait(act, done(p + "gate_ps"), n + 1)
                    wait(act, done(p + "t"), n - back(c, 2, nch) + 1)
                    act.activation(s_sb[:, c % 2, :], bank[c % 2][:, :], ACT.Silu).then_inc(done(p + "silu"), 1)
                    if moe and split and c < 2:
                        next(own)
                    if c >= 1:
                        hi(c - 1, n - 1)
                    elif prev:
                        hi(nch - 1, n - 1)
                    if moe and split and c + EARLY < nch:
                        act_split0(act, c + EARLY)
                    if prev and c == 2:
                        y_out(g - 1)
                    if nxt and c in ph["front_at"]:
                        next(front)
                    if c in after:
                        after[c]()

            group(0, False, True, True, after.get("first", {}))
            with act.Fori(1, NG - 1) as g:
                group(g, True, True, False, {})
            group(NG - 1, True, False, False, after)
            hi(nch - 1, NG * nch - 1)
            y_out(NG - 1)

        @block.scalar
        def _(act):
            act.dma_start(cst[:], consts).then_inc(done("setup_in"), 16)
            act.dma_start(ctxt[:], ctx_t).then_inc(done("setup_in"), 16)
            act.dma_start(ctxv[:], ctx_v).then_inc(done("v_in"), 16)

            def q_out(k):
                wait(act, done("a_xt_ps"), k + 1)
                wait(act, done("a_s_ps"), 2 * k)
                act.activation(a_qt[:], left(bank[4]), ACT.Copy).then_inc(done("a_qt"), 1)

            def late():
                act.wait_ge(done("late_in"), 64)
                act.activation(rw_hi[:], rw_raw[:], ACT.Copy).then_inc(done("late_hi"), 1)
                act.activation(sel_sb[:], sel_raw[:], ACT.Copy).then_inc(done("late_hi"), 1)

            q_out(0)
            for i in range(NG + 1):
                j, u = i - 1, i % 2
                if i < NG:
                    for f in range(2):
                        wait(act, done("a_s_ps"), 2 * i + f + 1)
                        if f == 0:
                            wait(act, done("a_pt_ps"), 2 * (i - 1))
                            wait(act, done("a_sm"), i - 1)
                        act.activation(a_s[:, u, 512 * f:512 * f + 512], bank[f][:, :], ACT.Copy).then_inc(done("a_s"), 1)
                if j >= 0:
                    for h in range(2):
                        wait(act, done("a_pt_ps"), 2 * j + h + 1)
                        wait(act, done("a_pv_ps"), j)
                        act.activation(a_ptb[:, 4 * h:4 * h + 4, :], bank[2 + h][:, :].rearrange("p (c t) -> p c t", c=4),
                                       ACT.Copy).then_inc(done("a_pt"), 1)
                if i < NG:
                    act.wait_ge(done("k_ps"), i + 1)
                    wait(act, done("k_sq"), i)
                    act.activation(bank[6][:, D:2 * D], bank[6][:, 0:D], ACT.Square, scale=RMS_SCALE, accum_out=k_ss[:, i:i + 1])\
                       .then_inc(done("k_sq"), 1)
                else:
                    own_b = act_front(act, MOE, 0, MOE["front0"])
                    next(own_b)
                if i == 0:
                    act.wait_ge(done("gates_in"), 32)
                    act.activation(gates[:], gates[:], ACT.Tanh).then_inc(done("gates"), 1)
                if i + 1 < NG:
                    q_out(i + 1)
                if i < NG:
                    act_split0(act, 2 * i)
                if j >= 0:
                    wait(act, done("a_pv_ps"), j + 1)
                    wait(act, done("a_o_ps"), j)
                    act.activation(a_at[:], left(bank[5]), ACT.Copy).then_inc(done("a_at"), 1)
                if i < NG:
                    wait(act, done("a_sub"), i + 1)
                    act.activation(a_s[:, u, :], a_s[:, u, :], ACT.Exp, scale=SCALE).then_inc(done("a_exp"), 1)
                    wait(act, done("kt_ps"), i + 1)
                    act.activation(kt_hi[:, :, i * P:(i + 1) * P], left(bank[4]), ACT.Copy).then_inc(done("kt_hi"), 1)
                    act_split0(act, 2 * i + 1)
                else:
                    next(own_b)
                if i == 2:
                    late()

            def xt_out(b, bk):
                wait(act, done("c_xt_ps"), b + 1)
                wait(act, done("c_q_ps"), b)
                act.activation(c_xt[:], halves(bk), ACT.Copy).then_inc(done("c_xt"), 1)

            def squares(b):
                wait(act, done("c_q"), b + 1)
                wait(act, done("c_rq_ve"), b)
                for t in range(2):
                    wait(act, done("c_sq"), 2 * b + t)
                    act.activation(stage[:, 1, 0:D], c_qb[:, t, :], ACT.Square, scale=RMS_SCALE / SCALE, accum_out=c_ss[:, t:t + 1])\
                       .then_inc(done("c_sq"), 1)

            def qt_out(b, bk):
                wait(act, done("c_qt_ps"), b + 1)
                wait(act, done("c_s_ps"), 2 * b)
                act.activation(c_qth[:], halves(bk), ACT.Copy).then_inc(done("c_qth"), 1)

            def p_out(b, t):
                for h in range(2):
                    n = 4 * b + 2 * t + h
                    wait(act, done("c_pt_ps"), n + 1)
                    wait(act, done("c_pv_ps"), b)
                    act.activation(c_ptb[:, 4 * h:4 * h + 4, t * P:(t + 1) * P],
                                   bank[4 + h][:, :].rearrange("p (c t) -> p c t", c=4), ACT.Copy).then_inc(done("c_pt"), 1)

            def exps(b, t):
                wait(act, done("c_rq"), b + 1)
                wait(act, done("c_sub"), 4 * b + 2 * t + 2)
                act.activation(c_e[:, t, :], c_e[:, t, :], ACT.Exp, scale=c_rq[:, t:t + 1]).then_inc(done("c_exp"), 1)

            def split1(c):
                act.wait_ge(done("w1_in"), 16 * (c + 1))
                act.activation(w_hi[:, bass.ds(c * CHUNK, CHUNK)], stage[:, 0], ACT.Copy).then_inc(done("w1_hi"), 1)

            def step_c(i, mid=True, front=True, rest=True, split=None, fronts=()):
                j = i - 1
                if rest:
                    p_out(j, 0)
                if front:
                    xt_out(i + 1, bank[6])
                for t in fronts[:1]:
                    next(t)
                if rest:
                    p_out(j, 1)
                    wait(act, done("c_pv_ps"), j)
                    act.activation(c_v[:], v1[:, j, :], ACT.Copy).then_inc(done("c_v"), 1)
                if split is not None:
                    split1(split)
                if mid:
                    exps(i, 0)
                if front:
                    squares(i + 1)
                    qt_out(i + 1, bank[6])
                if mid:
                    exps(i, 1)
                for t in fronts[1:]:
                    next(t)

            act.wait_ge(done("a_x"), 2 * NG)
            act.wait_ge(done("a_xm"), 3 * NG)
            act.wait_ge(done("late_lo"), 1)
            next(own_b)
            act_ffn(act, MOE, own_b, {5: lambda: xt_out(0, bank[7]), 8: lambda: squares(0), 9: lambda: qt_out(0, bank[7])})

            step_c(0, rest=False)
            step_c(1)
            with act.Fori(2, NB - 2) as i:
                step_c(i)
            step_c(NB - 2, split=0)
            step_c(NB - 1, front=False, split=1)
            own_d = act_front(act, FFN, 0, FFN["front0"])
            step_c(NB, mid=False, front=False, split=2, fronts=(own_d, own_d))

            act.wait_ge(done("c_pv_ps"), NB)
            act_ffn(act, FFN, None, {"first": {c: lambda c=c: split1(c + EARLY1) for c in range(NC1 - EARLY1)}})

        def dve_stats(dve, ph, g):
            p = ph["name"]
            wait(dve, done(p + "xn"), GT * g)
            for t in range(GT):
                dve.bn_stats(stat[:, t, :], x_sb[:, GT * g + t, :]).then_inc(done(p + "bn"), 1)

        def dve_aggr(dve, ph):
            for t in range(GT):
                dve.bn_aggr(mv[:, t, :], stat[:, t, :]).then_inc(done(ph["name"] + "mv"), 1)

        def dve_norm(dve, ph, g):
            p = ph["name"]
            dve.wait_ge(done(p + "rstd"), g + 1)
            wait(dve, done(p + "xt_ps"), 2 * g)
            for t in range(GT):
                dve.tensor_scalar(f_xnb[:, t, :], x_sb[:, GT * g + t, :], mv[:, t, 0:1], rstd[:, t:t + 1],
                                  ALU.subtract, ALU.mult).then_inc(done(p + "xn"), 1)

        def dve_front(dve, ph, g, bk):
            p = ph["name"]
            for f in range(2):
                dve.wait_ge(done(p + "xth"), 2 * g + f + 1)
                dve.tensor_tensor(xt[:, g % 2, 1, f, :], bk[:, :], xt[:, g % 2, 0, f, :].bitcast(F32),
                                  ALU.subtract).then_inc(done(p + "xtl"), 1)
                yield
            if ph["moe"]:
                dve.wait_ge(done(p + "lt_ps"), g + 1)
                wait(dve, done(p + "c"), g)
                dve.tensor_copy(lg[:], bk[:, :].rearrange("p (t e) -> p t e", t=GT)[:, :, 0:9]).then_inc(done(p + "lg"), 1)
                dve.wait_ge(done(p + "lg"), g + 1)
                dve.tensor_reduce(r_m[:], lg[:, :, 0:8], AX.X, ALU.max).then_inc(done(p + "m"), 1)
                dve.wait_ge(done(p + "m"), g + 1)
                dve.tensor_tensor(r_z[:], lg[:, :, 0:8], over(r_m), ALU.subtract).then_inc(done(p + "z"), 1)
                yield
                dve.wait_ge(done(p + "es"), g + 1)
                n = [0]

                def link(ins):
                    n[0] += 1
                    ins.then_inc(done(p + "r"), 1)
                    dve.wait_ge(done(p + "r"), ROUTER_STEPS * g + n[0])

                link(dve.tensor_reduce(r_den[:, :, 0:1], r_p[:], AX.X, ALU.add))
                link(dve.tensor_scalar(r_den[:, :, 1:2], r_es[:], 1.0, None, ALU.add))
                link(dve.reciprocal(r_inv[:], r_den[:]))
                link(dve.tensor_tensor(r_p[:], r_p[:], r_inv[:, :, 0:1].broadcast_to([P, GT, 8]), ALU.mult))
                link(dve.tensor_reduce(r_m[:], r_p[:], AX.X, ALU.max))
                link(dve.tensor_tensor(r_k[:], r_p[:], over(r_m), ALU.is_equal))
                link(dve.tensor_tensor(r_k[:], r_k[:], w8.unsqueeze(1).broadcast_to([P, GT, 8]), ALU.mult))
                link(dve.tensor_reduce(r_m[:], r_k[:], AX.X, ALU.max))
                link(dve.tensor_tensor(r_o1[:], r_k[:], over(r_m), ALU.is_equal))
                link(dve.scalar_tensor_tensor(out=r_z[:], in0=r_o1[:], scalar=-2.0, in1=r_p[:], op0=ALU.mult, op1=ALU.add))
                link(dve.tensor_reduce(r_m[:], r_z[:], AX.X, ALU.max))
                link(dve.tensor_tensor(r_k[:], r_z[:], over(r_m), ALU.is_equal))
                link(dve.tensor_tensor(r_k[:], r_k[:], w8.unsqueeze(1).broadcast_to([P, GT, 8]), ALU.mult))
                link(dve.tensor_reduce(r_m[:], r_k[:], AX.X, ALU.max))
                link(dve.tensor_tensor(r_o2[:], r_k[:], over(r_m), ALU.is_equal))
                link(dve.tensor_tensor(r_o1[:], r_o1[:], r_o2[:], ALU.add))
                link(dve.tensor_tensor(r_c[:, :, 0:8], r_o1[:], r_p[:], ALU.mult))
                link(dve.tensor_copy(r_c[:, :, 8:9], r_inv[:, :, 1:2]))
                wait(dve, done(p + "ct_ps"), g)
                link(dve.tensor_copy(r_cd[:, :, 0:9], r_c[:]))
                assert n[0] == ROUTER_STEPS
                dve.tensor_tensor(r_cd[:, :, 32:41], r_c[:], r_cd[:, :, 0:9].bitcast(F32), ALU.subtract)\
                   .then_inc(done(p + "c"), 1)
                yield
                yield

        ROUTER_STEPS = 19

        def over(m):
            return m[:].unsqueeze(2).broadcast_to([P, GT, 8])

        def dve_split0(dve, n):
            at = slice(n * CHUNK, (n + 1) * CHUNK)
            dve.wait_ge(done("w0_hi"), n + 1)
            dve.tensor_tensor(w_lo[:, at], stage[:, 1], w_hi[:, at].bitcast(F32), ALU.subtract).then_inc(done("w0_lo1"), 1)

        def dve_tail(dve, ph, g, q):
            p = ph["name"]
            dve.wait_ge(done(p + "yt_ps"), 2 * g + q + 1)
            xs = x_sb[:, bass.ds(GT * g + 2 * q, 2), :]
            dve.scalar_tensor_tensor(out=xs, in0=bank[7][:, :].rearrange("p (t d) -> p t d", t=2),
                                     scalar=gates[:, ph["gate"]:ph["gate"] + 1], in1=xs,
                                     op0=ALU.mult, op1=ALU.add).then_inc(done(p + "x"), 1)

        def low_part(eng, ph, c, n):
            p = ph["name"]
            eng.wait_ge(done(p + "hhi"), n + 1)
            wait(eng, done(p + "dn"), n - back(c, 3, ph["chunks"]) + 1)
            eng.tensor_tensor(h_lo[:, c % 3, :], h_sb[:, c % 2, :], h_hi[:, c % 3, :].bitcast(F32), ALU.subtract)\
               .then_inc(done(p + "hlo"), 1)

        def dve_ffn(dve, ph, after):
            p, nch, moe = ph["name"], ph["chunks"], ph["moe"]

            def group(g, prev, nxt, split, after):
                front = dve_front(dve, ph, g + 1, bank[7]) if nxt else None
                for c in range(nch):
                    n = g * nch + c
                    if nxt and c == 1:
                        dve.wait_ge(done(p + "bn"), GT * (g + 2))
                    dve.wait_ge(done(p + "silu"), n + 1)
                    dve.wait_ge(done(p + "up_ps"), n + 1)
                    wait(dve, done(p + "h" if moe else p + "hlo"), n - back(c, 2, nch) + 1)
                    if moe:
                        dve.tensor_tensor(t_sb[:, c % 2, :], s_sb[:, c % 2, :], bank[2 + c % 2][:, :], ALU.mult)\
                           .then_inc(done(p + "t"), 1)
                        dve.wait_ge(done(p + "t"), n + 1)
                        dve.wait_ge(done(p + "cb_ps"), n + 1)
                        wait(dve, done(p + "hlo"), n - back(c, 2, nch) + 1)
                        dve.tensor_tensor(h_sb[:, c % 2, :], t_sb[:, c % 2, :], bank[4][:, :], ALU.mult)\
                           .then_inc(done(p + "h"), 1)
                    else:
                        dve.tensor_tensor(h_sb[:, c % 2, :], s_sb[:, c % 2, :], bank[2 + c % 2][:, :], ALU.mult)\
                           .then_inc(done(p + "t"), 1)
                        if c >= 1:
                            low_part(dve, ph, c - 1, n - 1)
                        elif prev:
                            low_part(dve, ph, nch - 1, n - 1)
                    if moe and split and c + EARLY < nch and (c + EARLY) % 2:
                        dve_split0(dve, c + EARLY)
                    if nxt and c == 0:
                        dve_stats(dve, ph, g + 1)
                    if nxt and c == 1:
                        dve_aggr(dve, ph)
                    if nxt and c == 2:
                        dve_norm(dve, ph, g + 1)
                    if prev and c in ph["tail_at"]:
                        dve_tail(dve, ph, g - 1, ph["tail_at"].index(c))
                    if nxt and c in ph["front_at"]:
                        next(front)
                    if c in after:
                        after[c]()

            group(0, False, True, True, after.get("first", {}))
            with dve.Fori(1, NG - 1) as g:
                group(g, True, True, False, {})
            group(NG - 1, True, False, False, after)
            if not moe:
                low_part(dve, ph, nch - 1, NG * nch - 1)

        @block.vector
        def _(dve):
            dve.memset(avg[:], 1.0 / SK).then_inc(done("avg_set"), 1)

            def stats_a(k):
                wait(dve, done("a_xn"), 2 * k)
                for e in range(2):
                    dve.bn_stats(stat[own[e], 0, :], x_sb[own[e], GT * k + 1 + 2 * e, :]).then_inc(done("a_bn"), 1)

            def aggr_a(k):
                dve.wait_ge(done("a_bn"), 2 * (k + 1))
                dve.bn_aggr(mv[:, 0, :], stat[:, 0, :]).then_inc(done("a_mv"), 1)

            def norm_a(k):
                dve.wait_ge(done("a_rstd"), k + 1)
                wait(dve, done("a_xt_ps"), k)
                for e in range(2):
                    dve.tensor_scalar(a_xnb[own[e], :], x_sb[own[e], GT * k + 1 + 2 * e, :], mv[own[e], 0, 0:1], rstd[own[e], 0:1],
                                      ALU.subtract, ALU.mult).then_inc(done("a_xn"), 1)

            def per_head(t):
                return t.unsqueeze(2).broadcast_to([P, NH, SK])

            dve.wait_ge(done("x0_in"), 48)
            stats_a(0)
            aggr_a(0)
            norm_a(0)
            for i in range(NG + 1):
                j, u = i - 1, i % 2
                if i == 0:
                    dve.wait_ge(done("kv_in"), 32)
                    dve.tensor_tensor(bkv[:, 2, :], bkv[:, 2, :], bkv[:, 3, :], ALU.mult).then_inc(done("gain"), 1)
                    dve.wait_ge(done("x_in"), 48)
                if i == 1:
                    dve.wait_ge(done("x_rest_in"), 32)
                if i + 1 < NG:
                    stats_a(i + 1)
                    aggr_a(i + 1)
                    norm_a(i + 1)
                if i == NG:
                    dve_stats(dve, MOE, 0)
                if i < NG:
                    if i == 0:
                        dve.wait_ge(done("gain"), 1)
                    dve.wait_ge(done("k_r"), i + 1)
                    wait(dve, done("kt_ps"), i)
                    dve.scalar_tensor_tensor(out=kn_sb[:], in0=bank[6][:, 0:D], scalar=k_r[:, i:i + 1], in1=bkv[:, 2, :],
                                             op0=ALU.mult, op1=ALU.mult).then_inc(done("kn"), 1)
                    dve.wait_ge(done("a_msk"), 2 * (i + 1))
                    dve.tensor_reduce(a_mx[:], by_head(a_s[:, u, :], NH), AX.X, ALU.max).then_inc(done("a_mx"), 1)
                    dve.wait_ge(done("a_mx"), i + 1)
                    dve.tensor_tensor(by_head(a_s[:, u, :], NH), by_head(a_s[:, u, :], NH), per_head(a_mx[:]), ALU.subtract)\
                       .then_inc(done("a_sub"), 1)
                if i == NG:
                    dve.wait_ge(done("b_bn"), GT)
                    dve_aggr(dve, MOE)
                    dve_norm(dve, MOE, 0)
                    own_b = dve_front(dve, MOE, 0, MOE["front0"])
                    next(own_b)
                if i < NG:
                    dve.wait_ge(done("v_ps"), i + 1)
                    dve.tensor_tensor(v1[:, 2 * i:2 * i + 2, :], bank[7][:, :].rearrange("p (e d) -> p e d", e=2),
                                      vmask.unsqueeze(1).broadcast_to([P, 2, D]), ALU.mult).then_inc(done("v1_set"), 1)
                    dve.wait_ge(done("kt_hi"), i + 1)
                    at = slice(i * P, (i + 1) * P)
                    dve.tensor_tensor(kt_lo[:, :, at], left(bank[4]), kt_hi[:, :, at].bitcast(F32), ALU.subtract)\
                       .then_inc(done("kt_lo"), 1)
                if j >= 0:
                    dve.wait_ge(done("a_exp"), j + 1)
                    dve.tensor_reduce(a_sm[:], by_head(a_s[:, 1 - u, :], NH), AX.X, ALU.add).then_inc(done("a_sm"), 1)
                    dve.wait_ge(done("a_sm"), j + 1)
                    dve.reciprocal(a_ri[:], a_sm[:]).then_inc(done("a_ri"), 1)
                    dve.wait_ge(done("gates"), 1)
                    dve.wait_ge(done("a_m_ps"), j + 1)
                    for rows, tiles, cols in ((slice(0, P), slice(GT * j, GT * j + 3, 2), slice(0, 2 * D)),
                                              (upper, slice(GT * j + 1, GT * j + 2), slice(0, D)),
                                              (lower, slice(GT * j + 3, GT * j + 4), slice(D, 2 * D))):
                        xs = x_sb[rows, tiles, :]
                        dve.scalar_tensor_tensor(out=xs, in0=bank[7][rows, cols].rearrange("p (t d) -> p t d", d=D),
                                                 scalar=gates[rows, 0:1], in1=xs, op0=ALU.mult, op1=ALU.add)\
                           .then_inc(done("a_xm"), 1)
                    dve.wait_ge(done("a_ri"), j + 1)
                    dve.wait_ge(done("a_o_ps"), j + 1)
                    dve.tensor_tensor(a_tmpb[:].rearrange("p (h e) -> p h e", h=NH),
                                      bank[6][:, 0:D].rearrange("p (h e) -> p h e", h=NH),
                                      a_ri[:].unsqueeze(2).broadcast_to([P, NH, HD]), ALU.mult).then_inc(done("a_tmp"), 1)
                    dve.wait_ge(done("a_tmp"), j + 1)
                    for e in range(2):
                        xs = x_sb[own[e], GT * j + 1 + 2 * e, :]
                        dve.scalar_tensor_tensor(out=xs, in0=a_tmpb[own[e], :], scalar=gates[own[e], 0:1], in1=xs,
                                                 op0=ALU.mult, op1=ALU.add).then_inc(done("a_x"), 1)
                    dve.wait_ge(done("a_x"), 2 * (j + 1))
                if i < NG:
                    dve_split0(dve, 2 * i + 1)
                if i == 3:
                    dve.wait_ge(done("late_hi"), 1)
                    dve.tensor_tensor(rw_lo[:], rw_raw[:], rw_hi[:].bitcast(F32), ALU.subtract).then_inc(done("late_lo"), 1)

            def stats_c(b):
                wait(dve, done("c_xn"), b)
                for t in range(2):
                    dve.bn_stats(stat[:, t, :], x_sb[:, 2 * b + t, :]).then_inc(done("c_bn"), 1)

            def aggr_c():
                for t in range(2):
                    dve.bn_aggr(mv[:, t, :], stat[:, t, :]).then_inc(done("c_mv"), 1)

            def q_bias(b, bk):
                dve.wait_ge(done("c_q_ps"), b + 1)
                wait(dve, done("c_qt_ps"), b)
                wait(dve, done("c_sq"), 2 * b)
                dve.tensor_tensor(c_qb[:], halves(bk), bias_sb[:, 0, :].unsqueeze(1).broadcast_to([P, 2, D]), ALU.add)\
                   .then_inc(done("c_q"), 1)

            def qt_low(b, bk):
                dve.wait_ge(done("c_qth"), b + 1)
                dve.tensor_tensor(c_qtl[:], halves(bk), c_qth[:].bitcast(F32), ALU.subtract).then_inc(done("c_qtl"), 1)

            def shift(b, t, first):
                dve.wait_ge(done("c_s_ps"), 2 * b + t + 1)
                for f in range(2):
                    dve.tensor_reduce(c_mx[:, t, 8 * f:8 * f + 8], by_head(bank[2 * t + f][:, :], 8), AX.X, ALU.max)\
                       .then_inc(done("c_mx"), 1)
                if not first:
                    wait(dve, done("c_pt_ps"), 4 * b + 2 * t - 2)
                for f in range(2):
                    dve.wait_ge(done("c_mx"), 4 * b + 2 * t + f + 1)
                    sub = dve.tensor_tensor(by_head(c_e[:, t, 512 * f:512 * f + 512], 8), by_head(bank[2 * t + f][:, :], 8),
                                            c_mx[:, t, 8 * f:8 * f + 8].unsqueeze(2).broadcast_to([P, 8, SK]), ALU.subtract)
                    sub.then_inc(done("c_sub"), 1)

            def inverse(m, bk=bank[0]):
                dve.wait_ge(done("c_d_ps"), m + 1)
                dve.reciprocal(c_atb[:], halves(bk)).then_inc(done("c_rd"), 1)

            def divided(m):
                dve.wait_ge(done("c_rd"), m + 1)
                dve.wait_ge(done("c_pv_ps"), m + 1)
                dve.tensor_tensor(c_atb[:], halves(bank[7]), c_atb[:], ALU.mult).then_inc(done("c_at"), 1)

            def add_c(m):
                dve.wait_ge(done("c_o_ps"), m + 1)
                dve.wait_ge(done("c_xb"), m + 1)
                xs = x_sb[:, bass.ds(2 * m, 2), :]
                dve.scalar_tensor_tensor(out=xs, in0=halves(bank[7]), scalar=gates[:, 1:2], in1=xs,
                                         op0=ALU.mult, op1=ALU.add).then_inc(done("c_x"), 1)

            def step_c(i, mid=True, front=True, pre=True, rest=True, out=True, tails=(), first=False, fronts=()):
                m = i - 2
                if pre:
                    stats_c(i + 2)
                if mid and tails:
                    shift(i, 0, first)
                    for q in tails:
                        dve_tail(dve, MOE, NG - 1, q)
                    dve.wait_ge(done("b_x"), 2 * NG)
                if pre:
                    dve.wait_ge(done("c_bn"), 2 * (i + 3))
                if out:
                    inverse(m)
                elif pre:
                    dve.wait_ge(done("c_bn"), 2 * (i + 3))
                if pre:
                    aggr_c()
                for t in fronts[:1]:
                    next(t)
                if out:
                    divided(m)
                if mid and not tails:
                    shift(i, 0, first)
                if front:
                    q_bias(i + 1, bank[6])
                if out:
                    add_c(m)
                for t in fronts[1:]:
                    next(t)
                if mid:
                    shift(i, 1, first)
                if front:
                    qt_low(i + 1, bank[6])

            next(own_b)
            dve.wait_ge(done("a_xm"), 3 * NG)
            dve.memset(r_cd[:].bitcast(F32), 0.0).then_inc(done("cd_zero"), 1)
            dve.wait_ge(done("cd_zero"), 1)
            next(own_b)
            next(own_b)

            def ready(b):
                def go():
                    stats_c(b)
                    dve.wait_ge(done("c_bn"), 2 * (b + 1))
                    aggr_c()
                return go

            def gated_bias():
                dve.tensor_scalar(bias_sb[:, 1, :], bias_sb[:, 1, :], gates[:, 1:2], None, ALU.mult).then_inc(done("gate_bo"), 1)

            dve_ffn(dve, MOE, {1: gated_bias, 2: ready(0), 6: ready(1), 7: lambda: q_bias(0, bank[7]), 9: lambda: qt_low(0, bank[7])})

            step_c(0, rest=False, out=False, tails=(0, 1), first=True)
            step_c(1, out=False)
            with dve.Fori(2, NB - 2) as i:
                step_c(i)
            step_c(NB - 2, pre=False)
            dve_stats(dve, FFN, 0)
            step_c(NB - 1, front=False, pre=False)
            dve.wait_ge(done("d_bn"), GT)
            dve_aggr(dve, FFN)
            dve_norm(dve, FFN, 0)
            own_d = dve_front(dve, FFN, 0, FFN["front0"])
            step_c(NB, mid=False, front=False, pre=False, fronts=(own_d, own_d))
            inverse(NB - 1, bank[4])
            divided(NB - 1)

            dve_ffn(dve, FFN, {"first": {1: lambda: add_c(NB - 1)}})
            for q in range(2):
                dve_tail(dve, FFN, NG - 1, q)

        def power(pool, var, scratch, dst, eps, after, name):
            n = var.shape[1]
            pool.tensor_tensor(scratch, var, eps[:, 0:n], ALU.add).then_inc(done(name + "_ve"), 1)
            pool.wait_ge(done(name + "_ve"), after)
            pool.tensor_tensor(dst, scratch, neghalf[:, 0:n], ALU.pow).then_inc(done(name), 1)

        def pool_rsqrt(pool, ph, g):
            p = ph["name"]
            pool.wait_ge(done(p + "mv"), GT * (g + 1))
            wait(pool, done(p + "xn"), GT * g)
            power(pool, mv[:, :, 1], ve[:], rstd[:], ln_eps, g + 1, p + "rstd")

        def pool_split0(pool, n):
            at = slice(n * CHUNK, (n + 1) * CHUNK)
            pool.wait_ge(done("w0_hi"), n + 1)
            pool.tensor_tensor(w_lo[:, at], stage[:, 0], w_hi[:, at].bitcast(F32), ALU.subtract).then_inc(done("w0_lo0"), 1)

        def pool_ffn(pool, ph, after):
            p, nch = ph["name"], ph["chunks"]

            def group(g, nxt, split, after):
                for c in range(nch):
                    n = g * nch + c
                    if nxt and c == 1:
                        pool_rsqrt(pool, ph, g + 1)
                    if ph["moe"]:
                        low_part(pool, ph, c, n)
                    if ph["moe"] and split and c + EARLY < nch and (c + EARLY) % 2 == 0:
                        pool_split0(pool, c + EARLY)
                    if c in after:
                        after[c]()

            group(0, True, True, after.get("first", {}))
            with pool.Fori(1, NG - 1) as g:
                group(g, True, False, {})
            group(NG - 1, False, False, after)

        def spread(pool, dst, keys):
            return pool.tensor_tensor(by_head(dst, 8), keys.unsqueeze(1).broadcast_to([P, 8, SK]),
                                      headmask.unsqueeze(2).broadcast_to([P, 8, SK]), ALU.mult)

        @block.gpsimd
        def _(pool):
            def rsqrt_a(k):
                pool.wait_ge(done("a_mv"), k + 1)
                power(pool, mv[:, 0, 1:2], ve[:, 0:1], rstd[:, 0:1], ln_eps, k + 1, "a_rstd")

            def keys_a(k):
                for e in range(2):
                    for f in range(2):
                        wait(pool, done("a_s_ps"), 2 * k)
                        at = slice((2 * k + e) * SK, (2 * k + e + 1) * SK)
                        spread(pool, a_kb[:, e, f, :], ctxt[:, f, at]).then_inc(done("a_kb"), 1)

            pool.wait_ge(done("setup_in"), 32)
            rsqrt_a(0)
            keys_a(0)
            for i in range(NG):
                u = i % 2
                if i + 1 < NG:
                    rsqrt_a(i + 1)
                pool.wait_ge(done("a_s"), 2 * (i + 1))
                for e in range(2):
                    if e == 1:
                        pool.wait_ge(done("a_msk"), 2 * i + 1)
                    v = by_head(a_s[own[e], u, :], NH)
                    pool.affine_select(out=v, in_=v, compare_op=ALU.is_ge, fill=MASKED, base=0,
                                       pattern=[[0, NH], [-1, SK]], channel_multiplier=1).then_inc(done("a_msk"), 1)
                pool.wait_ge(done("a_msk"), 2 * (i + 1))
                pool.wait_ge(done("k_sq"), i + 1)
                power(pool, k_ss[:, i:i + 1], k_ve[:, i:i + 1], k_r[:, i:i + 1], rms_eps, i + 1, "k_r")
                if i + 1 < NG:
                    keys_a(i + 1)
                else:
                    pool_rsqrt(pool, MOE, 0)
                pool_split0(pool, 2 * i)

            def rstd_c(b):
                pool.wait_ge(done("c_mv"), 2 * (b + 1))
                power(pool, mv[:, 0:2, 1], ve[:, 0:2], rstd[:, 0:2], ln_eps, b + 1, "c_rstd")

            def norm_c(b):
                wait(pool, done("c_rstd"), b + 1)
                wait(pool, done("c_xt_ps"), b)
                pool.tensor_tensor(c_xnb[:], x_sb[:, bass.ds(2 * b, 2), :], mv[:, 0:2, 0:1].broadcast_to([P, 2, D]), ALU.subtract)\
                    .then_inc(done("c_xm"), 1)
                pool.wait_ge(done("c_xm"), b + 1)
                pool.tensor_tensor(c_xnb[:], c_xnb[:], rstd[:, 0:2].unsqueeze(2).broadcast_to([P, 2, D]), ALU.mult)\
                    .then_inc(done("c_xn"), 1)

            def keys_c(b):
                wait(pool, done("c_s_ps"), 2 * b)
                for f in range(2):
                    for dst, src in ((c_kbh, kt_hi), (c_kbl, kt_lo)):
                        spread(pool, dst[:, f, :], src[:, f, bass.ds(b * SK, SK)].bitcast(F32)).then_inc(done("c_kb"), 1)

            def bias_c(b):
                pool.wait_ge(done("c_xn"), b + 1)
                xs = x_sb[:, bass.ds(2 * b, 2), :]
                pool.tensor_tensor(xs, xs, bias_sb[:, 1, :].unsqueeze(1).broadcast_to([P, 2, D]), ALU.add).then_inc(done("c_xb"), 1)

            def rsqrt_q(b):
                pool.wait_ge(done("c_sq"), 2 * (b + 1))
                wait(pool, done("c_exp"), 2 * b)
                power(pool, c_ss[:], c_ve[:], c_rq[:], rmsq_eps, b + 1, "c_rq")

            def split1(c):
                pool.wait_ge(done("w1_hi"), c + 1)
                at = bass.ds(c * CHUNK, CHUNK)
                pool.tensor_tensor(w_lo[:, at], stage[:, 0], w_hi[:, at].bitcast(F32), ALU.subtract).then_inc(done("w1_lo"), 1)

            def step_c(i, front=True, pre=True, split=None):
                if front:
                    bias_c(i + 1)
                if split is not None:
                    split1(split)
                if pre:
                    rstd_c(i + 2)
                    norm_c(i + 2)
                if front:
                    keys_c(i + 1)
                    rsqrt_q(i + 1)

            pool.wait_ge(done("a_x"), 2 * NG)
            pool_ffn(pool, MOE, {2: lambda: (rstd_c(0), norm_c(0)), 5: lambda: bias_c(0), 6: lambda: (rstd_c(1), norm_c(1)),
                                 9: lambda: rsqrt_q(0)})

            keys_c(0)
            step_c(0)
            step_c(1)
            with pool.Fori(2, NB - 2) as i:
                step_c(i)
            step_c(NB - 2, pre=False, split=0)
            step_c(NB - 1, front=False, pre=False, split=1)
            pool_rsqrt(pool, FFN, 0)
            split1(2)

            pool_ffn(pool, FFN, {"first": {c: lambda c=c: split1(c + EARLY1) for c in range(NC1 - EARLY1)}})


def kernel(**inputs):
    import numpy as np
    import concourse.bacc as bacc
    from concourse.bass_utils import run_bass_kernel_spmd

    a = {k: np.asarray(v) for k, v in inputs.items()}

    def halves(w):
        return w.reshape(2, P, -1).transpose(1, 0, 2)

    def packed(gate, up, down):
        parts = [halves(w).reshape(P, 2, -1, P).transpose(0, 2, 1, 3).reshape(P, -1, D) for w in (gate, up)]
        parts.append(down.reshape(-1, P, D).transpose(1, 0, 2))
        return np.ascontiguousarray(np.stack(parts, axis=2).reshape(P, -1))

    def experts(w, shared):
        w = np.concatenate([w.transpose(1, 0, 2).reshape(D, NE * FE), shared], axis=1)
        return np.concatenate([w, np.zeros((D, HID0 - w.shape[1]), w.dtype)], axis=1)

    down0 = np.concatenate([a["L0_ffn_Wd"].reshape(NE * FE, D), a["L0_ffn_Sd"],
                            np.zeros((HID0 - NE * FE - FS, D), np.float32)], axis=0)

    def projections(*names):
        return np.ascontiguousarray(np.stack([halves(a["L1_xattn_w_" + n].T) for n in names], axis=1))

    rw = np.concatenate([a["L0_ffn_Wr"], a["L0_ffn_Wsg"], np.zeros((D, P - NE - 1), np.float32)], axis=1)
    p = np.arange(P)[:, None]
    col = np.arange(D)[None, :]
    consts = np.concatenate([
        p == np.arange(P)[None, :],
        p // HD == np.arange(8)[None, :],
        col // HD % 2 == p // SK,
        np.arange(32)[None, :] // HD == p // SK,
        np.full((P, 4), -0.5),
        np.broadcast_to(np.arange(8, 0, -1), (P, 8)),
        np.full((P, 4), LN_EPS), np.full((P, 4), RMS_EPS),
        np.full((P, 4), RMS_EPS / SCALE ** 2),
        np.broadcast_to(p == 0, (P, P)),
    ], axis=1).astype(np.float32)
    unit = np.arange(HID0)
    owner = np.where(unit < NE * FE, unit // FE, np.where(unit < NE * FE + FS, NE, -1))
    row = np.arange(P)[:, None]
    sel = ((row < 64) & (row % 32 == owner[None, :])).astype(np.float32)

    token = a["ctx_2048"].transpose(1, 0, 2)
    ctx_v = np.zeros((P, NB, D), np.float32)
    for parity in range(2):
        cols = np.arange(D) // HD % 2 == parity
        ctx_v[parity * SK:(parity + 1) * SK][:, :, cols] = token[:, :, cols]

    arrays = {
        "x": a["x"], "ctx_v": ctx_v,
        "ctx_t": np.ascontiguousarray(halves(a["ctx_2048"].reshape(NB * SK, D).T)),
        "xw_kv": projections("k_img", "v_img"), "xw_qo": projections("q", "o"), "rw": np.ascontiguousarray(halves(rw)),
        "moe_w": packed(experts(a["L0_ffn_Wg"], a["L0_ffn_Sg"]), experts(a["L0_ffn_Wu"], a["L0_ffn_Su"]), down0),
        "ffn_w": packed(a["L1_ffn_w_gate"].T, a["L1_ffn_w_up"].T, a["L1_ffn_w_down"].T),
        "bias_kv": np.stack([a["L1_xattn_" + n] for n in ("b_k_img", "b_v_img", "g_k_img", "g_q")]),
        "bias_qo": np.stack([a["L1_xattn_" + n] for n in ("b_q", "b_o")]),
        "gx": a["g_xattn"], "gf": a["g_ffn"], "consts": consts, "sel": sel,
    }
    nc = bacc.Bacc("TRN2", target_bir_lowering=False, num_devices=1, dynamic_dma_scratch_size=1024)
    args = {k: nc.dram_tensor("in_" + k, v.shape, mybir.dt.from_np(v.dtype), kind="ExternalInput").ap()
            for k, v in arrays.items()}
    args["out"] = nc.dram_tensor("result", (NB, SQ, D), F32, kind="ExternalOutput").ap()
    build(nc, **args)
    r = run_bass_kernel_spmd(nc, [{"in_" + k: v for k, v in arrays.items()}], core_ids=[0])
    return r.results[0]["result"]
```

```python
from contextlib import ExitStack

import concourse.bass as bass
from concourse import mybir

F32 = mybir.dt.float32
F32R = mybir.dt.float32r
ALU = mybir.AluOpType
ACT = mybir.ActivationFunctionType
AX = mybir.AxisListType

P = 128
NB, SQ, D = 8, 256, 256
SK = 64
NH, HD = 16, 16
NT = NB * SQ // P
NE, FE, FS = 8, 176, 704
GT = 4
GN = GT * P
NG = NT // GT
NC0 = -(-(NE * FE + FS) // P)
HID0 = NC0 * P
HID1 = 1024
NC1 = HID1 // P
SCALE = 0.25
MASKED = -10000.0 / SCALE
LN_EPS, RMS_EPS = 1e-5, 1e-6
RMS_SCALE = 1 / 16
CHUNK = 6 * P
EARLY = NT // 4
EARLY1 = 3
C_ID, C_HM, C_VM, C_NH, C_W8, C_LE, C_RE, C_RQ, C_R0 = 0, 128, 136, 392, 396, 404, 408, 412, 416
CST = 544


def wait(eng, sem, n):
    if isinstance(n, int) and n <= 0:
        return
    eng.wait_ge(sem, n)


def build(nc, x, ctx_v, ctx_t, xw_kv, xw_qo, rw, moe_w, ffn_w, bias_kv, bias_qo, gx, gf, consts, sel, out):
    first = [-(-nc.sbuf_base // 32) * 32]

    def sb(name, shape, dt=F32, at=None):
        cur = first if at is None else at
        size = 4
        for s in shape[1:]:
            size *= s
        h = nc.alloc_sbuf_tensor_at(name, list(shape), dt, offset=cur[0])
        cur[0] += -(-size // 32) * 32
        assert cur[0] <= nc.sbuf_top, (name, cur)
        return h

    with ExitStack() as es:
        x_sb = sb("x_sb", [P, NT, D])
        cst = sb("cst", [P, CST])
        avg = sb("avg", [P, P])
        gates = sb("gates", [P, 4])
        bias_sb = sb("bias_sb", [P, 2, D])
        xw = sb("xw", [P, 2, 2, D])
        w_hi = sb("w_hi", [P, NC0 * CHUNK], F32R)
        w_lo = sb("w_lo", [P, NC0 * CHUNK], F32R)
        stage = sb("stage", [P, 2, CHUNK])
        c_go = stage[:, 1, D:3 * D].rearrange("p (t d) -> p t d", t=2)
        stat = sb("stat", [P, 4, 6])
        mv = sb("mv", [P, 4, 2])
        ve = sb("ve", [P, 4])
        rstd = sb("rstd", [P, 4])
        rw_hi = sb("rw_hi", [P, 2, P], F32R)
        rw_lo = sb("rw_lo", [P, 2, P], F32R)
        sel_sb = sb("sel_sb", [P, HID0], F32R)
        kt_hi = sb("kt_hi", [P, 2, NB * SK], F32R)
        kt_lo = sb("kt_lo", [P, 2, NB * SK], F32R)
        v1 = sb("v1", [P, NB, D])
        c_mx = sb("c_mx", [P, 2, NH])
        c_sm = sb("c_sm", [P, 2, NH])
        c_ri = sb("c_ri", [P, 2, NH])
        c_ss = sb("c_ss", [P, 2])
        c_ve = sb("c_ve", [P, 2])
        c_rq = sb("c_rq", [P, 2])
        ident = cst[:, C_ID:C_ID + P]
        headmask = cst[:, C_HM:C_HM + 8]
        vmask = cst[:, C_VM:C_VM + D]
        neghalf = cst[:, C_NH:C_NH + 4]
        w8 = cst[:, C_W8:C_W8 + 8]
        ln_eps = cst[:, C_LE:C_LE + 4]
        rms_eps = cst[:, C_RE:C_RE + 4]
        rmsq_eps = cst[:, C_RQ:C_RQ + 4]
        row0 = cst[:, C_R0:C_R0 + P]

        ra = [first[0]]
        sel_raw = sb("sel_raw", [P, HID0], F32, ra)
        rw_raw = sb("rw_raw", [P, 2, P], F32, ra)
        ctxt = sb("ctxt", [P, 2, NG, 3 * SK], F32, ra)
        a_kb = sb("a_kb", [P, 2, 2, 512], F32, ra)
        kv_raw = sb("kv_raw", [P, 2, 2, D], F32, ra)
        bkv = sb("bkv", [P, 4, D], F32, ra)
        a_xnb = sb("a_xnb", [P, D], F32, ra)
        kn_sb = sb("kn_sb", [P, D], F32, ra)
        a_qt = sb("a_qt", [P, 2, P], F32, ra)
        k_ss = sb("k_ss", [P, NG], F32, ra)
        k_ve = sb("k_ve", [P, NG], F32, ra)
        k_r = sb("k_r", [P, NG], F32, ra)
        a_s = sb("a_s", [P, 2, NH * SK], F32, ra)
        a_mx = sb("a_mx", [P, NH], F32, ra)
        a_sm = sb("a_sm", [P, NH], F32, ra)
        a_ri = sb("a_ri", [P, NH], F32, ra)
        a_out = sb("a_out", [P, 2, D], F32, ra)
        a_ptb = sb("a_ptb", [P, 8, P], F32, ra)
        a_at = sb("a_at", [P, 2, P], F32, ra)
        ctxv = sb("ctxv", [P, NB, D], F32, ra)
        rf = [first[0]]
        f_xnb = sb("f_xnb", [P, GT, D], F32, rf)
        xt = sb("xt", [P, 2, 2, 2, GN], F32R, rf)
        s_sb = sb("s_sb", [P, 2, GN], F32, rf)
        t_sb = sb("t_sb", [P, 2, GN], F32, rf)
        h_sb = sb("h_sb", [P, 2, GN], F32, rf)
        h_hi = sb("h_hi", [P, 3, GN], F32R, rf)
        h_lo = sb("h_lo", [P, 3, GN], F32R, rf)
        y_t = sb("y_t", [P, 2, GN], F32, rf)
        lgt = sb("lgt", [P, GN], F32, rf)
        c_t = sb("c_t", [P, 2, GN], F32R, rf)
        lg = sb("lg", [P, GT, 9], F32, rf)
        r_z = sb("r_z", [P, GT, 8], F32, rf)
        r_p = sb("r_p", [P, GT, 8], F32, rf)
        r_den = sb("r_den", [P, GT, 2], F32, rf)
        r_inv = sb("r_inv", [P, GT, 2], F32, rf)
        r_es = sb("r_es", [P, GT, 1], F32, rf)
        r_m = sb("r_m", [P, GT], F32, rf)
        r_k = sb("r_k", [P, GT, 8], F32, rf)
        r_o1 = sb("r_o1", [P, GT, 8], F32, rf)
        r_o2 = sb("r_o2", [P, GT, 8], F32, rf)
        r_c = sb("r_c", [P, GT, 9], F32, rf)
        r_cd = sb("r_cd", [P, GT, P], F32R, rf)
        rc = [first[0]]
        c_xnb = sb("c_xnb", [P, 2, D], F32, rc)
        c_qb = sb("c_qb", [P, 2, D], F32, rc)
        c_xt = sb("c_xt", [P, 2, SQ], F32, rc)
        c_qth = sb("c_qth", [P, 2, SQ], F32R, rc)
        c_qtl = sb("c_qtl", [P, 2, SQ], F32R, rc)
        rc[0] += 2048 + 8192
        c_kbh = sb("c_kbh", [P, 2, 512], F32R, rc)
        c_kbl = sb("c_kbl", [P, 2, 512], F32R, rc)
        c_e = sb("c_e", [P, 2, NH * SK], F32, rc)
        c_ptb = sb("c_ptb", [P, 8, SQ], F32, rc)
        c_v = sb("c_v", [P, D], F32, rc)
        c_atb = sb("c_atb", [P, 2, SQ], F32, rc)
        c_rx = sb("c_rx", [P, 2, D], F32, rc)
        c_rt = sb("c_rt", [P, 2, SQ], F32, rc)

        bank = [es.enter_context(nc.psum_tensor(f"bank{i}", [P, 512], F32)) for i in range(8)]

        S = {}

        def done(name):
            if name not in S:
                S[name] = es.enter_context(nc.semaphore(name))
            return S[name]

        block = es.enter_context(nc.Block())
        x_v = x.rearrange("b (j p) d -> p (b j) d", p=P)
        out_v = out.rearrange("b (j p) d -> p (b j) d", p=P)
        lower, upper = slice(0, 64), slice(64, P)
        own = (lower, upper)

        def halves(bk):
            return bk[:, :].rearrange("p (f t) -> p f t", f=2)

        def left(bk):
            return bk[:, 0:D].rearrange("p (f t) -> p f t", f=2)

        def by_head(t, n):
            return t.rearrange("p (h k) -> p h k", h=n)

        MOE = dict(name="b_", moe=True, chunks=NC0, gate=2, tail_at=(3, 4), front_at=(6, 7, 9, 10, 14), front0=bank[4])
        FFN = dict(name="d_", moe=False, chunks=NC1, gate=3, tail_at=(3, 4), front_at=(5, 6), front0=bank[6])

        @block.sync
        def _(sp):
            sp.dma_start(x_sb[lower, 1, :], x_v[upper, 1, :]).then_inc(done("x0_in"), 16)
            sp.dma_start(x_sb[:, 2:4, :], x_v[:, 2:4, :]).then_inc(done("x0_in"), 16)
            sp.dma_start(x_sb[upper, 1, :], x_v[lower, 1, :]).then_inc(done("x0_in"), 16)
            sp.dma_start(gates[:, 0:2], gx.rearrange("(a n) -> a n", a=1).broadcast_to([P, 2])).then_inc(done("gates_in"), 16)
            sp.dma_start(gates[:, 2:4], gf.rearrange("(a n) -> a n", a=1).broadcast_to([P, 2])).then_inc(done("gates_in"), 16)
            sp.dma_start(kv_raw[:], xw_kv).then_inc(done("kv_in"), 16)
            sp.dma_start(bkv[:], bias_kv.rearrange("(a n) d -> a n d", a=1).broadcast_to([P, 4, D])).then_inc(done("kv_in"), 16)
            sp.dma_start(x_sb[lower, GT + 1::GT, :], x_v[upper, GT + 1::GT, :]).then_inc(done("x_in"), 16)
            sp.dma_start(x_sb[upper, GT + 1::GT, :], x_v[lower, GT + 1::GT, :]).then_inc(done("x_in"), 16)
            sp.dma_start(x_sb[:, GT + 3::GT, :], x_v[:, GT + 3::GT, :]).then_inc(done("x_in"), 16)
            for u in range(2):
                sp.dma_start(stage[:, u], moe_w[:, u * CHUNK:(u + 1) * CHUNK]).then_inc(done(f"w0_in{u}"), 16)
            sp.dma_start(x_sb[:, GT + 2::GT, :], x_v[:, GT + 2::GT, :]).then_inc(done("x_rest_in"), 16)
            sp.dma_start(x_sb[:, 0::GT, :], x_v[:, 0::GT, :]).then_inc(done("x_rest_in"), 16)
            sp.dma_start(rw_raw[:], rw).then_inc(done("late_in"), 16)
            sp.dma_start(sel_raw[:], sel).then_inc(done("late_in"), 16)
            sp.dma_start(xw[:], xw_qo).then_inc(done("late_in"), 16)
            sp.dma_start(bias_sb[:], bias_qo.rearrange("(a n) d -> a n d", a=1).broadcast_to([P, 2, D])).then_inc(done("late_in"), 16)
            with sp.Fori(1, NC0 // 2) as b:
                for u in range(2):
                    sp.wait_ge(done(f"w0_lo{u}"), b)
                    sp.dma_start(stage[:, u], moe_w[:, bass.ds((2 * b + u) * CHUNK, CHUNK)]).then_inc(done(f"w0_in{u}"), 16)
            sp.wait_ge(done("w0_lo0"), NC0 // 2)
            sp.dma_start(stage[:, 0], moe_w[:, (NC0 - 1) * CHUNK:]).then_inc(done("w0_in0"), 16)
            sp.wait_ge(done("w0_lo0"), NC0 // 2 + 1)
            sp.dma_start(stage[:, 0], ffn_w[:, 0:CHUNK]).then_inc(done("w1_in"), 16)
            with sp.Fori(1, NC1) as c:
                sp.wait_ge(done("w1_lo"), c)
                sp.dma_start(stage[:, 0], ffn_w[:, bass.ds(c * CHUNK, CHUNK)]).then_inc(done("w1_in"), 16)
            def stores(g):
                sp.wait_ge(done("d_x"), 2 * g + 1)
                sp.dma_start(out_v[:, bass.ds(GT * g, 1), :], x_sb[:, bass.ds(GT * g, 1), :]).then_inc(done("out_done"), 16)
                sp.dma_start(out_v[upper, bass.ds(GT * g + 1, 1), :], x_sb[lower, bass.ds(GT * g + 1, 1), :]).then_inc(done("out_done"), 16)
                sp.dma_start(out_v[lower, bass.ds(GT * g + 1, 1), :], x_sb[upper, bass.ds(GT * g + 1, 1), :]).then_inc(done("out_done"), 16)

            with sp.Fori(0, NG - 1) as g:
                stores(g)
                sp.wait_ge(done("d_x"), 2 * g + 2)
                sp.dma_start(out_v[:, bass.ds(GT * g + 2, 2), :], x_sb[:, bass.ds(GT * g + 2, 2), :]).then_inc(done("out_done"), 16)
            stores(NG - 1)
            sp.wait_ge(done("out_done"), 16 * 4 * NG)

        last_banks = {"b": (bank[7], bank[5]), "d": (bank[7], bank[4])}

        def split_matmul(pe, dst, w_h, w_l, m_h, m_l, first, last):
            pe.matmul(dst, w_h, m_h, start=first, stop=False)
            pe.matmul(dst, w_h, m_l, start=False, stop=False)
            return pe.matmul(dst, w_l, m_h, start=False, stop=last)

        def back(c, ring, chunks):
            if c >= ring:
                return ring
            return c + chunks - max(k for k in range(chunks) if k % ring == c % ring)

        def weights(kind, kk, c):
            at = c * CHUNK + {"gate": 0, "up": 2 * P, "down": 4 * P}[kind] + kk * P
            return slice(at, at + P)

        def pe_front(pe, ph, g, bk):
            p = ph["name"]
            for f in range(2):
                wait(pe, done(p + "xn"), GT * (g + 1))
                if f == 0:
                    wait(pe, done(p + "x"), 2 * (g - 1))
                    if ph["moe"]:
                        wait(pe, done(p + "ct"), g)
                wait(pe, done(p + "xtl"), 2 * g + f)
                for t in range(GT):
                    mm = pe.transpose(bk[:, t * P:(t + 1) * P], f_xnb[:, t, f * P:(f + 1) * P], ident)
                mm.then_inc(done(p + "xt_ps"), 1)
                yield
            if ph["moe"]:
                wait(pe, done(p + "xtl"), 2 * g + 2)
                for kk in range(2):
                    mm = split_matmul(pe, bk[:, :], rw_hi[:, kk, :], rw_lo[:, kk, :],
                                      xt[:, g % 2, 0, kk, :], xt[:, g % 2, 1, kk, :], kk == 0, kk == 1)
                mm.then_inc(done(p + "lg_ps"), 1)
                yield
                wait(pe, done(p + "lgt"), g + 1)
                for t in range(GT):
                    mm = pe.transpose(bk[:, t * P:(t + 1) * P], lgt[:, t * P:(t + 1) * P], ident)
                mm.then_inc(done(p + "lt_ps"), 1)
                yield
                wait(pe, done(p + "c"), g + 1)
                for t in range(GT):
                    mm = pe.transpose(bk[:, t * P:(t + 1) * P], r_cd[:, t, :].bitcast(F32), ident)
                mm.then_inc(done(p + "ct_ps"), 1)
                yield

        def pe_down(pe, ph, g, c, n):
            p = ph["name"]
            wait(pe, done(p + "hlo"), n + 1)
            for f in range(2):
                if c == 0:
                    wait(pe, done(p + "y"), 2 * g)
                w = weights("down", f, c)
                mm = split_matmul(pe, bank[5 + f][:, :], w_hi[:, w], w_lo[:, w], h_hi[:, c % 3, :], h_lo[:, c % 3, :],
                                  c == 0, c == ph["chunks"] - 1)
            mm.then_inc(done(p + "dn"), 1)

        def pe_tail(pe, ph, g, q, bk=bank[7]):
            p = ph["name"]
            wait(pe, done(p + "y"), 2 * (g + 1))
            if q == 1 and bk is bank[7]:
                wait(pe, done(p + "x"), 2 * g + 1)
            for t in range(2):
                for f in range(2):
                    mm = pe.transpose(bk[:, t * D + f * P:t * D + (f + 1) * P],
                                      y_t[:, f, (2 * q + t) * P:(2 * q + t + 1) * P], ident)
            mm.then_inc(done(p + "yt_ps"), 1)

        def pe_ffn(pe, ph, own, after):
            p, nch, moe = ph["name"], ph["chunks"], ph["moe"]

            def spread_weights(g, c, n):
                wait(pe, done(p + "h"), n)
                if c == 0:
                    wait(pe, done(p + "ct"), g + 1)
                pe.matmul(bank[4][:, :], sel_sb[:, c * P:(c + 1) * P], c_t[:, g % 2, :],
                          start=True, stop=True).then_inc(done(p + "cb_ps"), 1)

            def group(g, prev, nxt, split, after):
                front = pe_front(pe, ph, g + 1, bank[7]) if nxt else None
                for c in range(nch):
                    n = g * nch + c
                    if c == 0:
                        wait(pe, done(p + "xtl"), 2 * (g + 1))
                    if split and moe:
                        wait(pe, done(f"w0_lo{c % 2}"), c // 2 + 1)
                    elif split:
                        wait(pe, done("w1_lo"), c + 1)
                    for kind, bk, freed in (("gate", bank[c % 2], "silu"), ("up", bank[2 + c % 2], "t")):
                        wait(pe, done(p + freed), n - back(c, 2, nch) + 1)
                        for kk in range(2):
                            w = weights(kind, kk, c)
                            mm = split_matmul(pe, bk[:, :], w_hi[:, w], w_lo[:, w],
                                              xt[:, g % 2, 0, kk, :], xt[:, g % 2, 1, kk, :], kk == 0, kk == 1)
                        mm.then_inc(done(p + kind + "_ps"), 1)
                    if moe and split and c < 2:
                        next(own)
                        if c == 1:
                            spread_weights(g, 0, n - 1)
                            spread_weights(g, 1, n)
                    elif moe:
                        spread_weights(g, c, n)
                    if c >= 2:
                        pe_down(pe, ph, g, c - 2, n - 2)
                    elif prev:
                        pe_down(pe, ph, g - 1, nch - 2 + c, n - 2)
                    if prev and c in ph["tail_at"]:
                        if c == ph["tail_at"][0]:
                            wait(pe, done(p + ("ct" if moe else "xtl")), (1 if moe else 2) * (g + 1))
                        pe_tail(pe, ph, g - 1, ph["tail_at"].index(c))
                    if nxt and c in ph["front_at"]:
                        next(front)
                    if c in after:
                        after[c]()

            group(0, False, True, True, after.get("first", {}))
            with pe.Fori(1, NG - 1) as g:
                group(g, True, True, False, {})
            group(NG - 1, True, False, False, after)
            for c in (nch - 2, nch - 1):
                pe_down(pe, ph, NG - 1, c, (NG - 1) * nch + c)

        @block.tensor
        def _(pe):
            def turn_a(k):
                wait(pe, done("a_xn"), 2 * (k + 1))
                wait(pe, done("kt_lo"), k - 1)
                for f in range(2):
                    mm = pe.transpose(bank[4][:, f * P:(f + 1) * P], a_xnb[:, f * P:(f + 1) * P], ident)
                mm.then_inc(done("a_xt_ps"), 1)

            def keys_values(k):
                if k == 0:
                    pe.wait_ge(done("kv_in"), 32)
                wait(pe, done("a_tmp"), 2 * (k - 1))
                for kk in range(2):
                    pe.matmul(bank[6][:, 0:D], ctxt[:, kk, k, 0:P], kv_raw[:, 0, kk, :], start=kk == 0, stop=False)
                pe.matmul(bank[6][:, 0:D], row0, bkv[:, 0, :], start=False, stop=True).then_inc(done("k_ps"), 1)
                yield
                wait(pe, done("a_xm"), k - 1)
                wait(pe, done("a_mc"), 2 * (k - 1))
                wait(pe, done("v1_set"), k)
                for e in range(2):
                    for kk in range(2):
                        pe.matmul(bank[7][:, e * D:(e + 1) * D], ctxt[:, kk, k, e * SK:e * SK + P], kv_raw[:, 1, kk, :],
                                  start=kk == 0, stop=False)
                    mm = pe.matmul(bank[7][:, e * D:(e + 1) * D], row0, bkv[:, 1, :], start=False, stop=True)
                mm.then_inc(done("v_ps"), 1)
                yield

            def keys_turn(k):
                wait(pe, done("kn"), k + 1)
                wait(pe, done("a_qt"), min(k + 2, NG))
                for f in range(2):
                    mm = pe.transpose(bank[4][:, f * P:(f + 1) * P], kn_sb[:, f * P:(f + 1) * P], ident)
                mm.then_inc(done("kt_ps"), 1)

            pe.wait_ge(done("setup_in"), 32)
            turn_a(0)
            for i in range(NG + 1):
                j, w = i - 1, (i - 1) % 2
                kv = keys_values(i) if i < NG else None
                if i == NG:
                    own_b = pe_front(pe, MOE, 0, MOE["front0"])
                    wait(pe, done("kt_lo"), NG)
                if i < NG:
                    wait(pe, done("a_qt"), i + 1)
                    wait(pe, done("a_s"), 2 * i)
                    for f in range(2):
                        for e in range(2):
                            if f == 0:
                                wait(pe, done("a_kb"), 4 * i + 2 * (e + 1))
                            mm = pe.matmul(bank[f][own[e], :], a_qt[:, f, e * SK:(e + 1) * SK], a_kb[:, e, f, :],
                                           start=True, stop=True)
                        mm.then_inc(done("a_s_ps"), 1)
                if i < NG:
                    next(kv)
                if i == 0:
                    next(kv)
                if j >= 0:
                    wait(pe, done("a_exp"), j + 1)
                    for h in range(2):
                        wait(pe, done("a_pt"), 2 * (j - 1) + h + 1)
                        for c in range(4):
                            cc = 4 * h + c
                            mm = pe.transpose(bank[2 + h][:, c * P:(c + 1) * P], a_s[:, w, cc * P:(cc + 1) * P], ident)
                        mm.then_inc(done("a_pt_ps"), 1)
                if i == NG:
                    next(own_b)
                elif i > 0:
                    next(kv)
                if i + 1 < NG:
                    turn_a(i + 1)
                if j >= 0:
                    wait(pe, done("v_in"), 16)
                    wait(pe, done("a_pt"), 2 * j + 2)
                    wait(pe, done("a_at"), j)
                    for c in range(8):
                        r = 32 * (c % 4)
                        for e in range(2):
                            at = (c // 4) * P + e * SK
                            mm = pe.matmul(bank[5][r:r + 32, at:at + SK], ctxv[:, 2 * j + e, c * 32:(c + 1) * 32],
                                           a_ptb[:, c, e * SK:(e + 1) * SK], start=True, stop=True)
                    mm.then_inc(done("a_pv_ps"), 1)
                    wait(pe, done("avg_set"), 1)
                    wait(pe, done("v1_set"), min(i + 1, NG))
                    pe.matmul(bank[7][:, :], avg[:], ctxv[:, 2 * j:2 * j + 2, :], start=True, stop=True).then_inc(done("a_m_ps"), 1)
                if i < NG:
                    keys_turn(i)
                else:
                    next(own_b)
                if j >= 0:
                    wait(pe, done("a_at"), j + 1)
                    wait(pe, done("a_tmp"), 2 * j)
                    wait(pe, done("kn"), min(i + 1, NG))
                    for f in range(2):
                        mm = pe.transpose(bank[6][:, f * P:(f + 1) * P], a_at[:, f, :], ident)
                    mm.then_inc(done("a_o_ps"), 1)

            def turn_tokens(src, bk):
                for f in range(2):
                    for t in range(2):
                        mm = pe.transpose(bk[:, f * SQ + t * P:f * SQ + (t + 1) * P], src[:, t, f * P:(f + 1) * P], ident)
                return mm

            def x_turn(b, bk):
                wait(pe, done("c_xn"), b + 1)
                wait(pe, done("c_qtl"), b)
                turn_tokens(c_xnb, bk).then_inc(done("c_xt_ps"), 1)

            def projection(bk, src, which):
                for t in range(2):
                    for kk in range(2):
                        mm = pe.matmul(bk[:, t * D:(t + 1) * D], src[:, kk, t * P:(t + 1) * P], xw[:, which, kk, :],
                                       start=kk == 0, stop=kk == 1)
                return mm

            def q_proj(b, bk):
                wait(pe, done("c_xt"), b + 1)
                projection(bk, c_xt, 0).then_inc(done("c_q_ps"), 1)

            def q_turn(b, bk):
                wait(pe, done("c_q"), b + 1)
                turn_tokens(c_qb, bk).then_inc(done("c_qt_ps"), 1)

            def p_turn(b, t):
                wait(pe, done("c_exp"), 2 * b + t + 1)
                for h in range(2):
                    if t == 1:
                        pe.wait_ge(done("c_pt"), 4 * b + h + 1)
                    elif h == 0:
                        wait(pe, done("c_rt"), b)
                    for c in range(4):
                        cc = 4 * h + c
                        mm = pe.transpose(bank[4 + h][:, c * P:(c + 1) * P], c_e[:, t, cc * P:(cc + 1) * P], ident)
                    mm.then_inc(done("c_pt_ps"), 1)

            def scores(b, t):
                wait(pe, done("c_qtl"), b + 1)
                if not (isinstance(b, int) and b == 0):
                    wait(pe, done("c_sub"), 4 * b + 2 * t - 2)
                tok = slice(t * P, (t + 1) * P)
                for f in range(2):
                    if t == 0:
                        wait(pe, done("c_kb"), 4 * b + 2 * (f + 1))
                    mm = split_matmul(pe, bank[2 * t + f][:, :], c_qth[:, f, tok], c_qtl[:, f, tok],
                                      c_kbh[:, f, :], c_kbl[:, f, :], True, True)
                mm.then_inc(done("c_s_ps"), 1)

            def o_proj(m):
                wait(pe, done("c_at"), m + 1)
                projection(bank[7], c_atb, 1).then_inc(done("c_o_ps"), 1)

            def step_c(i, mid=True, front=True, rest=True, out=True, tails=(), fronts=()):
                j, m = i - 1, i - 2
                if front and not tails:
                    x_turn(i + 1, bank[6])
                if rest:
                    p_turn(j, 0)
                for t in fronts[:1]:
                    next(t)
                if mid:
                    scores(i, 0)
                if rest:
                    p_turn(j, 1)
                if front and not tails:
                    q_proj(i + 1, bank[6])
                if front and tails:
                    x_turn(i + 1, bank[4])
                    q_proj(i + 1, bank[4])
                if mid and not tails:
                    scores(i, 1)
                if out:
                    o_proj(m)
                if front and not tails:
                    q_turn(i + 1, bank[6])
                if rest:
                    wait(pe, done("c_rx"), j + 1)
                    wait(pe, done("c_pt"), 4 * j + 4)
                    turn_tokens(c_rx, bank[4]).then_inc(done("c_r_ps"), 1)
                for t in fronts[1:]:
                    next(t)
                if tails:
                    scores(i, 1)
                for q in tails:
                    pe_tail(pe, MOE, NG - 1, q, last_banks["b"][q])
                if tails:
                    q_turn(i + 1, bank[6])
                if rest:
                    wait(pe, done("c_v"), 2 * (j + 1))
                    if out:
                        wait(pe, done("c_go"), j)
                    else:
                        wait(pe, done("b_x"), 2 * NG)
                    for c in range(8):
                        r = 32 * (c % 4)
                        mm = pe.matmul(bank[7][r:r + 32, (c // 4) * SQ:(c // 4 + 1) * SQ], c_v[:, c * 32:(c + 1) * 32],
                                       c_ptb[:, c, :], start=True, stop=True)
                    mm.then_inc(done("c_pv_ps"), 1)

            pe.wait_ge(done("late_lo"), 1)
            pe.wait_ge(done("late_hi"), 2)

            def x_turn0():
                pe.wait_ge(done("b_x"), 2 * (NG - 1))
                x_turn(0, bank[7])

            next(own_b)
            pe_ffn(pe, MOE, own_b, {5: x_turn0, 7: lambda: q_proj(0, bank[7]), 9: lambda: q_turn(0, bank[7])})

            step_c(0, rest=False, out=False, tails=(0, 1))
            step_c(1, out=False)
            with pe.Fori(2, NB - 2) as i:
                step_c(i)
            step_c(NB - 2)
            step_c(NB - 1, front=False)
            own_d = pe_front(pe, FFN, 0, FFN["front0"])
            step_c(NB, mid=False, front=False, fronts=(own_d, own_d))

            def last_bank():
                wait(pe, done("c_x"), NB)
            pe_ffn(pe, FFN, None, {"first": {1: lambda: o_proj(NB - 1), FFN["front_at"][0] - 1: last_bank}})
            for q in range(2):
                pe_tail(pe, FFN, NG - 1, q, last_banks["d"][q])

        def act_front(act, ph, g, bk):
            p = ph["name"]
            for f in range(2):
                wait(act, done(p + "xt_ps"), 2 * g + f + 1)
                act.activation(xt[:, g % 2, 0, f, :], bk[:, :], ACT.Copy).then_inc(done(p + "xth"), 1)
                yield
            if ph["moe"]:
                wait(act, done(p + "lg_ps"), g + 1)
                act.activation(lgt[:], bk[:, :], ACT.Copy).then_inc(done(p + "lgt"), 1)
                yield
                wait(act, done(p + "z"), g + 1)
                act.activation(r_p[:], r_z[:], ACT.Exp).then_inc(done(p + "e"), 1)
                act.activation(r_es[:], lg[:, :, 8:9], ACT.Exp, scale=-1.0).then_inc(done(p + "es"), 1)
                yield
                wait(act, done(p + "ct_ps"), g + 1)
                act.activation(c_t[:, g % 2, :], bk[:, :], ACT.Copy).then_inc(done(p + "ct"), 1)
                yield

        def act_split0(act, n):
            wait(act, done(f"w0_in{n % 2}"), 16 * (n // 2 + 1))
            act.activation(w_hi[:, n * CHUNK:(n + 1) * CHUNK], stage[:, n % 2], ACT.Copy).then_inc(done("w0_hi"), 1)

        def act_ffn(act, ph, own, after):
            p, nch, moe = ph["name"], ph["chunks"], ph["moe"]

            def hi(c, n):
                wait(act, done(p + ("h" if moe else "t")), n + 1)
                wait(act, done(p + "dn"), n - back(c, 3, nch) + 1)
                act.activation(h_hi[:, c % 3, :], h_sb[:, c % 2, :], ACT.Copy).then_inc(done(p + "hhi"), 1)

            def y_out(g):
                wait(act, done(p + "dn"), (g + 1) * nch)
                for f in range(2):
                    act.activation(y_t[:, f, :], bank[5 + f][:, :], ACT.Copy).then_inc(done(p + "y"), 1)

            def group(g, prev, nxt, split, after):
                front = act_front(act, ph, g + 1, bank[7]) if nxt else None
                for c in range(nch):
                    n = g * nch + c
                    wait(act, done(p + "gate_ps"), n + 1)
                    wait(act, done(p + "t"), n - back(c, 2, nch) + 1)
                    act.activation(s_sb[:, c % 2, :], bank[c % 2][:, :], ACT.Silu).then_inc(done(p + "silu"), 1)
                    if moe and split and c < 2:
                        next(own)
                    if c >= 1:
                        hi(c - 1, n - 1)
                    elif prev:
                        hi(nch - 1, n - 1)
                    if moe and split and c + EARLY < nch:
                        act_split0(act, c + EARLY)
                    if prev and c == 2:
                        y_out(g - 1)
                    if nxt and c in ph["front_at"]:
                        next(front)
                    if c in after:
                        after[c]()

            group(0, False, True, True, after.get("first", {}))
            with act.Fori(1, NG - 1) as g:
                group(g, True, True, False, {})
            group(NG - 1, True, False, False, after)
            hi(nch - 1, NG * nch - 1)
            y_out(NG - 1)

        @block.scalar
        def _(act):
            act.dma_start(cst[:], consts).then_inc(done("setup_in"), 16)
            act.dma_start(ctxt[:], ctx_t).then_inc(done("setup_in"), 16)
            act.dma_start(ctxv[:], ctx_v).then_inc(done("v_in"), 16)

            def q_out(k):
                wait(act, done("a_xt_ps"), k + 1)
                wait(act, done("a_s_ps"), 2 * k)
                act.activation(a_qt[:], left(bank[4]), ACT.Copy).then_inc(done("a_qt"), 1)

            def late():
                act.wait_ge(done("late_in"), 64)
                act.activation(rw_hi[:], rw_raw[:], ACT.Copy).then_inc(done("late_hi"), 1)
                act.activation(sel_sb[:], sel_raw[:], ACT.Copy).then_inc(done("late_hi"), 1)

            q_out(0)
            for i in range(NG + 1):
                j, u = i - 1, i % 2
                if i < NG:
                    for f in range(2):
                        wait(act, done("a_s_ps"), 2 * i + f + 1)
                        if f == 0:
                            wait(act, done("a_pt_ps"), 2 * (i - 1))
                            wait(act, done("a_sm"), i - 1)
                        act.activation(a_s[:, u, 512 * f:512 * f + 512], bank[f][:, :], ACT.Copy).then_inc(done("a_s"), 1)
                if j >= 0:
                    for h in range(2):
                        wait(act, done("a_pt_ps"), 2 * j + h + 1)
                        wait(act, done("a_pv_ps"), j)
                        act.activation(a_ptb[:, 4 * h:4 * h + 4, :], bank[2 + h][:, :].rearrange("p (c t) -> p c t", c=4),
                                       ACT.Copy).then_inc(done("a_pt"), 1)
                if i < NG:
                    act.wait_ge(done("k_ps"), i + 1)
                    wait(act, done("k_sq"), i)
                    act.activation(bank[6][:, D:2 * D], bank[6][:, 0:D], ACT.Square, scale=RMS_SCALE, accum_out=k_ss[:, i:i + 1])\
                       .then_inc(done("k_sq"), 1)
                else:
                    own_b = act_front(act, MOE, 0, MOE["front0"])
                    next(own_b)
                if i == 0:
                    act.wait_ge(done("gates_in"), 32)
                    act.activation(gates[:], gates[:], ACT.Tanh).then_inc(done("gates"), 1)
                if i + 1 < NG:
                    q_out(i + 1)
                if i < NG:
                    act_split0(act, i)
                if j >= 0:
                    wait(act, done("a_pv_ps"), j + 1)
                    wait(act, done("a_o_ps"), j)
                    act.activation(a_at[:], left(bank[5]), ACT.Copy).then_inc(done("a_at"), 1)
                    for e in range(2):
                        wait(act, done("a_m_ps"), j + 1)
                        wait(act, done("a_x"), j)
                        act.activation(a_out[own[1 - e], e, :], bank[7][own[1 - e], e * D:(e + 1) * D], ACT.Copy)\
                           .then_inc(done("a_mc"), 1)
                if i < NG:
                    wait(act, done("a_sub"), i + 1)
                    act.activation(a_s[:, u, :], a_s[:, u, :], ACT.Exp, scale=SCALE).then_inc(done("a_exp"), 1)
                    wait(act, done("kt_ps"), i + 1)
                    act.activation(kt_hi[:, :, i * P:(i + 1) * P], left(bank[4]), ACT.Copy).then_inc(done("kt_hi"), 1)
                else:
                    next(own_b)
                if i == 2:
                    late()

            def xt_out(b, bk):
                wait(act, done("c_xt_ps"), b + 1)
                wait(act, done("c_q_ps"), b)
                act.activation(c_xt[:], halves(bk), ACT.Copy).then_inc(done("c_xt"), 1)

            def squares(b):
                wait(act, done("c_q"), b + 1)
                wait(act, done("c_rq_ve"), b)
                for t in range(2):
                    wait(act, done("c_sq"), 2 * b + t)
                    act.activation(stage[:, 1, 0:D], c_qb[:, t, :], ACT.Square, scale=RMS_SCALE / SCALE, accum_out=c_ss[:, t:t + 1])\
                       .then_inc(done("c_sq"), 1)

            def qt_out(b, bk):
                wait(act, done("c_qt_ps"), b + 1)
                wait(act, done("c_s_ps"), 2 * b)
                act.activation(c_qth[:], halves(bk), ACT.Copy).then_inc(done("c_qth"), 1)

            def p_out(b, t):
                for h in range(2):
                    n = 4 * b + 2 * t + h
                    wait(act, done("c_pt_ps"), n + 1)
                    wait(act, done("c_pv_ps"), b)
                    act.activation(c_ptb[:, 4 * h:4 * h + 4, t * P:(t + 1) * P],
                                   bank[4 + h][:, :].rearrange("p (c t) -> p c t", c=4), ACT.Copy).then_inc(done("c_pt"), 1)

            def exps(b, t):
                wait(act, done("c_rq"), b + 1)
                wait(act, done("c_sub"), 4 * b + 2 * t + 2)
                act.activation(c_e[:, t, :], c_e[:, t, :], ACT.Exp, scale=c_rq[:, t:t + 1]).then_inc(done("c_exp"), 1)

            def gated(m):
                wait(act, done("c_o_ps"), m + 1)
                wait(act, done("c_x"), m)
                act.activation(c_go, halves(bank[7]), ACT.Copy, scale=gates[:, 1:2]).then_inc(done("c_go"), 1)

            def other(b):
                return b + 1 - 2 * (b % 2)

            def split1(c):
                act.wait_ge(done("w1_in"), 16 * (c + 1))
                act.activation(w_hi[:, bass.ds(c * CHUNK, CHUNK)], stage[:, 0], ACT.Copy).then_inc(done("w1_hi"), 1)

            def step_c(i, mid=True, front=True, rest=True, out=True, split=None, fronts=()):
                j = i - 1
                if rest:
                    p_out(j, 0)
                if front:
                    xt_out(i + 1, bank[6 if rest else 4])
                for t in fronts[:1]:
                    next(t)
                if rest:
                    p_out(j, 1)
                    wait(act, done("c_pv_ps"), j)
                    act.activation(c_v[lower, :], v1[lower, j, :], ACT.Copy).then_inc(done("c_v"), 1)
                    act.activation(c_v[upper, :], v1[upper, other(j), :], ACT.Copy).then_inc(done("c_v"), 1)
                    wait(act, done("c_ri"), j + 1)
                    wait(act, done("c_r_ps"), j)
                    act.activation(c_rx[:].rearrange("p t (h e) -> p (t h) e", h=NH),
                                   c_ri[:].rearrange("p t h -> p (t h)").unsqueeze(2).broadcast_to([P, 2 * NH, HD]),
                                   ACT.Copy).then_inc(done("c_rx"), 1)
                if split is not None:
                    split1(split)
                if mid and not rest:
                    exps(i, 0)
                if front:
                    squares(i + 1)
                if out:
                    gated(i - 2)
                if front:
                    qt_out(i + 1, bank[6])
                if rest:
                    wait(act, done("c_r_ps"), j + 1)
                    wait(act, done("c_at"), j)
                    act.activation(c_rt[:], halves(bank[4]), ACT.Copy).then_inc(done("c_rt"), 1)
                if mid and rest:
                    exps(i, 0)
                if mid:
                    exps(i, 1)
                for t in fronts[1:]:
                    next(t)

            next(own_b)
            act_ffn(act, MOE, own_b, {5: lambda: xt_out(0, bank[7]), 8: lambda: squares(0), 9: lambda: qt_out(0, bank[7])})

            step_c(0, rest=False, out=False)
            step_c(1, out=False)
            with act.Fori(2, NB - 2) as i:
                step_c(i)
            step_c(NB - 2, split=0)
            step_c(NB - 1, front=False, split=1)
            own_d = act_front(act, FFN, 0, FFN["front0"])
            step_c(NB, mid=False, front=False, split=2, fronts=(own_d, own_d))

            act.wait_ge(done("c_pv_ps"), NB)
            act_ffn(act, FFN, None, {"first": {c: lambda c=c: split1(c + EARLY1) for c in range(NC1 - EARLY1)}})
            act.wait_ge(done("d_x"), 2 * NG)
            act.dma_start(out_v[:, NT - 2:NT, :], x_sb[:, NT - 2:NT, :]).then_inc(done("out_done"), 16)

        def dve_stats(dve, ph, g):
            p = ph["name"]
            wait(dve, done(p + "xn"), GT * g)
            for t in range(GT):
                dve.bn_stats(stat[:, t, :], x_sb[:, GT * g + t, :]).then_inc(done(p + "bn"), 1)

        def dve_aggr(dve, ph):
            for t in range(GT):
                dve.bn_aggr(mv[:, t, :], stat[:, t, :]).then_inc(done(ph["name"] + "mv"), 1)

        def dve_norm(dve, ph, g):
            p = ph["name"]
            dve.wait_ge(done(p + "rstd"), g + 1)
            wait(dve, done(p + "xt_ps"), 2 * g)
            for t in range(GT):
                dve.tensor_scalar(f_xnb[:, t, :], x_sb[:, GT * g + t, :], mv[:, t, 0:1], rstd[:, t:t + 1],
                                  ALU.subtract, ALU.mult).then_inc(done(p + "xn"), 1)

        def dve_front(dve, ph, g, bk):
            p = ph["name"]
            for f in range(2):
                dve.wait_ge(done(p + "xth"), 2 * g + f + 1)
                dve.tensor_tensor(xt[:, g % 2, 1, f, :], bk[:, :], xt[:, g % 2, 0, f, :].bitcast(F32),
                                  ALU.subtract).then_inc(done(p + "xtl"), 1)
                yield
            if ph["moe"]:
                dve.wait_ge(done(p + "lt_ps"), g + 1)
                wait(dve, done(p + "c"), g)
                dve.tensor_copy(lg[:], bk[:, :].rearrange("p (t e) -> p t e", t=GT)[:, :, 0:9]).then_inc(done(p + "lg"), 1)
                dve.wait_ge(done(p + "lg"), g + 1)
                dve.tensor_reduce(r_m[:], lg[:, :, 0:8], AX.X, ALU.max).then_inc(done(p + "m"), 1)
                dve.wait_ge(done(p + "m"), g + 1)
                dve.tensor_tensor(r_z[:], lg[:, :, 0:8], over(r_m), ALU.subtract).then_inc(done(p + "z"), 1)
                yield
                dve.wait_ge(done(p + "es"), g + 1)
                n = [0]

                def link(ins):
                    n[0] += 1
                    ins.then_inc(done(p + "r"), 1)
                    dve.wait_ge(done(p + "r"), ROUTER_STEPS * g + n[0])

                link(dve.tensor_reduce(r_den[:, :, 0:1], r_p[:], AX.X, ALU.add))
                link(dve.tensor_scalar(r_den[:, :, 1:2], r_es[:], 1.0, None, ALU.add))
                link(dve.reciprocal(r_inv[:], r_den[:]))
                link(dve.tensor_tensor(r_p[:], r_p[:], r_inv[:, :, 0:1].broadcast_to([P, GT, 8]), ALU.mult))
                link(dve.tensor_reduce(r_m[:], r_p[:], AX.X, ALU.max))
                link(dve.tensor_tensor(r_k[:], r_p[:], over(r_m), ALU.is_equal))
                link(dve.tensor_tensor(r_k[:], r_k[:], w8.unsqueeze(1).broadcast_to([P, GT, 8]), ALU.mult))
                link(dve.tensor_reduce(r_m[:], r_k[:], AX.X, ALU.max))
                link(dve.tensor_tensor(r_o1[:], r_k[:], over(r_m), ALU.is_equal))
                link(dve.scalar_tensor_tensor(out=r_z[:], in0=r_o1[:], scalar=-2.0, in1=r_p[:], op0=ALU.mult, op1=ALU.add))
                link(dve.tensor_reduce(r_m[:], r_z[:], AX.X, ALU.max))
                link(dve.tensor_tensor(r_k[:], r_z[:], over(r_m), ALU.is_equal))
                link(dve.tensor_tensor(r_k[:], r_k[:], w8.unsqueeze(1).broadcast_to([P, GT, 8]), ALU.mult))
                link(dve.tensor_reduce(r_m[:], r_k[:], AX.X, ALU.max))
                link(dve.tensor_tensor(r_o2[:], r_k[:], over(r_m), ALU.is_equal))
                link(dve.tensor_tensor(r_o1[:], r_o1[:], r_o2[:], ALU.add))
                link(dve.tensor_tensor(r_c[:, :, 0:8], r_o1[:], r_p[:], ALU.mult))
                link(dve.tensor_copy(r_c[:, :, 8:9], r_inv[:, :, 1:2]))
                wait(dve, done(p + "ct_ps"), g)
                link(dve.tensor_copy(r_cd[:, :, 0:9], r_c[:]))
                assert n[0] == ROUTER_STEPS
                dve.tensor_tensor(r_cd[:, :, 32:41], r_c[:], r_cd[:, :, 0:9].bitcast(F32), ALU.subtract)\
                   .then_inc(done(p + "c"), 1)
                yield
                yield

        ROUTER_STEPS = 19

        def over(m):
            return m[:].unsqueeze(2).broadcast_to([P, GT, 8])

        def dve_split0(dve, n):
            at = slice(n * CHUNK, (n + 1) * CHUNK)
            dve.wait_ge(done("w0_hi"), n + 1)
            dve.tensor_tensor(w_lo[:, at], stage[:, 1], w_hi[:, at].bitcast(F32), ALU.subtract).then_inc(done("w0_lo1"), 1)

        def dve_tail(dve, ph, g, q, bk=bank[7]):
            p = ph["name"]
            dve.wait_ge(done(p + "yt_ps"), 2 * g + q + 1)
            xs = x_sb[:, bass.ds(GT * g + 2 * q, 2), :]
            dve.scalar_tensor_tensor(out=xs, in0=bk[:, :].rearrange("p (t d) -> p t d", t=2),
                                     scalar=gates[:, ph["gate"]:ph["gate"] + 1], in1=xs,
                                     op0=ALU.mult, op1=ALU.add).then_inc(done(p + "x"), 1)

        def low_part(eng, ph, c, n):
            p = ph["name"]
            eng.wait_ge(done(p + "hhi"), n + 1)
            wait(eng, done(p + "dn"), n - back(c, 3, ph["chunks"]) + 1)
            eng.tensor_tensor(h_lo[:, c % 3, :], h_sb[:, c % 2, :], h_hi[:, c % 3, :].bitcast(F32), ALU.subtract)\
               .then_inc(done(p + "hlo"), 1)

        def dve_ffn(dve, ph, after):
            p, nch, moe = ph["name"], ph["chunks"], ph["moe"]

            def group(g, prev, nxt, split, after):
                front = dve_front(dve, ph, g + 1, bank[7]) if nxt else None
                for c in range(nch):
                    n = g * nch + c
                    if nxt and c == 1:
                        dve.wait_ge(done(p + "bn"), GT * (g + 2))
                    dve.wait_ge(done(p + "silu"), n + 1)
                    dve.wait_ge(done(p + "up_ps"), n + 1)
                    wait(dve, done(p + "h" if moe else p + "hlo"), n - back(c, 2, nch) + 1)
                    if moe:
                        dve.tensor_tensor(t_sb[:, c % 2, :], s_sb[:, c % 2, :], bank[2 + c % 2][:, :], ALU.mult)\
                           .then_inc(done(p + "t"), 1)
                        dve.wait_ge(done(p + "t"), n + 1)
                        dve.wait_ge(done(p + "cb_ps"), n + 1)
                        wait(dve, done(p + "hlo"), n - back(c, 2, nch) + 1)
                        dve.tensor_tensor(h_sb[:, c % 2, :], t_sb[:, c % 2, :], bank[4][:, :], ALU.mult)\
                           .then_inc(done(p + "h"), 1)
                    else:
                        dve.tensor_tensor(h_sb[:, c % 2, :], s_sb[:, c % 2, :], bank[2 + c % 2][:, :], ALU.mult)\
                           .then_inc(done(p + "t"), 1)
                        if c >= 1:
                            low_part(dve, ph, c - 1, n - 1)
                        elif prev:
                            low_part(dve, ph, nch - 1, n - 1)
                    if moe and split and c + EARLY < nch and (c + EARLY) % 2:
                        dve_split0(dve, c + EARLY)
                    if nxt and c == 0:
                        dve_stats(dve, ph, g + 1)
                    if nxt and c == 1:
                        dve_aggr(dve, ph)
                    if nxt and c == 2:
                        dve_norm(dve, ph, g + 1)
                    if prev and c in ph["tail_at"]:
                        dve_tail(dve, ph, g - 1, ph["tail_at"].index(c))
                    if nxt and c in ph["front_at"]:
                        next(front)
                    if c in after:
                        after[c]()

            group(0, False, True, True, after.get("first", {}))
            with dve.Fori(1, NG - 1) as g:
                group(g, True, True, False, {})
            group(NG - 1, True, False, False, after)
            if not moe:
                low_part(dve, ph, nch - 1, NG * nch - 1)

        @block.vector
        def _(dve):
            dve.memset(avg[:], 1.0 / SK).then_inc(done("avg_set"), 1)

            def stats_a(k):
                wait(dve, done("a_xn"), 2 * k)
                for e in range(2):
                    dve.bn_stats(stat[own[e], 0, :], x_sb[own[e], GT * k + 1 + 2 * e, :]).then_inc(done("a_bn"), 1)

            def aggr_a(k):
                dve.wait_ge(done("a_bn"), 2 * (k + 1))
                dve.bn_aggr(mv[:, 0, :], stat[:, 0, :]).then_inc(done("a_mv"), 1)

            def norm_a(k):
                dve.wait_ge(done("a_rstd"), k + 1)
                wait(dve, done("a_xt_ps"), k)
                for e in range(2):
                    dve.tensor_scalar(a_xnb[own[e], :], x_sb[own[e], GT * k + 1 + 2 * e, :], mv[own[e], 0, 0:1], rstd[own[e], 0:1],
                                      ALU.subtract, ALU.mult).then_inc(done("a_xn"), 1)

            def per_head(t):
                return t.unsqueeze(2).broadcast_to([P, NH, SK])

            dve.wait_ge(done("x0_in"), 48)
            stats_a(0)
            aggr_a(0)
            norm_a(0)
            for i in range(NG + 1):
                j, u = i - 1, i % 2
                if i == 0:
                    dve.wait_ge(done("kv_in"), 32)
                    dve.tensor_tensor(bkv[:, 2, :], bkv[:, 2, :], bkv[:, 3, :], ALU.mult).then_inc(done("gain"), 1)
                    dve.wait_ge(done("x_in"), 48)
                if i == 1:
                    dve.wait_ge(done("x_rest_in"), 32)
                if i + 1 < NG:
                    stats_a(i + 1)
                    aggr_a(i + 1)
                elif i == NG - 1:
                    dve.wait_ge(done("late_hi"), 2)
                    dve.tensor_tensor(rw_lo[:], rw_raw[:], rw_hi[:].bitcast(F32), ALU.subtract).then_inc(done("late_lo"), 1)
                    dve.wait_ge(done("late_lo"), 1)
                    dve_stats(dve, MOE, 0)
                    dve.wait_ge(done("b_bn"), GT)
                    dve_aggr(dve, MOE)
                if j >= 0:
                    dve.wait_ge(done("a_exp"), j + 1)
                    dve.tensor_reduce(a_sm[:], by_head(a_s[:, 1 - u, :], NH), AX.X, ALU.add).then_inc(done("a_sm"), 1)
                    dve.wait_ge(done("a_sm"), j + 1)
                    dve.reciprocal(a_ri[:], a_sm[:]).then_inc(done("a_ri"), 1)
                if i < NG:
                    dve.wait_ge(done("a_msk"), 2 * (i + 1))
                    dve.tensor_reduce(a_mx[:], by_head(a_s[:, u, :], NH), AX.X, ALU.max).then_inc(done("a_mx"), 1)
                if i + 1 < NG:
                    norm_a(i + 1)
                if i < NG:
                    dve.wait_ge(done("v_ps"), i + 1)
                    dve.tensor_tensor(v1[:, 2 * i:2 * i + 2, :], bank[7][:, :].rearrange("p (e d) -> p e d", e=2),
                                      vmask.unsqueeze(1).broadcast_to([P, 2, D]), ALU.mult).then_inc(done("v1_set"), 1)
                    dve.wait_ge(done("a_mx"), i + 1)
                    dve.tensor_tensor(by_head(a_s[:, u, :], NH), by_head(a_s[:, u, :], NH), per_head(a_mx[:]), ALU.subtract)\
                       .then_inc(done("a_sub"), 1)
                if i == NG - 1:
                    dve_norm(dve, MOE, 0)
                if i < NG:
                    if i == 0:
                        dve.wait_ge(done("gain"), 1)
                    dve.wait_ge(done("k_r"), i + 1)
                    wait(dve, done("kt_ps"), i)
                    dve.scalar_tensor_tensor(out=kn_sb[:], in0=bank[6][:, 0:D], scalar=k_r[:, i:i + 1], in1=bkv[:, 2, :],
                                             op0=ALU.mult, op1=ALU.mult).then_inc(done("kn"), 1)
                if i == NG:
                    own_b = dve_front(dve, MOE, 0, MOE["front0"])
                    next(own_b)
                if j >= 0:
                    dve.wait_ge(done("gates"), 1)
                    dve.wait_ge(done("a_m_ps"), j + 1)
                    dve.wait_ge(done("a_mc"), 2 * (j + 1))
                    xs = x_sb[:, GT * j:GT * j + 3:2, :]
                    dve.scalar_tensor_tensor(out=xs, in0=bank[7][:, :].rearrange("p (t d) -> p t d", t=2),
                                             scalar=gates[:, 0:1], in1=xs, op0=ALU.mult, op1=ALU.add).then_inc(done("a_xm"), 1)
                if i < NG:
                    dve.wait_ge(done("kt_hi"), i + 1)
                    at = slice(i * P, (i + 1) * P)
                    dve.tensor_tensor(kt_lo[:, :, at], left(bank[4]), kt_hi[:, :, at].bitcast(F32), ALU.subtract)\
                       .then_inc(done("kt_lo"), 1)
                if i == NG:
                    next(own_b)
                if j >= 0:
                    dve.wait_ge(done("a_ri"), j + 1)
                    dve.wait_ge(done("a_o_ps"), j + 1)
                    for e in range(2):
                        dve.tensor_tensor(a_out[own[e], e, :].rearrange("p (h e) -> p h e", h=NH),
                                          bank[6][own[e], 0:D].rearrange("p (h e) -> p h e", h=NH),
                                          a_ri[own[e], :].unsqueeze(2).broadcast_to([SK, NH, HD]), ALU.mult)\
                           .then_inc(done("a_tmp"), 1)
                    dve.wait_ge(done("a_tmp"), 2 * (j + 1))
                    xs = x_sb[:, GT * j + 1:GT * j + 4:2, :]
                    dve.scalar_tensor_tensor(out=xs, in0=a_out[:], scalar=gates[:, 0:1], in1=xs,
                                             op0=ALU.mult, op1=ALU.add).then_inc(done("a_x"), 1)
                    dve.wait_ge(done("a_x"), j + 1)
                if i < NG and i % 2:
                    dve_split0(dve, i)
            def stats_c(b):
                wait(dve, done("c_xn"), b)
                for t in range(2):
                    dve.bn_stats(stat[:, t, :], x_sb[:, 2 * b + t, :]).then_inc(done("c_bn"), 1)

            def aggr_c():
                for t in range(2):
                    dve.bn_aggr(mv[:, t, :], stat[:, t, :]).then_inc(done("c_mv"), 1)

            def q_bias(b, bk):
                dve.wait_ge(done("c_q_ps"), b + 1)
                wait(dve, done("c_qt_ps"), b)
                wait(dve, done("c_sq"), 2 * b)
                dve.tensor_tensor(c_qb[:], halves(bk), bias_sb[:, 0, :].unsqueeze(1).broadcast_to([P, 2, D]), ALU.add)\
                   .then_inc(done("c_q"), 1)

            def qt_low(b, bk):
                dve.wait_ge(done("c_qth"), b + 1)
                dve.tensor_tensor(c_qtl[:], halves(bk), c_qth[:].bitcast(F32), ALU.subtract).then_inc(done("c_qtl"), 1)

            def shift(b, t, first):
                dve.wait_ge(done("c_s_ps"), 2 * b + t + 1)
                for f in range(2):
                    dve.tensor_reduce(c_mx[:, t, 8 * f:8 * f + 8], by_head(bank[2 * t + f][:, :], 8), AX.X, ALU.max)\
                       .then_inc(done("c_mx"), 1)
                if not first:
                    wait(dve, done("c_pt_ps"), 4 * b + 2 * t - 2)
                for f in range(2):
                    dve.wait_ge(done("c_mx"), 4 * b + 2 * t + f + 1)
                    sub = dve.tensor_tensor(by_head(c_e[:, t, 512 * f:512 * f + 512], 8), by_head(bank[2 * t + f][:, :], 8),
                                            c_mx[:, t, 8 * f:8 * f + 8].unsqueeze(2).broadcast_to([P, 8, SK]), ALU.subtract)
                    sub.then_inc(done("c_sub"), 1)

            def inverse(j, pre):
                for t in range(2):
                    if pre and t:
                        dve.wait_ge(done("c_bn"), 2 * (j + 4))
                    wait(dve, done("c_exp"), 2 * j + t + 1)
                    wait(dve, done("c_ri"), j)
                    dve.tensor_reduce(c_sm[:, t, :], by_head(c_e[:, t, :], NH), AX.X, ALU.add).then_inc(done("c_sm"), 1)
                dve.wait_ge(done("c_sm"), 2 * (j + 1))
                wait(dve, done("c_rx"), j)
                dve.reciprocal(c_ri[:], c_sm[:]).then_inc(done("c_ri"), 1)

            def divided(m):
                dve.wait_ge(done("c_rt"), m + 1)
                dve.wait_ge(done("c_pv_ps"), m + 1)
                dve.tensor_tensor(c_atb[:], halves(bank[7]), c_rt[:], ALU.mult).then_inc(done("c_at"), 1)

            def add_c(m):
                dve.wait_ge(done("c_o_ps"), m + 1)
                dve.wait_ge(done("c_x"), m)
                dve.wait_ge(done("c_xb"), m + 1)
                xs = x_sb[:, bass.ds(2 * m, 2), :]
                dve.scalar_tensor_tensor(out=xs, in0=halves(bank[7]), scalar=gates[:, 1:2], in1=xs,
                                         op0=ALU.mult, op1=ALU.add).then_inc(done("c_x"), 1)

            def step_c(i, mid=True, front=True, pre=True, rest=True, out=True, tails=(), first=False, fronts=(), between=None):
                if pre:
                    stats_c(i + 2)
                if rest:
                    inverse(i - 1, pre)
                elif pre:
                    dve.wait_ge(done("c_bn"), 2 * (i + 3))
                if pre:
                    aggr_c()
                for t in fronts[:1]:
                    next(t)
                if mid:
                    shift(i, 0, first)
                if front:
                    q_bias(i + 1, bank[4 if tails else 6])
                for q in tails:
                    dve_tail(dve, MOE, NG - 1, q, last_banks["b"][q])
                if tails:
                    dve.wait_ge(done("b_x"), 2 * NG)
                for t in fronts[1:]:
                    next(t)
                if tails:
                    qt_low(i + 1, bank[6])
                if mid:
                    shift(i, 1, first)
                if between:
                    between()
                if front and not tails:
                    qt_low(i + 1, bank[6])
                if rest:
                    divided(i - 1)

            dve.wait_ge(done("a_xm"), NG)
            dve.memset(r_cd[:].bitcast(F32), 0.0).then_inc(done("cd_zero"), 1)
            dve.wait_ge(done("cd_zero"), 1)
            next(own_b)
            next(own_b)

            def ready(b):
                def go():
                    stats_c(b)
                    dve.wait_ge(done("c_bn"), 2 * (b + 1))
                    aggr_c()
                return go

            def gated_bias():
                dve.tensor_scalar(bias_sb[:, 1, :], bias_sb[:, 1, :], gates[:, 1:2], None, ALU.mult).then_inc(done("gate_bo"), 1)

            dve_ffn(dve, MOE, {1: gated_bias, 2: ready(0), 6: ready(1), 7: lambda: q_bias(0, bank[7]), 9: lambda: qt_low(0, bank[7])})

            step_c(0, rest=False, out=False, tails=(0, 1), first=True)
            step_c(1, out=False)
            with dve.Fori(2, NB - 2) as i:
                step_c(i)
            step_c(NB - 2, pre=False)
            dve.wait_ge(done("c_x"), GT // 2)
            dve_stats(dve, FFN, 0)
            dve.wait_ge(done("d_bn"), GT)
            dve_aggr(dve, FFN)
            step_c(NB - 1, front=False, pre=False, between=lambda: dve_norm(dve, FFN, 0))
            own_d = dve_front(dve, FFN, 0, FFN["front0"])
            step_c(NB, mid=False, front=False, pre=False, fronts=(own_d, own_d))

            dve_ffn(dve, FFN, {"first": {1: lambda: add_c(NB - 1)}})
            for q in range(2):
                dve_tail(dve, FFN, NG - 1, q, last_banks["d"][q])

        def power(pool, var, scratch, dst, eps, after, name):
            n = var.shape[1]
            pool.tensor_tensor(scratch, var, eps[:, 0:n], ALU.add).then_inc(done(name + "_ve"), 1)
            pool.wait_ge(done(name + "_ve"), after)
            pool.tensor_tensor(dst, scratch, neghalf[:, 0:n], ALU.pow).then_inc(done(name), 1)

        def pool_rsqrt(pool, ph, g):
            p = ph["name"]
            pool.wait_ge(done(p + "mv"), GT * (g + 1))
            wait(pool, done(p + "xn"), GT * g)
            power(pool, mv[:, :, 1], ve[:], rstd[:], ln_eps, g + 1, p + "rstd")

        def pool_split0(pool, n):
            at = slice(n * CHUNK, (n + 1) * CHUNK)
            pool.wait_ge(done("w0_hi"), n + 1)
            pool.tensor_tensor(w_lo[:, at], stage[:, 0], w_hi[:, at].bitcast(F32), ALU.subtract).then_inc(done("w0_lo0"), 1)

        def pool_ffn(pool, ph, after):
            p, nch = ph["name"], ph["chunks"]

            def group(g, nxt, split, after):
                for c in range(nch):
                    n = g * nch + c
                    if nxt and c == 1:
                        pool_rsqrt(pool, ph, g + 1)
                    if ph["moe"]:
                        low_part(pool, ph, c, n)
                    if ph["moe"] and split and c + EARLY < nch and (c + EARLY) % 2 == 0:
                        pool_split0(pool, c + EARLY)
                    if c in after:
                        after[c]()

            group(0, True, True, after.get("first", {}))
            with pool.Fori(1, NG - 1) as g:
                group(g, True, False, {})
            group(NG - 1, False, False, after)

        def spread(pool, dst, keys):
            return pool.tensor_tensor(by_head(dst, 8), keys.unsqueeze(1).broadcast_to([P, 8, SK]),
                                      headmask.unsqueeze(2).broadcast_to([P, 8, SK]), ALU.mult)

        @block.gpsimd
        def _(pool):
            def rsqrt_a(k):
                pool.wait_ge(done("a_mv"), k + 1)
                power(pool, mv[:, 0, 1:2], ve[:, 0:1], rstd[:, 0:1], ln_eps, k + 1, "a_rstd")

            def keys_a(k):
                for e in range(2):
                    for f in range(2):
                        wait(pool, done("a_s_ps"), 2 * k)
                        spread(pool, a_kb[:, e, f, :], ctxt[:, f, k, e * SK:(e + 1) * SK]).then_inc(done("a_kb"), 1)

            pool.wait_ge(done("setup_in"), 32)
            rsqrt_a(0)
            keys_a(0)
            for i in range(NG):
                u = i % 2
                pool.wait_ge(done("a_s"), 2 * (i + 1))
                for e in range(2):
                    if e == 1:
                        pool.wait_ge(done("a_msk"), 2 * i + 1)
                    v = by_head(a_s[own[e], u, :], NH)
                    pool.affine_select(out=v, in_=v, compare_op=ALU.is_ge, fill=MASKED, base=0,
                                       pattern=[[0, NH], [-1, SK]], channel_multiplier=1).then_inc(done("a_msk"), 1)
                pool.wait_ge(done("a_msk"), 2 * (i + 1))
                if i + 1 < NG:
                    rsqrt_a(i + 1)
                else:
                    pool_rsqrt(pool, MOE, 0)
                pool.wait_ge(done("k_sq"), i + 1)
                power(pool, k_ss[:, i:i + 1], k_ve[:, i:i + 1], k_r[:, i:i + 1], rms_eps, i + 1, "k_r")
                if i + 1 < NG:
                    keys_a(i + 1)
                if i % 2 == 0:
                    pool_split0(pool, i)

            def rstd_c(b):
                pool.wait_ge(done("c_mv"), 2 * (b + 1))
                power(pool, mv[:, 0:2, 1], ve[:, 0:2], rstd[:, 0:2], ln_eps, b + 1, "c_rstd")

            def norm_c(b):
                wait(pool, done("c_rstd"), b + 1)
                wait(pool, done("c_xt_ps"), b)
                pool.tensor_tensor(c_xnb[:], x_sb[:, bass.ds(2 * b, 2), :], mv[:, 0:2, 0:1].broadcast_to([P, 2, D]), ALU.subtract)\
                    .then_inc(done("c_xm"), 1)
                pool.wait_ge(done("c_xm"), b + 1)
                pool.tensor_tensor(c_xnb[:], c_xnb[:], rstd[:, 0:2].unsqueeze(2).broadcast_to([P, 2, D]), ALU.mult)\
                    .then_inc(done("c_xn"), 1)

            def keys_c(b):
                wait(pool, done("c_s_ps"), 2 * b)
                for f in range(2):
                    for dst, src in ((c_kbh, kt_hi), (c_kbl, kt_lo)):
                        spread(pool, dst[:, f, :], src[:, f, bass.ds(b * SK, SK)].bitcast(F32)).then_inc(done("c_kb"), 1)

            def bias_c(b):
                pool.wait_ge(done("c_xn"), b + 1)
                xs = x_sb[:, bass.ds(2 * b, 2), :]
                pool.tensor_tensor(xs, xs, bias_sb[:, 1, :].unsqueeze(1).broadcast_to([P, 2, D]), ALU.add).then_inc(done("c_xb"), 1)

            def add_c(m):
                pool.wait_ge(done("c_go"), m + 1)
                wait(pool, done("c_xb"), m + 1)
                xs = x_sb[:, bass.ds(2 * m, 2), :]
                pool.tensor_tensor(xs, xs, c_go, ALU.add).then_inc(done("c_x"), 1)

            def rsqrt_q(b):
                pool.wait_ge(done("c_sq"), 2 * (b + 1))
                wait(pool, done("c_exp"), 2 * b)
                power(pool, c_ss[:], c_ve[:], c_rq[:], rmsq_eps, b + 1, "c_rq")

            def split1(c):
                pool.wait_ge(done("w1_hi"), c + 1)
                at = bass.ds(c * CHUNK, CHUNK)
                pool.tensor_tensor(w_lo[:, at], stage[:, 0], w_hi[:, at].bitcast(F32), ALU.subtract).then_inc(done("w1_lo"), 1)

            def step_c(i, front=True, pre=True, out=True, split=None):
                if front:
                    bias_c(i + 1)
                if split is not None:
                    split1(split)
                if pre:
                    rstd_c(i + 2)
                    norm_c(i + 2)
                if front:
                    keys_c(i + 1)
                if out:
                    add_c(i - 2)
                if front:
                    rsqrt_q(i + 1)

            pool_ffn(pool, MOE, {2: lambda: (rstd_c(0), norm_c(0)), 5: lambda: bias_c(0), 6: lambda: (rstd_c(1), norm_c(1)),
                                 9: lambda: rsqrt_q(0)})

            keys_c(0)
            step_c(0, out=False)
            step_c(1, out=False)
            with pool.Fori(2, NB - 2) as i:
                step_c(i)
            step_c(NB - 2, pre=False, split=0)
            pool_rsqrt(pool, FFN, 0)
            step_c(NB - 1, front=False, pre=False, split=1)
            step_c(NB, front=False, pre=False, split=2)

            pool_ffn(pool, FFN, {"first": {c: lambda c=c: split1(c + EARLY1) for c in range(NC1 - EARLY1)}})


def kernel(**inputs):
    import numpy as np
    import concourse.bacc as bacc
    from concourse.bass_utils import run_bass_kernel_spmd

    a = {k: np.asarray(v) for k, v in inputs.items()}

    def halves(w):
        return w.reshape(2, P, -1).transpose(1, 0, 2)

    def packed(gate, up, down):
        parts = [halves(w).reshape(P, 2, -1, P).transpose(0, 2, 1, 3).reshape(P, -1, D) for w in (gate, up)]
        parts.append(down.reshape(-1, P, D).transpose(1, 0, 2))
        return np.ascontiguousarray(np.stack(parts, axis=2).reshape(P, -1))

    def experts(w, shared):
        w = np.concatenate([w.transpose(1, 0, 2).reshape(D, NE * FE), shared], axis=1)
        return np.concatenate([w, np.zeros((D, HID0 - w.shape[1]), w.dtype)], axis=1)

    down0 = np.concatenate([a["L0_ffn_Wd"].reshape(NE * FE, D), a["L0_ffn_Sd"],
                            np.zeros((HID0 - NE * FE - FS, D), np.float32)], axis=0)

    def projections(*names):
        return np.ascontiguousarray(np.stack([halves(a["L1_xattn_w_" + n].T) for n in names], axis=1))

    rw = np.concatenate([a["L0_ffn_Wr"], a["L0_ffn_Wsg"], np.zeros((D, P - NE - 1), np.float32)], axis=1)
    p = np.arange(P)[:, None]
    col = np.arange(D)[None, :]
    consts = np.concatenate([
        p == np.arange(P)[None, :],
        p // HD == np.arange(8)[None, :],
        col // HD % 2 == p // SK,
        np.full((P, 4), -0.5),
        np.broadcast_to(np.arange(8, 0, -1), (P, 8)),
        np.full((P, 4), LN_EPS), np.full((P, 4), RMS_EPS),
        np.full((P, 4), RMS_EPS / SCALE ** 2),
        np.broadcast_to(p == 0, (P, P)),
    ], axis=1).astype(np.float32)
    unit = np.arange(HID0)
    owner = np.where(unit < NE * FE, unit // FE, np.where(unit < NE * FE + FS, NE, -1))
    row = np.arange(P)[:, None]
    sel = ((row < 64) & (row % 32 == owner[None, :])).astype(np.float32)

    token = a["ctx_2048"].transpose(1, 0, 2)
    ctx_v = np.zeros((P, NB, D), np.float32)
    for parity in range(2):
        cols = np.arange(D) // HD % 2 == parity
        ctx_v[parity * SK:(parity + 1) * SK][:, :, cols] = token[:, :, cols]

    arrays = {
        "x": a["x"], "ctx_v": ctx_v,
        "ctx_t": np.ascontiguousarray(halves(a["ctx_2048"].reshape(NG, 2, SK, D)[:, [0, 1, 0]].reshape(-1, D).T)
                                      .reshape(P, 2, NG, 3 * SK)),
        "xw_kv": projections("k_img", "v_img"), "xw_qo": projections("q", "o"), "rw": np.ascontiguousarray(halves(rw)),
        "moe_w": packed(experts(a["L0_ffn_Wg"], a["L0_ffn_Sg"]), experts(a["L0_ffn_Wu"], a["L0_ffn_Su"]), down0),
        "ffn_w": packed(a["L1_ffn_w_gate"].T, a["L1_ffn_w_up"].T, a["L1_ffn_w_down"].T),
        "bias_kv": np.stack([a["L1_xattn_" + n] for n in ("b_k_img", "b_v_img", "g_k_img", "g_q")]),
        "bias_qo": np.stack([a["L1_xattn_" + n] for n in ("b_q", "b_o")]),
        "gx": a["g_xattn"], "gf": a["g_ffn"], "consts": consts, "sel": sel,
    }
    nc = bacc.Bacc("TRN2", target_bir_lowering=False, num_devices=1, dynamic_dma_scratch_size=1024)
    args = {k: nc.dram_tensor("in_" + k, v.shape, mybir.dt.from_np(v.dtype), kind="ExternalInput").ap()
            for k, v in arrays.items()}
    args["out"] = nc.dram_tensor("result", (NB, SQ, D), F32, kind="ExternalOutput").ap()
    build(nc, **args)
    r = run_bass_kernel_spmd(nc, [{"in_" + k: v for k, v in arrays.items()}], core_ids=[0])
    return r.results[0]["result"]
```
